# Optimizing a Trainium2 kernel written in Bass

```python
import numpy as np
import jax
import jax.numpy as jnp

def _softmax(x, axis=-1):
    return jax.nn.softmax(x, axis=axis)

def _gelu(x):
    return jax.nn.gelu(x, approximate=True)

def _silu(x):
    return jax.nn.silu(x)

def _sigmoid(x):
    return jax.nn.sigmoid(x)

def _layernorm(x, axis=-1, eps=1e-05):
    m = jnp.mean(x, axis=axis, keepdims=True)
    v = jnp.var(x, axis=axis, keepdims=True)
    return (x - m) / jnp.sqrt(v + eps)

def _scatter_add(tgt, idx, src, axis=0):
    return tgt.at[idx].add(src)

def _segment_sum(src, seg, n):
    return jax.ops.segment_sum(src, seg, n)
kernel_name = 'mk_gnn_resnorm_d4_gnn_r16_9a7dcf'

def setup_inputs(seed: int=0):
    np.random.seed(seed)
    _w = jnp.asarray

    def _rec_inputs():
        import jax
        import jax.numpy as jnp
        _gk = jax.random.key(seed)
        x = -0.0003713 + 1 * jax.random.normal(jax.random.fold_in(_gk, 1), (6250, 128), jnp.float32)
        src = jax.random.randint(jax.random.fold_in(_gk, 2), (100000,), 0, 6250, jnp.int32)
        dst = jnp.minimum((6250 * jax.random.uniform(jax.random.fold_in(_gk, 3), (100000,)) ** 2.0).astype(jnp.int32), 99999)
        _o = jnp.argsort(dst, stable=True)
        src = src[_o]
        dst = dst[_o]
        edge_attr_128 = -2.25437e-05 + 0.999858 * jax.random.normal(jax.random.fold_in(_gk, 12), (100000, 128), jnp.float32)
        edge_weight = jax.random.uniform(jax.random.fold_in(_gk, 14), (100000,), jnp.float32, 0.0, 1)
        return (x, src, dst, edge_attr_128, edge_weight)
    x, src, dst, edge_attr_128, edge_weight = _rec_inputs()

    def _L0_gnn_setup():
        import jax, jax.numpy as jnp
        import numpy as np
        N = 6250
        E = 100000
        D_IN = 128
        D_HID = 64
        key = jax.random.key(seed)
        k1, k2, k3, k4, k5 = jax.random.split(key, 5)
        x = jax.random.normal(k1, (N, D_IN), dtype=jnp.float32)
        edge_index = jax.random.randint(k2, (2, E), 0, N, dtype=jnp.int64)
        s1 = (6.0 / (D_IN + D_HID)) ** 0.5
        s2 = (6.0 / (D_HID + D_IN)) ** 0.5
        W1 = jax.random.uniform(k3, (D_IN, D_HID), jnp.float32, -s1, s1)
        W2 = jax.random.uniform(k4, (D_HID, D_IN), jnp.float32, -s2, s2)
        b1 = jnp.zeros((D_HID,), jnp.float32)
        b2 = jnp.zeros((D_IN,), jnp.float32)
        return {'x': x, 'edge_index': edge_index, 'W1': W1, 'b1': b1, 'W2': W2, 'b2': b2}
    _L0_gnn_all = _L0_gnn_setup()
    _L0_gnn_in = {k: v for k, v in _L0_gnn_all.items() if k in ('W1', 'b1', 'W2', 'b2')}
    del _L0_gnn_all

    def _L1_gnn_setup():
        import jax, jax.numpy as jnp
        import numpy as np
        NUM_NODES = 625
        key = jax.random.key(seed)
        k1, k2, k3, k4 = jax.random.split(key, 4)
        x = jax.random.normal(k1, (NUM_NODES, 128), dtype=jnp.float32)
        edge_index = jax.random.randint(k2, (2, 40000), 0, NUM_NODES, dtype=jnp.int64)
        W = jax.random.normal(k3, (128, 128), dtype=jnp.float32) * (1.0 / np.sqrt(128))
        b = jax.random.normal(k4, (128,), dtype=jnp.float32) * 0.01
        return {'x': x, 'edge_index': edge_index, 'W': W, 'b': b}
    _L1_gnn_all = _L1_gnn_setup()
    _L1_gnn_in = {k: v for k, v in _L1_gnn_all.items() if k in ('W', 'b')}
    del _L1_gnn_all

    def _L2_gnn_setup():
        import jax, jax.numpy as jnp
        import numpy as np
        N = 3125
        E = 31250
        D = 128
        L = 5
        IN_DIM = 128
        BN_EPS = 1e-05

        def _bn(z, g, b):
            mu = jnp.mean(z, axis=0)
            var = jnp.mean(jnp.square(z - mu), axis=0)
            return (z - mu) * jax.lax.rsqrt(var + BN_EPS) * g + b
        key = jax.random.key(seed)
        ks = jax.random.split(key, 8)
        s = 0.05
        return {'x': jax.random.normal(ks[0], (N, IN_DIM), jnp.float32), 'edge_attr': jax.random.normal(ks[1], (E, D), jnp.float32), 'src': jax.random.randint(ks[2], (E,), 0, N, jnp.int32), 'dst': jax.random.randint(ks[3], (E,), 0, N, jnp.int32), 'enc_W': jax.random.normal(ks[4], (IN_DIM, D), jnp.float32) * s, 'enc_b': jnp.zeros((D,), jnp.float32), 'W1': jax.random.normal(ks[5], (L, D, 2 * D), jnp.float32) * s, 'b1': jnp.zeros((L, 2 * D), jnp.float32), 'bn1_g': jnp.ones((L, 2 * D), jnp.float32), 'bn1_b': jnp.zeros((L, 2 * D), jnp.float32), 'W2': jax.random.normal(ks[6], (L, 2 * D, D), jnp.float32) * s, 'b2': jnp.zeros((L, D), jnp.float32), 'bn_g': jnp.ones((L, D), jnp.float32), 'bn_b': jnp.zeros((L, D), jnp.float32)}
    _L2_gnn_all = _L2_gnn_setup()
    _L2_gnn_in = {k: v for k, v in _L2_gnn_all.items() if k in ('enc_W', 'enc_b', 'W1', 'b1', 'bn1_g', 'bn1_b', 'W2', 'b2', 'bn_g', 'bn_b')}
    del _L2_gnn_all

    def _L3_gnn_setup():
        import jax, jax.numpy as jnp
        import numpy as np
        N, E, IN_DIM, OUT_DIM, HEADS = (3125, 50000, 128, 32, 4)

        def _linear_params(key, fan_in, fan_out, bias=True):
            kw, kb = jax.random.split(key)
            s = 1.0 / np.sqrt(fan_in)
            W = jax.random.uniform(kw, (fan_in, fan_out), jnp.float32, -s, s)
            b = jax.random.uniform(kb, (fan_out,), jnp.float32, -s, s) if bias else None
            return (W, b)

        def _transformer_conv(x, src, dst, ea, Wq, bq, Wk, bk, Wv, bv, We, Ws, bs, H, C):
            n = x.shape[0]
            q = (x @ Wq + bq).reshape(n, H, C)
            k = (x @ Wk + bk).reshape(n, H, C)
            v = (x @ Wv + bv).reshape(n, H, C)
            e = (ea @ We).reshape(-1, H, C)
            kj = k[src] + e
            vj = v[src] + e
            alpha = jnp.einsum('ehc,ehc->eh', q[dst], kj) / jnp.sqrt(jnp.asarray(C, x.dtype))
            amax = jax.ops.segment_max(alpha, dst, num_segments=n)
            p = jnp.exp(alpha - amax[dst])
            denom = jax.ops.segment_sum(p, dst, num_segments=n)
            w = p / denom[dst]
            msg = (vj * w[..., None]).reshape(-1, H * C)
            out = jax.ops.segment_sum(msg, dst, num_segments=n)
            return out + x @ Ws + bs
        key = jax.random.key(seed)
        ks = jax.random.split(key, 24)
        H, C = (HEADS, OUT_DIM)
        inp = {'x': jax.random.normal(ks[0], (N, IN_DIM), jnp.float32), 'edge_weight': jax.random.uniform(ks[1], (E,), jnp.float32)}
        for li, fan_in in ((1, IN_DIM), (2, H * C)):
            base = 2 + (li - 1) * 10
            inp[f'Wq{li}'], inp[f'bq{li}'] = _linear_params(ks[base + 0], fan_in, H * C)
            inp[f'Wk{li}'], inp[f'bk{li}'] = _linear_params(ks[base + 1], fan_in, H * C)
            inp[f'Wv{li}'], inp[f'bv{li}'] = _linear_params(ks[base + 2], fan_in, H * C)
            We, _ = _linear_params(ks[base + 3], 1, H * C, bias=False)
            inp[f'We{li}'] = We
            inp[f'Ws{li}'], inp[f'bs{li}'] = _linear_params(ks[base + 4], fan_in, H * C)
        inp['edge_index'] = jax.random.randint(ks[22], (2, E), 0, N, jnp.int64)
        return inp
    _L3_gnn_all = _L3_gnn_setup()
    _L3_gnn_in = {k: v for k, v in _L3_gnn_all.items() if k in ('Wq1', 'bq1', 'Wk1', 'bk1', 'Wv1', 'bv1', 'We1', 'Ws1', 'bs1', 'Wq2', 'bq2', 'Wk2', 'bk2', 'Wv2', 'bv2', 'We2', 'Ws2', 'bs2')}
    del _L3_gnn_all
    return {'x': x, 'src': src, 'dst': dst, 'edge_attr_128': edge_attr_128, 'edge_weight': edge_weight, 'L0_gnn_W1': _L0_gnn_in['W1'], 'L0_gnn_b1': _L0_gnn_in['b1'], 'L0_gnn_W2': _L0_gnn_in['W2'], 'L0_gnn_b2': _L0_gnn_in['b2'], 'L1_gnn_W': _L1_gnn_in['W'], 'L1_gnn_b': _L1_gnn_in['b'], 'L2_gnn_enc_W': _L2_gnn_in['enc_W'], 'L2_gnn_enc_b': _L2_gnn_in['enc_b'], 'L2_gnn_W1': _L2_gnn_in['W1'], 'L2_gnn_b1': _L2_gnn_in['b1'], 'L2_gnn_bn1_g': _L2_gnn_in['bn1_g'], 'L2_gnn_bn1_b': _L2_gnn_in['bn1_b'], 'L2_gnn_W2': _L2_gnn_in['W2'], 'L2_gnn_b2': _L2_gnn_in['b2'], 'L2_gnn_bn_g': _L2_gnn_in['bn_g'], 'L2_gnn_bn_b': _L2_gnn_in['bn_b'], 'L3_gnn_Wq1': _L3_gnn_in['Wq1'], 'L3_gnn_bq1': _L3_gnn_in['bq1'], 'L3_gnn_Wk1': _L3_gnn_in['Wk1'], 'L3_gnn_bk1': _L3_gnn_in['bk1'], 'L3_gnn_Wv1': _L3_gnn_in['Wv1'], 'L3_gnn_bv1': _L3_gnn_in['bv1'], 'L3_gnn_We1': _L3_gnn_in['We1'], 'L3_gnn_Ws1': _L3_gnn_in['Ws1'], 'L3_gnn_bs1': _L3_gnn_in['bs1'], 'L3_gnn_Wq2': _L3_gnn_in['Wq2'], 'L3_gnn_bq2': _L3_gnn_in['bq2'], 'L3_gnn_Wk2': _L3_gnn_in['Wk2'], 'L3_gnn_bk2': _L3_gnn_in['bk2'], 'L3_gnn_Wv2': _L3_gnn_in['Wv2'], 'L3_gnn_bv2': _L3_gnn_in['bv2'], 'L3_gnn_We2': _L3_gnn_in['We2'], 'L3_gnn_Ws2': _L3_gnn_in['Ws2'], 'L3_gnn_bs2': _L3_gnn_in['bs2']}

def reference(x, src, dst, edge_attr_128, edge_weight, L0_gnn_W1, L0_gnn_b1, L0_gnn_W2, L0_gnn_b2, L1_gnn_W, L1_gnn_b, L2_gnn_enc_W, L2_gnn_enc_b, L2_gnn_W1, L2_gnn_b1, L2_gnn_bn1_g, L2_gnn_bn1_b, L2_gnn_W2, L2_gnn_b2, L2_gnn_bn_g, L2_gnn_bn_b, L3_gnn_Wq1, L3_gnn_bq1, L3_gnn_Wk1, L3_gnn_bk1, L3_gnn_Wv1, L3_gnn_bv1, L3_gnn_We1, L3_gnn_Ws1, L3_gnn_bs1, L3_gnn_Wq2, L3_gnn_bq2, L3_gnn_Wk2, L3_gnn_bk2, L3_gnn_Wv2, L3_gnn_bv2, L3_gnn_We2, L3_gnn_Ws2, L3_gnn_bs2):
    import jax
    import jax.numpy as jnp

    def _L0_gnn_ref(x, edge_index, W1, b1, W2, b2):
        import jax, jax.numpy as jnp
        import numpy as np
        N = 6250
        E = 100000
        D_IN = 128
        D_HID = 64
        n = x.shape[0]
        loops = jnp.arange(n, dtype=edge_index.dtype)
        src = jnp.concatenate([edge_index[0], loops])
        dst = jnp.concatenate([edge_index[1], loops])
        deg = jnp.zeros((n,), x.dtype).at[dst].add(jnp.ones((), x.dtype))
        dinv = jnp.where(deg > 0, jax.lax.rsqrt(deg), 0.0)
        norm = dinv[src] * dinv[dst]

        def gcn_conv(h, W, b):
            h = h @ W
            msg = h[src] * norm[:, None]
            agg = jax.ops.segment_sum(msg, dst, num_segments=n)
            return agg + b
        h = jax.nn.relu(gcn_conv(x, W1, b1))
        return gcn_conv(h, W2, b2)

    def _L1_gnn_ref(x, edge_index, W, b):
        import jax, jax.numpy as jnp
        import numpy as np
        NUM_NODES = 625
        src, dst = (edge_index[0], edge_index[1])
        num_nodes = x.shape[0]
        aggregated = jax.ops.segment_sum(x[src], dst, num_segments=num_nodes)
        degree = jax.ops.segment_sum(jnp.ones_like(dst, dtype=x.dtype), dst, num_segments=num_nodes)
        degree = jnp.maximum(degree, 1.0)
        aggregated = aggregated / degree[:, None]
        out = jax.nn.relu(jnp.einsum('nd,od->no', aggregated + x, W) + b)
        return out

    def _L2_gnn_ref(x, edge_attr, src, dst, enc_W, enc_b, W1, b1, bn1_g, bn1_b, W2, b2, bn_g, bn_b):
        import jax, jax.numpy as jnp
        import numpy as np
        N = 3125
        E = 31250
        D = 128
        L = 5
        IN_DIM = 128
        BN_EPS = 1e-05

        def _bn(z, g, b):
            mu = jnp.mean(z, axis=0)
            var = jnp.mean(jnp.square(z - mu), axis=0)
            return (z - mu) * jax.lax.rsqrt(var + BN_EPS) * g + b
        n = x.shape[0]
        h = x @ enc_W + enc_b
        num_layer = W1.shape[0]
        for l in range(num_layer):
            m = jax.nn.relu(h[src] + edge_attr)
            agg = jax.ops.segment_sum(m, dst, num_segments=n)
            z = h + agg
            z = jax.nn.relu(_bn(z @ W1[l] + b1[l], bn1_g[l], bn1_b[l])) @ W2[l] + b2[l]
            z = _bn(z, bn_g[l], bn_b[l])
            if l < num_layer - 1:
                z = jax.nn.relu(z)
            h = z + h
        return h

    def _L3_gnn_ref(x, edge_weight, Wq1, bq1, Wk1, bk1, Wv1, bv1, We1, Ws1, bs1, Wq2, bq2, Wk2, bk2, Wv2, bv2, We2, Ws2, bs2, edge_index):
        import jax, jax.numpy as jnp
        import numpy as np
        N, E, IN_DIM, OUT_DIM, HEADS = (3125, 50000, 128, 32, 4)

        def _linear_params(key, fan_in, fan_out, bias=True):
            kw, kb = jax.random.split(key)
            s = 1.0 / np.sqrt(fan_in)
            W = jax.random.uniform(kw, (fan_in, fan_out), jnp.float32, -s, s)
            b = jax.random.uniform(kb, (fan_out,), jnp.float32, -s, s) if bias else None
            return (W, b)

        def _transformer_conv(x, src, dst, ea, Wq, bq, Wk, bk, Wv, bv, We, Ws, bs, H, C):
            n = x.shape[0]
            q = (x @ Wq + bq).reshape(n, H, C)
            k = (x @ Wk + bk).reshape(n, H, C)
            v = (x @ Wv + bv).reshape(n, H, C)
            e = (ea @ We).reshape(-1, H, C)
            kj = k[src] + e
            vj = v[src] + e
            alpha = jnp.einsum('ehc,ehc->eh', q[dst], kj) / jnp.sqrt(jnp.asarray(C, x.dtype))
            amax = jax.ops.segment_max(alpha, dst, num_segments=n)
            p = jnp.exp(alpha - amax[dst])
            denom = jax.ops.segment_sum(p, dst, num_segments=n)
            w = p / denom[dst]
            msg = (vj * w[..., None]).reshape(-1, H * C)
            out = jax.ops.segment_sum(msg, dst, num_segments=n)
            return out + x @ Ws + bs
        src, dst = (edge_index[0], edge_index[1])
        ea = edge_weight[:, None]
        h = _transformer_conv(x, src, dst, ea, Wq1, bq1, Wk1, bk1, Wv1, bv1, We1, Ws1, bs1, HEADS, OUT_DIM)
        out = _transformer_conv(h, src, dst, ea, Wq2, bq2, Wk2, bk2, Wv2, bv2, We2, Ws2, bs2, HEADS, OUT_DIM)
        return out
    edge_index = jnp.stack([src, dst])
    x = _layernorm(x + _L0_gnn_ref(x, edge_index, L0_gnn_W1, L0_gnn_b1, L0_gnn_W2, L0_gnn_b2), axis=-1)
    x = _layernorm(x + _L1_gnn_ref(x, edge_index, L1_gnn_W, L1_gnn_b), axis=-1)
    x = _layernorm(x + _L2_gnn_ref(x, edge_attr_128, src, dst, L2_gnn_enc_W, L2_gnn_enc_b, L2_gnn_W1, L2_gnn_b1, L2_gnn_bn1_g, L2_gnn_bn1_b, L2_gnn_W2, L2_gnn_b2, L2_gnn_bn_g, L2_gnn_bn_b), axis=-1)
    x = _layernorm(x + _L3_gnn_ref(x, edge_weight, L3_gnn_Wq1, L3_gnn_bq1, L3_gnn_Wk1, L3_gnn_bk1, L3_gnn_Wv1, L3_gnn_bv1, L3_gnn_We1, L3_gnn_Ws1, L3_gnn_bs1, L3_gnn_Wq2, L3_gnn_bq2, L3_gnn_Wk2, L3_gnn_bk2, L3_gnn_Wv2, L3_gnn_bv2, L3_gnn_We2, L3_gnn_Ws2, L3_gnn_bs2, edge_index), axis=-1)
    return x

_drawn_inputs = setup_inputs


def setup_inputs(seed=0):
    import zlib

    import numpy as np

    out = dict(_drawn_inputs(seed))
    spreads = {'L0_gnn_b1': (0.0, 0.1),
     'L0_gnn_b2': (0.0, 0.1),
     'L2_gnn_enc_b': (0.0, 0.1),
     'L2_gnn_b1': (0.0, 0.8),
     'L2_gnn_bn1_g': (1.0, 0.2),
     'L2_gnn_bn1_b': (0.0, 0.1),
     'L2_gnn_b2': (0.0, 0.8),
     'L2_gnn_bn_g': (1.0, 0.2),
     'L2_gnn_bn_b': (0.0, 0.1)}
    factors = {'L1_gnn_b': 8.0,
     'L3_gnn_bq1': 8.0,
     'L3_gnn_bk1': 8.0,
     'L3_gnn_Wq2': 3.053,
     'L3_gnn_bq2': 8.0,
     'L3_gnn_Wk2': 4.149,
     'L3_gnn_bk2': 8.0}
    for name, (base, spread) in spreads.items():
        noise = np.random.default_rng([zlib.crc32(name.encode()), seed]).standard_normal(out[name].shape)
        drawn = base * np.exp(spread * noise) if base else spread * noise
        out[name] = jnp.asarray(drawn.astype(out[name].dtype))
    for name, factor in factors.items():
        out[name] = (out[name] * factor).astype(out[name].dtype)
    return out
```

```python
import concourse.bass as bass
import concourse.mybir as mybir
from contextlib import ExitStack

F32 = mybir.dt.float32
I32 = mybir.dt.int32
ALU = mybir.AluOpType
ACT = mybir.ActivationFunctionType
AX = mybir.AxisListType

P = 128
N, E, D, HID = 6250, 100000, 128, 64
LAYERS, HEADS, HEAD = 5, 4, 32
EDGE_TILES = -(-E // P)
NODE_TILES = -(-N // P)
WINDOWS = NODE_TILES + 1
COLS = WINDOWS * P
GROUP = 4
RING = 4
PAIRS = -(-(EDGE_TILES + NODE_TILES - 1) // (GROUP * RING)) * GROUP * RING
GROUPS = PAIRS // GROUP
ROUNDS = GROUPS // RING
KBLOCKS = -(-(PAIRS + 2 * GROUP) // P)
KCOLS = KBLOCKS * P
CHUNK = 400
CHUNKS = COLS // CHUNK
FULL = N // CHUNK
TURN = 5
SEQ_ROWS = 32
SEQ = PAIRS * P // SEQ_ROWS
SEQ_PAIRS = PAIRS // SEQ_ROWS
FAR = -1.0e30
EPS = 1e-5
CREDIT = 64
PAD_NODE = WINDOWS * P


class Gate:

    def __init__(self, ctx, nc, name, credit=CREDIT):
        self.sem = ctx.enter_context(nc.semaphore(name))
        self.base = credit
        self.credit = credit

    def at(self, n):
        return self.base + n

    def passed(self, n):
        self.base += n


class Ctx:
    pass


def _setup(ctx, nc):
    c = Ctx()
    c.nc = nc

    def sb(name, shape, dt=F32):
        return ctx.enter_context(nc.sbuf_tensor(name, shape, dt))

    c.A = sb("bigA", [P, COLS])
    c.B = sb("bigB", [P, COLS])
    c.C = sb("bigC", [P, COLS])
    c.DE = sb("bigDE", [P, 2 * COLS])
    c.D = c.DE[:, 0:COLS]
    c.E = c.DE[:, COLS:2 * COLS]
    c.F = sb("bigF", [P, COLS])
    rings = sb("rings", [P, 3 * RING * GROUP * P])
    c.gbuf, c.ebuf, c.sel = (
        rings[:, i * RING * GROUP * P:(i + 1) * RING * GROUP * P].rearrange("p (a b x) -> p a b x", a=RING, b=GROUP)
        for i in range(3))
    c.soft = rings[:, 0:SEQ]
    c.rows = c.DE[0:1, 3 * SEQ + 8:3 * SEQ + 8 + 3 * P + 2]
    c.idx = sb("idx", [P, RING, GROUP], I32)
    c.srcK = sb("srcK", [P, KCOLS], I32)
    c.relK = sb("relK", [P, KCOLS])
    c.wK = sb("wK", [P, KCOLS])
    c.tRow = sb("tRow", [1, KCOLS], I32)
    c.nRow = sb("nRow", [1, KCOLS], I32)
    c.ident = sb("ident", [P, P])
    c.ones = sb("ones", [P, P])
    c.mean = sb("mean", [P, P])
    c.iota = sb("iota", [P, P])
    c.small = sb("small", [P, 64])
    c.eps = sb("eps", [P, 1])
    c.stats = sb("stats", [P, 2, (FULL + 1) * 6])
    c.W1g = sb("W1g", [P, HID])
    c.W2g = sb("W2g", [HID, D])
    c.W1T = sb("W1T", [P, D])
    c.encW = sb("encW", [P, D])
    c.W1 = sb("W1", [P, 2 * D])
    c.W2 = sb("W2", [P, 2, D])
    c.W3 = sb("W3", [P, 4, D])
    c.We = sb("We", [P, 2, D])
    c.cols = sb("cols", [P, 64])
    c.gates = {}

    def gate(name, credit=CREDIT):
        g = Gate(ctx, nc, name, credit)
        c.gates[name] = g
        return g

    c.index = gate("index")
    c.select = gate("select")
    c.joined = gate("joined")
    c.message = gate("message")
    c.product = gate("product")
    c.added = gate("added")
    c.turned = gate("turned")
    c.scored = gate("scored")
    c.centred = gate("centred")
    c.squared = gate("squared")
    c.varied = gate("varied")
    c.rooted = gate("rooted")
    c.chunked = gate("chunked")
    c.meaned = gate("meaned")
    c.small_dve = gate("small_dve")
    c.small_pe = gate("small_pe")
    c.small_pool = gate("small_pool")
    c.tick_pe = gate("tick_pe")
    c.tick_act = gate("tick_act")
    c.tick_dve = gate("tick_dve")
    c.tick_pool = gate("tick_pool")
    c.tick_sp = gate("tick_sp")
    c.staged = gate("staged")
    c.cleared = gate("cleared")
    c.applied = gate("applied")
    c.keyed = gate("keyed")
    c.expanded = gate("expanded")
    c.gathered = [gate(f"gathered{i}", 0) for i in range(RING)]
    c.attrs = [gate(f"attrs{i}", 0) for i in range(RING)]
    c.loaded = gate("loaded", 0)
    c.stored = [gate(f"stored{i}", 0) for i in range(2)]
    c.moved = gate("moved", 0)
    c.whole = gate("whole")
    c.sent = gate("sent")
    c.names = [0]

    def name(what):
        c.names[0] += 1
        return f"{what}_{c.names[0]}"
    c.name = name
    return c


def _hold(eng, gate, n, tick=None):
    v = gate.at(n)
    eng.wait_ge(gate.sem, v)
    if tick is not None and not isinstance(v, int):
        eng.sem_inc(tick.sem, 1)


def _small(c, eng, gate, count, make):
    make().then_inc(gate.sem, 1)
    gate.passed(1)
    eng.wait_ge(gate.sem, gate.at(0))


def _start(c, ins):
    nc = c.nc
    loads = [
        (c.A[:, :], ins["xT"]),
        (c.W1g[:, :], ins["L0_gnn_W1"]), (c.W2g[:, :], ins["L0_gnn_W2"]), (c.W1T[:, :], ins["L1_W_T"]),
        (c.encW[:, :], ins["L2_gnn_enc_W"]),
        (c.cols[:, 0:ins["cols"].shape[1]], ins["cols"]),
    ]
    for i in (0, 1):
        loads.append((c.We[:, i, :], ins[f"L3_gnn_We{i + 1}"].to_broadcast([P, D])))
    with nc.Block() as block:
        @block.sync
        def _(e):
            for dst, src in loads:
                e.dma_start(dst, src).then_inc(c.loaded.sem, 16)
            c.loaded.passed(16 * len(loads))
            e.wait_ge(c.loaded.sem, c.loaded.at(0))

        @block.vector
        def _(e):
            for g in c.gates.values():
                if g.credit:
                    e.sem_inc(g.sem, g.credit)
            e.memset(c.ones[:, :], 1.0)
            e.memset(c.mean[:, :], 1.0 / D)
            e.memset(c.eps[:, :], EPS)

    with nc.Block() as block:
        @block.gpsimd
        def _(e):
            _small(c, e, c.small_pool, 1, lambda: e.iota(
                c.idx[:, :, :].rearrange("p a b -> p (a b)"), [[1, RING * GROUP]], base=0, channel_multiplier=0))
            _small(c, e, c.small_pool, 1, lambda: e.memset(c.ident[:, :], 0.0))
            _small(c, e, c.small_pool, 1, lambda: e.affine_select(
                out=c.ident[:, :], in_=c.ident[:, :], compare_op=ALU.not_equal, fill=1.0, base=0,
                pattern=[[-1, P]], channel_multiplier=1))
            _small(c, e, c.small_pool, 1, lambda: e.iota(c.iota[:, :], [[1, P]], base=0, channel_multiplier=0,
                                                          allow_small_or_imprecise_dtypes=True))


def _walk(c, ins, dram):
    nc = c.nc
    s = c.small
    start, edge_lo, edge_hi, full, steps, ends, shift, number = (
        c.B[:, 64 * i:64 * i + WINDOWS] for i in range(8))
    raw = c.B[:, 1024:1024 + EDGE_TILES].bitcast(I32)
    flat = c.B[:, 2048:2048 + EDGE_TILES]
    hit = c.B[:, 3072:3072 + EDGE_TILES]
    whole = c.B[:, 512:512 + 2 * 64].bitcast(I32)
    pair = c.B[:, 704:704 + KBLOCKS]
    node = c.B[:, 720:720 + KBLOCKS]
    edge = c.B[:, 736:736 + KBLOCKS]
    node_i = c.B[:, 752:752 + KBLOCKS].bitcast(I32)
    edge_i = c.B[:, 768:768 + KBLOCKS].bitcast(I32)
    far = c.B[:, 784:784 + KBLOCKS]
    grid = c.C[:, 0:KBLOCKS * NODE_TILES].rearrange("p (k n) -> p k n", n=NODE_TILES)
    grid2 = c.C[:, 512:512 + KBLOCKS * NODE_TILES].rearrange("p (k n) -> p k n", n=NODE_TILES)
    bounds = c.B[:, 832:832 + WINDOWS]
    n = NODE_TILES
    with nc.psum_tensor("walk_ps", [P, WINDOWS], F32) as ps:
        with nc.Block() as block:
            @block.sync
            def _(e):
                e.dma_start(raw, ins["dst"].rearrange("t p -> (t p)").rearrange("(a b) -> a b", a=P)
                            ).then_inc(c.loaded.sem, 16)
                e.wait_ge(c.loaded.sem, c.loaded.at(16))

            @block.gpsimd
            def _(e):
                e.iota(bounds, [[P, WINDOWS]], base=0, channel_multiplier=0, allow_small_or_imprecise_dtypes=True)
                e.iota(number, [[1, WINDOWS]], base=0, channel_multiplier=0, allow_small_or_imprecise_dtypes=True)
                e.iota(pair, [[P, KBLOCKS]], base=0, channel_multiplier=1, allow_small_or_imprecise_dtypes=True)
        c.loaded.passed(16)
        with nc.Block() as block:
            @block.vector
            def _(e):
                _small(c, e, c.small_dve, 1, lambda: e.tensor_copy(flat, raw))
                with e.Fori(0, WINDOWS) as i:
                    _hold(e, c.added, i, c.tick_dve)
                    e.tensor_scalar(hit, flat, bounds[:, bass.ds(i, 1)], 0.0, ALU.is_lt, ALU.add,
                                    accum_out=start[:, bass.ds(i, 1)]).then_inc(c.added.sem, 1)
        c.added.passed(WINDOWS)
        with nc.Block() as block:
            @block.tensor
            def _(e):
                e.matmul(ps[:, :], c.ones[:, :], start, start=True, stop=True).then_inc(c.small_pe.sem, 1)

            @block.vector
            def _(e):
                def step(make):
                    _small(c, e, c.small_dve, 1, make)
                e.wait_ge(c.small_pe.sem, c.small_pe.at(1))
                step(lambda: e.tensor_copy(start, ps[:, :]))
                step(lambda: e.tensor_copy(whole[:, 0:WINDOWS], start))
                step(lambda: e.tensor_scalar(whole[:, 0:WINDOWS], whole[:, 0:WINDOWS], 7, None,
                                             ALU.arith_shift_right))
                step(lambda: e.tensor_copy(edge_lo, whole[:, 0:WINDOWS]))
                step(lambda: e.tensor_scalar(edge_hi, start, -1.0, None, ALU.add))
                step(lambda: e.tensor_copy(whole[:, 64:64 + WINDOWS], edge_hi))
                step(lambda: e.tensor_scalar(whole[:, 64:64 + WINDOWS], whole[:, 64:64 + WINDOWS], 7, None,
                                             ALU.arith_shift_right))
                step(lambda: e.tensor_copy(edge_hi, whole[:, 64:64 + WINDOWS]))
                step(lambda: e.tensor_tensor(full[:, 0:n], start[:, 1:n + 1], start[:, 0:n], ALU.is_gt))
                step(lambda: e.tensor_tensor(steps[:, 0:n], edge_hi[:, 1:n + 1], edge_lo[:, 0:n], ALU.subtract))
                step(lambda: e.scalar_tensor_tensor(steps[:, 0:n], steps[:, 0:n], 1.0, full[:, 0:n],
                                                    ALU.add, ALU.mult))
                step(lambda: e.tensor_tensor_scan(ends[:, 0:n], c.ones[:, 0:n], steps[:, 0:n], 0.0,
                                                  ALU.mult, ALU.add))
                step(lambda: e.tensor_tensor(shift[:, 0:n], steps[:, 0:n], ends[:, 0:n], ALU.subtract))
                step(lambda: e.tensor_tensor(shift[:, 0:n], shift[:, 0:n], edge_lo[:, 0:n], ALU.add))
                step(lambda: e.tensor_tensor(grid, ends[:, 0:n].unsqueeze(1).to_broadcast([P, KBLOCKS, n]),
                                             pair.unsqueeze(2).to_broadcast([P, KBLOCKS, n]), ALU.is_le))
                step(lambda: e.tensor_reduce(node, grid, AX.X, ALU.add))
                step(lambda: e.tensor_tensor(grid, number[:, 0:n].unsqueeze(1).to_broadcast([P, KBLOCKS, n]),
                                             node.unsqueeze(2).to_broadcast([P, KBLOCKS, n]), ALU.is_equal))
                step(lambda: e.tensor_tensor(grid2, grid,
                                             shift[:, 0:n].unsqueeze(1).to_broadcast([P, KBLOCKS, n]), ALU.mult))
                step(lambda: e.tensor_reduce(edge, grid2, AX.X, ALU.add))
                step(lambda: e.tensor_tensor(edge, edge, pair, ALU.add))
                step(lambda: e.tensor_scalar(edge, edge, float(EDGE_TILES - 1), 0.0, ALU.min, ALU.max))
                step(lambda: e.tensor_copy(edge_i, edge))
                step(lambda: e.tensor_copy(node_i, node))
                step(lambda: e.tensor_scalar(far, node, float(P), None, ALU.mult))
    c.small_pe.passed(1)
    rows_d = c.C[:, 1024:1024 + KBLOCKS * P].rearrange("p (k x) -> p k x", x=P)
    rows_s = c.C[:, 2048:2048 + KBLOCKS * P].rearrange("p (k x) -> p k x", x=P)
    rows_w = c.C[:, 3072:3072 + KBLOCKS * P].rearrange("p (k x) -> p k x", x=P)
    with nc.Block() as block:
        @block.sync
        def _(e):
            with nc.allow_non_contiguous_dma(reason="two rows of small integers"):
                e.dma_start(dram.t.rearrange("(k p) -> p k", p=P), edge_i).then_inc(c.moved.sem, 16)
                e.dma_start(dram.n.rearrange("(k p) -> p k", p=P), node_i).then_inc(c.moved.sem, 16)
            e.wait_ge(c.moved.sem, c.moved.at(32))
            e.dma_start(c.tRow[:, :], dram.t.rearrange("(a x) -> a x", a=1)).then_inc(c.moved.sem, 16)
            e.dma_start(c.nRow[:, :], dram.n.rearrange("(a x) -> a x", a=1)).then_inc(c.moved.sem, 16)
            e.wait_ge(c.moved.sem, c.moved.at(64))

        @block.gpsimd
        def _(e):
            for k in range(KBLOCKS):
                e.tensor_copy(c.idx[:, 0, 0:1], edge_i[:, k:k + 1]).then_inc(c.small_pool.sem, 1)
                c.small_pool.passed(1)
                e.wait_ge(c.small_pool.sem, c.small_pool.at(0))
                for t, (rows, src) in enumerate(((rows_d, "dst"), (rows_s, "src"), (rows_w, "w"))):
                    out = rows[:, k, :] if src == "w" else rows[:, k, :].bitcast(I32)
                    e.indirect_dma_start(out, None, ins[src],
                                         bass.IndirectOffsetOnAxis(ap=c.idx[:, 0, 0:1], axis=0)
                                         ).then_inc(c.gathered[t].sem, 16)
                for t in range(3):
                    c.gathered[t].passed(16)
                    e.wait_ge(c.gathered[t].sem, c.gathered[t].at(0))
    c.moved.passed(64)
    size = P * KBLOCKS
    with nc.psum_tensor("rel_ps", [P, 1024], F32) as rel_ps, nc.psum_tensor("src_ps", [P, 1024], F32) as src_ps, \
            nc.psum_tensor("w_ps", [P, 1024], F32) as w_ps:
        wide_d = c.C[:, 1024:1024 + size]
        wide_s = c.C[:, 2048:2048 + size]
        with nc.Block() as block:
            @block.vector
            def _(e):
                def step(make):
                    _small(c, e, c.small_dve, 1, make)
                step(lambda: e.tensor_copy(c.B[:, 1024:1024 + size], wide_d.bitcast(I32)))
                step(lambda: e.tensor_copy(c.B[:, 2048:2048 + size], wide_s.bitcast(I32)))
                step(lambda: e.tensor_tensor(
                    c.B[:, 3072:3072 + size].rearrange("p (k x) -> p k x", x=P),
                    c.B[:, 1024:1024 + size].rearrange("p (k x) -> p k x", x=P),
                    far.unsqueeze(2).to_broadcast([P, KBLOCKS, P]), ALU.subtract))
        with nc.Block() as block:
            @block.sync
            def _(e):
                e.dma_start(dram.seq[1:1 + KCOLS * P].rearrange("(k p x) -> p k x", p=P, x=P),
                            c.B[:, 1024:1024 + size].rearrange("p (k x) -> p k x", x=P)).then_inc(c.moved.sem, 16)
                e.wait_ge(c.moved.sem, c.moved.at(16))

            @block.tensor
            def _(e):
                for k in range(KBLOCKS):
                    for ps, at in ((rel_ps, c.B[:, 3072:]), (src_ps, c.B[:, 2048:])):
                        e.transpose(ps[:, k * P:k * P + P], at[:, k * P:k * P + P], c.ident[:, :])
                    last = e.transpose(w_ps[:, k * P:k * P + P], rows_w[:, k, :], c.ident[:, :])
                last.then_inc(c.small_pe.sem, 1)

            @block.vector
            def _(e):
                e.wait_ge(c.small_pe.sem, c.small_pe.at(1))
                e.tensor_copy(c.relK[:, :], rel_ps[:, 0:KCOLS])
                e.tensor_copy(c.srcK[:, :], src_ps[:, 0:KCOLS])
                e.tensor_copy(c.wK[:, :], w_ps[:, 0:KCOLS])
                e.memset(s[0:1, 0:1], -1.0)
                e.memset(s[0:1, 1:2], -2.0)
        c.small_pe.passed(1)
        c.moved.passed(16)
    with nc.Block() as block:
        @block.sync
        def _(e):
            e.dma_start(dram.seq[0:1].rearrange("(a b) -> a b", a=1), s[0:1, 0:1]).then_inc(c.moved.sem, 16)
            end = 1 + PAIRS * P
            e.dma_start(dram.seq[end:end + 1].rearrange("(a b) -> a b", a=1), s[0:1, 1:2]
                        ).then_inc(c.moved.sem, 16)
            e.wait_ge(c.moved.sem, c.moved.at(32))
    c.moved.passed(32)


def _node(nc, c, eng, pair):
    return nc.values_load(c.nRow[0:1, bass.ds(pair, 1)], engines=[eng.engine], min_val=0, max_val=WINDOWS - 1,
                          skip_runtime_bounds_check_because="it counts node tiles")


def _pass(c, kind, table, agg, width=D, attr=None, we=None, query=None, score=None):
    nc = c.nc
    cells = 1 if agg is None else agg.shape[1] // COLS
    win = None if agg is None else agg.rearrange("p (w x) -> p w x", w=WINDOWS)
    banks = 2 if kind in ("look", "attend") else RING
    used = c.joined if kind == "look" else c.product
    with ExitStack() as ctx:
        part = ctx.enter_context(nc.psum_tensor(c.name("part"), [P, banks, GROUP, cells * P], F32))
        if kind == "look":
            turned = ctx.enter_context(nc.psum_tensor(c.name("turned"), [P, 2, GROUP, P], F32))
        block = ctx.enter_context(nc.Block())

        if kind == "edge":
            @block.sync
            def _(e):
                with e.Fori(0, ROUNDS) as i:
                    for g in range(RING):
                        q = i * RING + g
                        tile = [nc.values_load(c.tRow[0:1, bass.ds(q * GROUP + r, 1)], engines=[e.engine],
                                               min_val=0, max_val=EDGE_TILES - 1,
                                               skip_runtime_bounds_check_because="clamped when it was made")
                                for r in range(GROUP)]
                        _hold(e, c.joined, q - RING + 1, c.tick_sp)
                        for r in range(GROUP):
                            e.dma_start(c.ebuf[:, g, r, :],
                                        attr[bass.ds(tile[r], 1), :, :].rearrange("a p f -> (a p) f")
                                        ).then_inc(c.attrs[g].sem, 16)

        if kind != "degree":
            @block.gpsimd
            def _(e):
                with e.Fori(0, ROUNDS) as i:
                    for g in range(RING):
                        _hold(e, c.index, i * RING + g + 1, c.tick_pool)
                        for r in range(GROUP):
                            e.indirect_dma_start(c.gbuf[:, g, r, 0:width], None, table,
                                                 bass.IndirectOffsetOnAxis(ap=c.idx[:, g, r:r + 1], axis=0)
                                                 ).then_inc(c.gathered[g].sem, 16)

            @block.scalar
            def _(e):
                def index(q, g):
                    _hold(e, used, q - RING + 1, c.tick_act)
                    e.copy(c.idx[:, g, :], c.srcK[:, bass.ds(q * GROUP, GROUP)]).then_inc(c.index.sem, 1)

                index(0, 0)
                index(1, 1)
                with e.Fori(0, ROUNDS) as i:
                    for g in range(RING):
                        q = i * RING + g
                        index(q + 2, (g + 2) % RING)
                        if kind == "edge":
                            e.wait_ge(c.joined.sem, c.joined.at(q + 1))
                            e.activation(c.gbuf[:, g, :, :], c.gbuf[:, g, :, :], ACT.Relu).then_inc(c.message.sem, 1)
                        elif kind == "look":
                            _hold(e, c.product, q - 1, c.tick_act)
                            e.wait_ge(c.turned.sem, c.turned.at(q + 1))
                            e.activation(c.ebuf[:, g % 2, :, :], turned[:, g % 2, :, :], ACT.Copy
                                         ).then_inc(c.message.sem, 1)

        @block.tensor
        def _(e):
            with e.Fori(0, ROUNDS) as i:
                for g in range(RING):
                    q = i * RING + g
                    b = g % banks
                    _hold(e, c.select, q + 1, c.tick_pe)
                    if kind == "look":
                        _hold(e, c.message, q - 1, c.tick_pe)
                        for r in range(GROUP):
                            last = e.transpose(turned[:, b, r, :], c.sel[:, g, r, :], c.ident[:, :])
                        last.then_inc(c.turned.sem, 1)
                        where = [_node(nc, c, e, q * GROUP + r) for r in range(GROUP)]
                        _hold(e, c.message, q + 1, c.tick_pe)
                        _hold(e, c.scored, q - 1, c.tick_pe)
                        for r in range(GROUP):
                            last = e.matmul(part[:, b, r, :], c.ebuf[:, b, r, :],
                                            query[:, bass.ds(where[r] * P, P)], start=True, stop=True)
                        last.then_inc(c.product.sem, 1)
                        continue
                    _hold(e, c.added, (q - banks + 1) * GROUP, c.tick_pe)
                    if kind == "sum":
                        _hold(e, c.gathered[g], 16 * GROUP * (i + 1), c.tick_pe)
                    elif kind == "edge":
                        _hold(e, c.message, q + 1, c.tick_pe)
                    elif kind == "attend":
                        _hold(e, c.scored, q + 1, c.tick_pe)
                    for r in range(GROUP):
                        lhs = c.ones[:, :] if kind == "degree" else \
                            c.gbuf[:, g, r, 0:width]
                        last = e.matmul(part[0:width, b, r, 0:P], lhs, c.sel[:, g, r, :], start=True, stop=True)
                        if kind == "attend":
                            last = e.matmul(part[:, b, r, P:2 * P], c.ebuf[:, g, r, :], c.sel[:, g, r, :],
                                            start=True, stop=True)
                    last.then_inc(c.product.sem, 1)

        @block.vector
        def _(e):
            def select(q, g):
                e.wait_ge(c.product.sem, c.product.at(q - RING + 1))
                e.tensor_tensor(c.sel[:, g, :, :],
                                c.relK[:, bass.ds(q * GROUP, GROUP)].unsqueeze(2).to_broadcast([P, GROUP, P]),
                                c.iota[:, :].unsqueeze(1).to_broadcast([P, GROUP, P]), ALU.is_equal
                                ).then_inc(c.select.sem, 1)

            def prepare(q, g, i):
                if kind in ("degree", "sum"):
                    return
                _hold(e, c.gathered[g], 16 * GROUP * (i + 1), c.tick_dve)
                if kind == "edge":
                    _hold(e, c.attrs[g], 16 * GROUP * (i + 1), c.tick_dve)
                    e.tensor_tensor(c.gbuf[:, g, :, :], c.gbuf[:, g, :, :], c.ebuf[:, g, :, :], ALU.add
                                    ).then_inc(c.joined.sem, 1)
                    return
                for r in range(GROUP):
                    e.scalar_tensor_tensor(c.gbuf[:, g, r, :], we, c.wK[:, bass.ds(q * GROUP + r, 1)],
                                           c.gbuf[:, g, r, :], ALU.mult, ALU.add).then_inc(c.keyed.sem, 1)
                if kind == "look":
                    _hold(e, c.keyed, (q + 1) * GROUP, c.tick_dve)
                    e.wait_ge(c.product.sem, c.product.at(q + 1))
                    e.tensor_tensor(c.gbuf[:, g, :, :], c.gbuf[:, g, :, :], part[:, g % 2, :, :], ALU.mult
                                    ).then_inc(c.scored.sem, 1)
                    _hold(e, c.scored, q + 1, c.tick_dve)
                    e.tensor_reduce(score[:, bass.ds(q * GROUP * HEADS, GROUP * HEADS)],
                                    c.gbuf[:, g, :, :].rearrange("p r (h x) -> p (r h) x", h=HEADS),
                                    AX.X, ALU.add).then_inc(c.joined.sem, 1)
                else:
                    _hold(e, c.product, q - RING + 1, c.tick_dve)
                    e.tensor_copy(c.ebuf[:, g, :, :].rearrange("p r (h x) -> p (r h) x", h=HEADS),
                                  score[:, bass.ds(q * GROUP * HEADS, GROUP * HEADS)].unsqueeze(2
                                  ).to_broadcast([P, GROUP * HEADS, HEAD])).then_inc(c.expanded.sem, 1)
                    _hold(e, c.keyed, (q + 1) * GROUP, c.tick_dve)
                    _hold(e, c.expanded, q + 1, c.tick_dve)
                    e.tensor_tensor(c.gbuf[:, g, :, :], c.gbuf[:, g, :, :], c.ebuf[:, g, :, :], ALU.mult
                                    ).then_inc(c.scored.sem, 1)

            def add(q, g):
                where = [_node(nc, c, e, q * GROUP + r) for r in range(GROUP)]
                _hold(e, c.product, q + 1, c.tick_dve)
                for r in range(GROUP):
                    into = win[0:width, bass.ds(where[r], 1), :].rearrange("p a x -> p (a x)")
                    e.wait_ge(c.added.sem, c.added.at(q * GROUP + r))
                    e.tensor_tensor(into, into, part[0:width, g % banks, r, :], ALU.add
                                    ).then_inc(c.added.sem, 1)

            if agg is None:
                select(0, 0)
                with e.Fori(0, ROUNDS) as i:
                    for g in range(RING):
                        q = i * RING + g
                        select(q + 1, (g + 1) % RING)
                        prepare(q, g, i)
                return
            e.memset(agg, 0.0).then_inc(c.cleared.sem, 1)
            e.wait_ge(c.cleared.sem, c.cleared.at(1))
            select(0, 0)
            select(1, 1)
            prepare(0, 0, 0)

            def steps(i, last):
                for g in range(RING):
                    q = i * RING + g
                    left = RING - 1 - g if last else RING
                    if left > 1:
                        select(q + 2, (g + 2) % RING)
                    if left > 0:
                        prepare(q + 1, (g + 1) % RING, i + (g + 1) // RING)
                    add(q, g)
            with e.Fori(0, ROUNDS - 1) as i:
                steps(i, False)
            steps(ROUNDS - 1, True)

    c.product.passed(GROUPS)
    c.select.passed(GROUPS + (agg is None))
    if agg is not None:
        c.added.passed(PAIRS)
        c.cleared.passed(1)
    if kind != "degree":
        c.index.passed(GROUPS + 2)
        for g in c.gathered:
            g.passed(16 * GROUP * ROUNDS)
    if kind == "edge":
        for g in c.attrs:
            g.passed(16 * GROUP * ROUNDS)
    if kind in ("edge", "look"):
        c.joined.passed(GROUPS)
        c.message.passed(GROUPS)
    if kind in ("look", "attend"):
        c.scored.passed(GROUPS)
        c.keyed.passed(PAIRS)
    if kind == "look":
        c.turned.passed(GROUPS)
    if kind == "attend":
        c.expanded.passed(GROUPS)


def _chunk(i, size=CHUNK):
    return bass.ds(i * size, size)


def _load(c, *pairs):
    with c.nc.Block() as block:
        @block.sync
        def _(e):
            for dst, src in pairs:
                e.dma_start(dst, src).then_inc(c.loaded.sem, 16)
            c.loaded.passed(16 * len(pairs))
            e.wait_ge(c.loaded.sem, c.loaded.at(0))


def _dense(c, parts, prepare=None, groups=1):
    nc = c.nc
    rounds = CHUNKS // 2
    with nc.psum_tensor(c.name("dense"), [P, 2, len(parts), 512], F32) as ps, nc.Block() as block:
        @block.scalar
        def _(e):
            def ready(i):
                for x, scale, shift in prepare or ():
                    e.activation(x[:, _chunk(i)], x[:, _chunk(i)], ACT.Relu, bias=shift, scale=scale
                                 ).then_inc(c.applied.sem, 1)
            ready(0)
            def steps(i, b, last):
                if not last:
                    ready(i + 1)
                _hold(e, c.product, i + 1, c.tick_act)
                for o, (_, out, bias, scale, rows) in enumerate(parts):
                    kw = {} if bias is None else {"bias": bias}
                    e.activation(out[0:rows, _chunk(i)], ps[0:rows, b, o, 0:CHUNK],
                                 ACT.Copy if bias is None else ACT.Identity, scale=scale, **kw
                                 ).then_inc(c.chunked.sem, 1)
            with e.Fori(0, rounds - 1) as i:
                steps(i * 2, 0, False)
                steps(i * 2 + 1, 1, False)
            steps(CHUNKS - 2, 0, False)
            steps(CHUNKS - 1, 1, True)

        @block.tensor
        def _(e):
            with e.Fori(0, rounds) as i:
                for b in range(2):
                    n = i * 2 + b
                    _hold(e, c.chunked, (n - 1) * len(parts), c.tick_pe)
                    if prepare:
                        _hold(e, c.applied, (n + 1) * len(prepare), c.tick_pe)
                    for o, (terms, _, _, _, rows) in enumerate(parts):
                        for j, (w, x) in enumerate(terms):
                            last = e.matmul(ps[0:rows, b, o, 0:CHUNK], w, x[0:w.shape[0], _chunk(n)],
                                            start=j == 0, stop=j == len(terms) - 1)
                    last.then_inc(c.product.sem, 1)
    c.product.passed(CHUNKS)
    c.chunked.passed(CHUNKS * len(parts))
    if prepare:
        c.applied.passed(CHUNKS * len(prepare))


def _whole(c, *steps):
    with c.nc.Block() as block:
        def run(mine, eng):
            for who, make in steps:
                if who == mine:
                    make(eng).then_inc(c.whole.sem, 1)
                c.whole.passed(1)
                eng.wait_ge(c.whole.sem, c.whole.at(0))
            c.whole.passed(-len(steps))

        @block.vector
        def _(e):
            run("v", e)

        @block.scalar
        def _(e):
            run("s", e)
    c.whole.passed(len(steps))


def _table(c, x, out, width=D):
    nc = c.nc
    to_dram = out.shape[0] != P
    size = TURN * P
    steps = WINDOWS // TURN
    stage = c.sel[:, :, :, :].rearrange("p a b x -> p (a b x)")
    rows = c.ebuf[:, :, :, :].rearrange("p a b x -> p (a b x)")
    with nc.psum_tensor(c.name("turn"), [P, 2, 1024], F32) as ps, nc.Block() as block:
        @block.vector
        def _(e):
            with e.Fori(0, steps // 2) as i:
                for b in range(2):
                    n = i * 2 + b
                    _hold(e, c.turned, n - 1, c.tick_dve)
                    e.tensor_copy(stage[0:width, b * size:b * size + size], x[0:width, _chunk(n, size)]
                                  ).then_inc(c.staged.sem, 1)

        @block.tensor
        def _(e):
            with e.Fori(0, steps // 2) as i:
                for b in range(2):
                    n = i * 2 + b
                    _hold(e, c.staged, n + 1, c.tick_pe)
                    _hold(e, c.chunked, n - 1, c.tick_pe)
                    for t in range(TURN):
                        at = b * size + t * P
                        last = e.transpose(ps[:, b, t * width:t * width + width], stage[0:width, at:at + P],
                                           c.ident[0:width, 0:width])
                    last.then_inc(c.turned.sem, 1)

        @block.scalar
        def _(e):
            with e.Fori(0, steps // 2) as i:
                for b in range(2):
                    n = i * 2 + b
                    got = ps[:, b, 0:TURN * width]
                    _hold(e, c.turned, n + 1, c.tick_act)
                    if to_dram:
                        _hold(e, c.sent, n - 1, c.tick_act)
                        e.copy(rows[:, b * size:b * size + TURN * width], got).then_inc(c.chunked.sem, 1)
                    else:
                        e.copy(out[:, _chunk(n, size)], got).then_inc(c.chunked.sem, 1)

        if to_dram:
            view = out.rearrange("(n t p) f -> n p t f", p=P, t=TURN)

            @block.sync
            def _(e):
                with e.Fori(0, steps // 2) as i:
                    for b in range(2):
                        n = i * 2 + b
                        _hold(e, c.chunked, n + 1, c.tick_sp)
                        e.dma_start(view[bass.ds(n, 1), :, :, :].rearrange("a p t f -> (a p) t f"),
                                    rows[:, b * size:b * size + TURN * width].rearrange("p (t f) -> p t f", t=TURN)
                                    ).then_inc(c.stored[b].sem, 16)
                        _hold(e, c.stored[b], 16 * (i + 1), c.tick_sp)
                        e.sem_inc(c.sent.sem, 1)
    c.staged.passed(steps)
    c.turned.passed(steps)
    c.chunked.passed(steps)
    if to_dram:
        c.sent.passed(steps)
        for g in c.stored:
            g.passed(16 * (steps // 2))


def _norm(c, x):
    nc = c.nc
    sq = c.gbuf[:, 0:2, :, :].rearrange("p a b x -> p a (b x)")
    root = c.gbuf[:, 2:4, :, :].rearrange("p a b x -> p a (b x)")
    with nc.psum_tensor(c.name("mean"), [P, 2, 512], F32) as mean_ps, \
            nc.psum_tensor(c.name("var"), [P, 2, 512], F32) as var_ps, nc.Block() as block:
        @block.tensor
        def _(e):
            with e.Fori(0, CHUNKS // 2) as i:
                for b in range(2):
                    n = i * 2 + b
                    _hold(e, c.centred, n - 1, c.tick_pe)
                    e.matmul(mean_ps[:, b, 0:CHUNK], c.mean[:, :], x[:, _chunk(n)], start=True, stop=True
                             ).then_inc(c.meaned.sem, 1)
                    _hold(e, c.squared, n + 1, c.tick_pe)
                    _hold(e, c.rooted, n - 1, c.tick_pe)
                    e.matmul(var_ps[:, b, 0:CHUNK], c.mean[:, :], sq[:, b, 0:CHUNK], start=True, stop=True
                             ).then_inc(c.varied.sem, 1)

        @block.scalar
        def _(e):
            with e.Fori(0, CHUNKS // 2) as i:
                for b in range(2):
                    n = i * 2 + b
                    _hold(e, c.varied, n - 1, c.tick_act)
                    _hold(e, c.centred, n + 1, c.tick_act)
                    e.activation(sq[:, b, 0:CHUNK], x[:, _chunk(n)], ACT.Square).then_inc(c.squared.sem, 1)
                    _hold(e, c.applied, n - 1, c.tick_act)
                    _hold(e, c.varied, n + 1, c.tick_act)
                    e.activation(root[:, b, 0:CHUNK], var_ps[:, b, 0:CHUNK], ACT.Sqrt, bias=c.eps[:, :]
                                 ).then_inc(c.rooted.sem, 1)

        @block.vector
        def _(e):
            with e.Fori(0, CHUNKS // 2) as i:
                for b in range(2):
                    n = i * 2 + b
                    _hold(e, c.meaned, n + 1, c.tick_dve)
                    e.tensor_tensor(x[:, _chunk(n)], x[:, _chunk(n)], mean_ps[:, b, 0:CHUNK], ALU.subtract
                                    ).then_inc(c.centred.sem, 1)
                    _hold(e, c.rooted, n + 1, c.tick_dve)
                    e.reciprocal(root[:, b, 0:CHUNK], root[:, b, 0:CHUNK]).then_inc(c.scored.sem, 1)
                    _hold(e, c.scored, n + 1, c.tick_dve)
                    e.tensor_tensor(x[:, _chunk(n)], x[:, _chunk(n)], root[:, b, 0:CHUNK], ALU.mult
                                    ).then_inc(c.applied.sem, 1)
    for g in (c.centred, c.meaned, c.squared, c.varied, c.rooted, c.scored, c.applied):
        g.passed(CHUNKS)


def _batch(c, halves, out):
    nc = c.nc
    with nc.Block() as block:
        @block.vector
        def _(e):
            for h, (x, _, _) in enumerate(halves):
                with e.Fori(0, FULL) as i:
                    e.bn_stats(c.stats[:, h, bass.ds(i * 6, 6)], x[:, _chunk(i)]).then_inc(c.varied.sem, 1)
                e.bn_stats(c.stats[:, h, FULL * 6:FULL * 6 + 6], x[:, FULL * CHUNK:N]).then_inc(c.varied.sem, 1)
            e.wait_ge(c.varied.sem, c.varied.at((FULL + 1) * len(halves)))
    c.varied.passed((FULL + 1) * len(halves))
    steps = []
    for h, (x, gain, offset) in enumerate(halves):
        mv = c.small[:, 8 * h + 2:8 * h + 4]
        root = c.small[:, 8 * h + 4:8 * h + 5]
        scale, shift = out[h]
        steps += [
            ("v", lambda e, h=h, mv=mv: e.bn_aggr(mv, c.stats[:, h, :])),
            ("s", lambda e, mv=mv, root=root: e.activation(root, mv[:, 1:2], ACT.Sqrt, bias=c.eps[:, :])),
            ("v", lambda e, root=root: e.reciprocal(root, root)),
            ("v", lambda e, root=root, s=scale, g=gain: e.tensor_tensor(s, root, g, ALU.mult)),
            ("v", lambda e, root=root, s=scale, mv=mv: e.tensor_tensor(root, mv[:, 0:1], s, ALU.mult)),
            ("v", lambda e, root=root, t=shift, o=offset: e.tensor_tensor(t, o, root, ALU.subtract)),
        ]
    _whole(c, *steps)


def _softmax(c, score, dram):
    nc = c.nc
    flags = c.DE[:, 0:SEQ + 2]
    new = c.DE[:, SEQ + 2:2 * SEQ + 3]
    run = c.DE[:, 2 * SEQ + 4:3 * SEQ + 4]
    alpha = c.soft
    rows = c.rows
    cols = c.small[:, 32:40]
    view = score.rearrange("p (c j h) -> p j h c", h=HEADS, j=SEQ_PAIRS)
    with nc.Block() as block:
        @block.sync
        def _(e):
            src = dram.seq[0:SEQ_ROWS * SEQ].rearrange("(c x) -> c x", x=SEQ)
            wide = bass.AP(src.tensor, src.offset, [[SEQ, SEQ_ROWS], [1, SEQ + 2]])
            for h in range(HEADS):
                e.dma_start(flags[h * SEQ_ROWS:(h + 1) * SEQ_ROWS, :], wide).then_inc(c.moved.sem, 16)
            e.wait_ge(c.moved.sem, c.moved.at(16 * HEADS))
    c.moved.passed(16 * HEADS)
    turns = [(a, min(a + 8, SEQ_PAIRS)) for a in range(0, SEQ_PAIRS, 8)]

    def turned(forward):
        with nc.psum_tensor(c.name("soft"), [P, 2, 8 * P], F32) as ps, nc.Block() as block:
            @block.tensor
            def _(e):
                for n, (a, z) in enumerate(turns):
                    e.wait_ge(c.chunked.sem, c.chunked.at(n - 1))
                    for j in range(a, z):
                        at = ps[:, n % 2, (j - a) * P:(j - a + 1) * P]
                        if forward:
                            last = e.transpose(at, run[:, j * P:(j + 1) * P], c.ident[:, :])
                        else:
                            last = e.transpose(at, alpha[:, j * P:(j + 1) * P], c.ident[:, :])
                    last.then_inc(c.turned.sem, 1)

            @block.scalar
            def _(e):
                for n, (a, z) in enumerate(turns):
                    e.wait_ge(c.turned.sem, c.turned.at(n + 1))
                    if forward:
                        e.copy(alpha[:, a * P:z * P], ps[:, n % 2, 0:(z - a) * P]).then_inc(c.chunked.sem, 1)
                        continue
                    for h in range(HEADS):
                        k = e.copy(view[:, a:z, h, :],
                                   ps[:, n % 2, 0:(z - a) * P].rearrange("p (j h c) -> p j h c", h=HEADS,
                                                                         c=SEQ_ROWS)[:, :, h, :])
                    k.then_inc(c.chunked.sem, 1)
        c.turned.passed(len(turns))
        c.chunked.passed(len(turns))

    _whole(c, *(("v", lambda e, h=h: e.tensor_copy(
        run.rearrange("p (j h c) -> p j h c", h=HEADS, c=SEQ_ROWS)[:, :, h, :], view[:, :, h, :]))
        for h in range(HEADS)))
    turned(True)
    _whole(c,
           ("v", lambda e: e.tensor_tensor(new, flags[:, 1:SEQ + 2], flags[:, 0:SEQ + 1], ALU.not_equal)),
           ("v", lambda e: e.tensor_scalar(new, new, FAR, None, ALU.mult)))

    for back in (False, True):
        data = run if back else alpha
        if back:
            fence, line = new[:, 1:SEQ + 1][:, ::-1], run[:, ::-1]
            end = run[:, 0:1]
        else:
            fence, line = new[:, 0:SEQ], alpha
            end = run[:, SEQ - 1:SEQ]
        out = run[:, ::-1] if back else run
        _whole(c,
               ("v", lambda e: e.tensor_tensor_scan(out, fence, line, FAR, ALU.add, ALU.max)),
               ("v", lambda e: e.tensor_copy(cols[:, 0:1], end)),
               ("v", lambda e: e.tensor_reduce(cols[:, 1:2], new[:, 1:SEQ + 1] if back else new[:, 0:SEQ],
                                               AX.X, ALU.min)))
        with nc.psum_tensor(c.name("carry"), [P, 2 * P + 8], F32) as ps:
            with nc.Block() as block:
                @block.tensor
                def _(e):
                    e.transpose(ps[0:1, 0:P], cols[:, 0:1], c.ident[:, :])
                    e.transpose(ps[0:1, P:2 * P], cols[:, 1:2], c.ident[:, :]).then_inc(c.small_pe.sem, 1)
            c.small_pe.passed(1)
            best, shut = rows[:, 0:P], rows[:, P:2 * P]
            carry = rows[:, 2 * P:3 * P + 2]
            if back:
                chain = ("v", lambda e: e.tensor_tensor_scan(carry[:, 0:P][:, ::-1], shut[:, ::-1], best[:, ::-1],
                                                             FAR, ALU.add, ALU.max))
                enter = carry[:, 1:P + 1]
            else:
                chain = ("v", lambda e: e.tensor_tensor_scan(carry[:, 1:P + 1], shut, best, FAR,
                                                             ALU.add, ALU.max))
                enter = carry[:, 0:P]
            _whole(c,
                   ("v", lambda e: e.tensor_copy(rows[:, 0:2 * P], ps[0:1, 0:2 * P])),
                   ("v", lambda e: e.memset(carry, FAR)),
                   chain)
            with nc.Block() as block:
                @block.tensor
                def _(e):
                    e.transpose(ps[:, 2 * P:2 * P + 1], enter, c.ident[0:1, 0:1]).then_inc(c.small_pe.sem, 1)
            c.small_pe.passed(1)
            _whole(c,
                   ("v", lambda e: e.tensor_copy(cols[:, 2:3], ps[:, 2 * P:2 * P + 1])),
                   ("v", lambda e: e.tensor_tensor_scan(out, fence, line, cols[:, 2:3], ALU.add, ALU.max)))
    _whole(c,
           ("v", lambda e: e.tensor_tensor(alpha, alpha, run, ALU.subtract)),
           ("s", lambda e: e.activation(alpha, alpha, ACT.Exp)))
    turned(False)


def build(nc, ins, out):
    with ExitStack() as ctx:
        c = _setup(ctx, nc)
        dram = Ctx()
        dram.t = nc.dram_tensor("walk_edge", [KCOLS], I32, kind="Internal").ap()
        dram.n = nc.dram_tensor("walk_node", [KCOLS], I32, kind="Internal").ap()
        dram.seq = nc.dram_tensor("walk_dst", [KCOLS * P + 2], F32, kind="Internal").ap()
        hid = nc.dram_tensor("rows_hidden", [COLS, HID], F32, kind="Internal").ap()
        keys = nc.dram_tensor("rows_key", [COLS, D], F32, kind="Internal").ap()
        values = nc.dram_tensor("rows_value", [COLS, D], F32, kind="Internal").ap()
        A, B, C, D_, E_, F, DE = c.A[:, :], c.B[:, :], c.C[:, :], c.D, c.E, c.F[:, :], c.DE[:, :]
        column = {name: c.cols[:, i:i + w] for name, (i, w) in ins["at"].items()}

        def vv(out_, a, b, op):
            return ("v", lambda e: e.tensor_tensor(out_, a, b, op))

        _start(c, ins)
        _walk(c, ins, dram)

        _pass(c, "degree", None, C)
        h = slice(0, HID)
        _whole(c,
               ("v", lambda e: e.tensor_scalar(F, C, 1.0, None, ALU.add)),
               ("s", lambda e: e.activation(F, F, ACT.Sqrt)),
               ("v", lambda e: e.reciprocal(F, F)),
               ("v", lambda e: e.tensor_scalar(C, C, 1.0, None, ALU.max)),
               ("v", lambda e: e.reciprocal(C, C)))
        _dense(c, [([(c.W1g[:, :], A)], B, None, 1.0, HID)])
        _whole(c, vv(B[h, :], B[h, :], F[h, :], ALU.mult))
        _table(c, B, hid, HID)
        _pass(c, "sum", hid, D_, HID)
        _whole(c, vv(D_[h, :], D_[h, :], B[h, :], ALU.add),
               vv(D_[h, :], D_[h, :], F[h, :], ALU.mult),
               ("s", lambda e: e.activation(B[h, :], D_[h, :], ACT.Relu, bias=column["L0_gnn_b1"][h, :])),
               vv(B[h, :], B[h, :], F[h, :], ALU.mult))
        _table(c, B, hid, HID)
        _pass(c, "sum", hid, D_, HID)
        _whole(c, vv(D_[h, :], D_[h, :], B[h, :], ALU.add),
               vv(D_[h, :], D_[h, :], F[h, :], ALU.mult))
        _dense(c, [([(c.W2g[:, :], D_)], B, column["L0_gnn_b2"], 1.0, P)])
        _whole(c, vv(A, A, B, ALU.add))
        _norm(c, A)

        _table(c, A, keys)
        _pass(c, "sum", keys, D_)
        _whole(c, vv(D_, D_, C, ALU.mult), vv(D_, D_, A, ALU.add))
        _dense(c, [([(c.W1T[:, :], D_)], B, column["L1_gnn_b"], 1.0, P)])
        _whole(c, ("s", lambda e: e.activation(B, B, ACT.Relu)), vv(A, A, B, ALU.add))
        _norm(c, A)

        _dense(c, [([(c.encW[:, :], A)], B, column["L2_gnn_enc_b"], 1.0, P)])
        attr = ins["attr"]
        E2 = E_
        for layer in range(LAYERS):
            def col(name, n, w=1):
                return column[name][:, n:n + w]
            coef = [(c.small[:, 20 + 2 * j:21 + 2 * j], c.small[:, 21 + 2 * j:22 + 2 * j]) for j in range(3)]
            _table(c, B, keys)
            _pass(c, "edge", keys, D_, attr=attr)
            _whole(c, vv(D_, D_, B, ALU.add))
            _load(c, (c.W1[:, :], ins["L2_gnn_W1"][layer, :, :]),
                  (c.W2[:, :, :], ins["L2_gnn_W2"][layer, :, :].rearrange("(h k) m -> k h m", h=2)))
            _dense(c, [([(c.W1[:, j * P:(j + 1) * P], D_)], (E2, F)[j],
                        col("L2_gnn_b1", 2 * layer + j), 1.0, P) for j in range(2)])
            _batch(c, [((E2, F)[j], col("L2_gnn_bn1_g", 2 * layer + j), col("L2_gnn_bn1_b", 2 * layer + j))
                       for j in range(2)], coef[0:2])
            _dense(c, [([(c.W2[:, j, :], (E2, F)[j]) for j in range(2)], D_,
                        col("L2_gnn_b2", layer), 1.0, P)],
                   prepare=[((E2, F)[j], *coef[j]) for j in range(2)])
            _batch(c, [(D_, col("L2_gnn_bn_g", layer), col("L2_gnn_bn_b", layer))], coef[2:3])
            act = ACT.Relu if layer < LAYERS - 1 else ACT.Identity
            _whole(c, ("s", lambda e: e.activation(D_, D_, act, bias=coef[2][1], scale=coef[2][0])),
                   vv(B, B, D_, ALU.add))
        _whole(c, vv(A, A, B, ALU.add))
        _norm(c, A)

        score = c.F[:, 0:PAIRS * HEADS]
        x = A
        for conv in range(2):
            tag = str(conv + 1)
            _load(c, *((c.W3[:, j, :], ins[f"L3_gnn_W{w}{tag}"]) for j, w in enumerate("qkvs")))
            _dense(c, [([(c.W3[:, 1, :], x)], D_, column["L3_gnn_bk" + tag], 1.0, P),
                       ([(c.W3[:, 2, :], x)], E_, column["L3_gnn_bv" + tag], 1.0, P),
                       ([(c.W3[:, 0, :], x)], F, column["L3_gnn_bq" + tag], 1.0, P)])
            _table(c, D_, keys)
            _table(c, E_, values)
            _whole(c, ("s", lambda e: e.activation(F, F, ACT.Copy, scale=HEAD ** -0.5)))
            _table(c, F, B)
            _dense(c, [([(c.W3[:, 3, :], x)], C, column["L3_gnn_bs" + tag], 1.0, P)])
            _pass(c, "look", keys, None, we=c.We[:, conv, :], query=B, score=score)
            _softmax(c, score, dram)
            _pass(c, "attend", values, DE, we=c.We[:, conv, :], score=score)
            pairs = DE.rearrange("p (w b x) -> p w b x", w=WINDOWS, b=2)
            up, down = pairs[:, :, 0, :], pairs[:, :, 1, :]
            wide = C.rearrange("p (w x) -> p w x", w=WINDOWS)
            _whole(c,
                   ("v", lambda e: e.tensor_scalar(down, down, 1e-30, None, ALU.max)),
                   ("v", lambda e: e.reciprocal(down, down)),
                   ("v", lambda e: e.tensor_tensor(up, up, down, ALU.mult)),
                   ("v", lambda e: e.tensor_tensor(wide, wide, up, ALU.add)))
            x = C
        _whole(c, vv(A, A, C, ALU.add))
        _norm(c, A)
        with nc.Block() as block:
            @block.sync
            def _(e):
                e.dma_start(out, A).then_inc(c.moved.sem, 16)
                e.wait_ge(c.moved.sem, c.moved.at(16))


_COLUMNS = ["L0_gnn_b1", "L0_gnn_b2", "L1_gnn_b", "L2_gnn_enc_b", "L2_gnn_b1", "L2_gnn_bn1_g", "L2_gnn_bn1_b",
            "L2_gnn_b2", "L2_gnn_bn_g", "L2_gnn_bn_b", "L3_gnn_bq1", "L3_gnn_bk1", "L3_gnn_bv1", "L3_gnn_bs1",
            "L3_gnn_bq2", "L3_gnn_bk2", "L3_gnn_bv2", "L3_gnn_bs2"]


def kernel(**inputs):
    import numpy as np
    import concourse.bacc as bacc
    from concourse.bass_utils import run_bass_kernel_spmd

    nc = bacc.Bacc("TRN2", target_bir_lowering=False, num_devices=1)
    given = {k: np.asarray(v) for k, v in inputs.items()}
    x_cols = np.zeros((P, COLS), np.float32)
    x_cols[:, :N] = given["x"].T
    arrays = {"xT": x_cols}
    for name, key, fill in (("src", "src", 0), ("dst", "dst", PAD_NODE), ("edge_weight", "w", 0)):
        tiles = np.full((EDGE_TILES * P,), fill, given[name].dtype)
        tiles[:E] = given[name]
        arrays[key] = tiles.reshape(EDGE_TILES, P)
    attr = np.zeros((EDGE_TILES * P, D), np.float32)
    attr[:E] = given["edge_attr_128"]
    arrays["attr"] = attr.reshape(EDGE_TILES, P, D)
    arrays["L1_W_T"] = np.ascontiguousarray(given["L1_gnn_W"].T)
    for name in ("L0_gnn_W1", "L0_gnn_W2", "L2_gnn_enc_W", "L2_gnn_W1", "L2_gnn_W2"):
        arrays[name] = given[name]
    for i in (1, 2):
        for w in ("Wq", "Wk", "Wv", "Ws", "We"):
            arrays[f"L3_gnn_{w}{i}"] = given[f"L3_gnn_{w}{i}"]
    columns, at = [], {}
    for name in _COLUMNS:
        v = given[name].reshape(-1)
        width = -(-v.size // P)
        block = np.zeros((width * P,), np.float32)
        block[:v.size] = v
        at[name] = (sum(b.shape[1] for b in columns), width)
        columns.append(block.reshape(width, P).T)
    arrays["cols"] = np.concatenate(columns, axis=1)
    ins = {"at": at}
    for name, a in arrays.items():
        arrays[name] = np.ascontiguousarray(a)
        ins[name] = nc.dram_tensor(f"in_{name}", a.shape, mybir.dt.from_np(a.dtype), kind="ExternalInput").ap()
    out = nc.dram_tensor("out_0", (P, COLS), F32, kind="ExternalOutput").ap()
    build(nc, ins, out)
    r = run_bass_kernel_spmd(nc, [{f"in_{k}": v for k, v in arrays.items()}], core_ids=[0])
    return np.ascontiguousarray(r.results[0]["out_0"][:, :N].T)
```

```python
import concourse.bass as bass
import concourse.mybir as mybir
from contextlib import ExitStack

F32 = mybir.dt.float32
I32 = mybir.dt.int32
BF16 = mybir.dt.bfloat16
ALU = mybir.AluOpType
ACT = mybir.ActivationFunctionType
AX = mybir.AxisListType

P = 128
N, E, D, HID = 6250, 100000, 128, 64
LAYERS, HEADS, HEAD = 5, 4, 32
EDGE_TILES = -(-E // P)
NODE_TILES = -(-N // P)
WINDOWS = NODE_TILES + 1
COLS = WINDOWS * P
GROUP = 4
RING = 4
PAIRS = -(-(EDGE_TILES + NODE_TILES - 1) // (GROUP * RING)) * GROUP * RING
GROUPS = PAIRS // GROUP
ROUNDS = GROUPS // RING
KBLOCKS = -(-(PAIRS + 2 * GROUP) // P)
KCOLS = KBLOCKS * P
CHUNK = 400
CHUNKS = COLS // CHUNK
FULL = N // CHUNK
TURN = 5
SEQ_ROWS = 32
SEQ = PAIRS * P // SEQ_ROWS
SEQ_PAIRS = PAIRS // SEQ_ROWS
FAR = -1.0e30
EPS = 1e-5
CREDIT = 64
PAD_NODE = WINDOWS * P


class Gate:

    def __init__(self, ctx, nc, name, credit=CREDIT):
        self.sem = ctx.enter_context(nc.semaphore(name))
        self.base = credit
        self.credit = credit

    def at(self, n):
        return self.base + n

    def passed(self, n):
        self.base += n


class Ctx:
    pass


def _setup(ctx, nc):
    c = Ctx()
    c.nc = nc

    def sb(name, shape, dt=F32):
        return ctx.enter_context(nc.sbuf_tensor(name, shape, dt))

    c.A = sb("bigA", [P, COLS])
    c.Bwide = sb("bigB", [P, WINDOWS * (D + HEADS)])
    c.B = c.Bwide[:, 0:COLS]
    c.C = sb("bigC", [P, COLS])
    c.DE = sb("bigDE", [P, 2 * COLS])
    c.D = c.DE[:, 0:COLS]
    c.E = c.DE[:, COLS:2 * COLS]
    c.F = sb("bigF", [P, COLS])
    rings = sb("rings", [P, 3 * RING * GROUP * P])
    c.gbuf, c.ebuf, c.sel = (
        rings[:, i * RING * GROUP * P:(i + 1) * RING * GROUP * P].rearrange("p (a b x) -> p a b x", a=RING, b=GROUP)
        for i in range(3))
    c.soft = rings[:, 0:SEQ]
    c.rows = c.DE[0:1, 3 * SEQ + 8:3 * SEQ + 8 + 3 * P + 2]
    c.idx = sb("idx", [P, RING, GROUP], I32)
    c.srcK = sb("srcK", [P, KCOLS], I32)
    c.relK = sb("relK", [P, KCOLS])
    c.wK = sb("wK", [P, KCOLS])
    c.tRow = sb("tRow", [1, KCOLS], I32)
    c.nRow = sb("nRow", [1, KCOLS], I32)
    c.ident = sb("ident", [P, P])
    c.ones = sb("ones", [P, P])
    c.mean = sb("mean", [P, P])
    c.iota = sb("iota", [P, P])
    c.small = sb("small", [P, 64])
    c.eps = sb("eps", [P, 1])
    c.stats = sb("stats", [P, 2, (FULL + 1) * 6])
    c.W1g = sb("W1g", [P, HID])
    c.W2g = sb("W2g", [HID, D])
    c.W1T = sb("W1T", [P, D])
    c.encW = sb("encW", [P, D])
    c.W1 = sb("W1", [P, 2 * D])
    c.W2 = sb("W2", [P, 2, D])
    c.W3 = sb("W3", [P, 4, D])
    c.We = sb("We", [P, 2, D])
    c.cols = sb("cols", [P, 64])
    c.gates = {}

    def gate(name, credit=CREDIT):
        g = Gate(ctx, nc, name, credit)
        c.gates[name] = g
        return g

    c.index = gate("index")
    c.select = gate("select")
    c.joined = gate("joined")
    c.message = gate("message")
    c.product = gate("product")
    c.added = gate("added")
    c.turned = gate("turned")
    c.scored = gate("scored")
    c.centred = gate("centred")
    c.squared = gate("squared")
    c.varied = gate("varied")
    c.rooted = gate("rooted")
    c.chunked = gate("chunked")
    c.meaned = gate("meaned")
    c.small_dve = gate("small_dve")
    c.small_pe = gate("small_pe")
    c.small_pool = gate("small_pool")
    c.tick_pe = gate("tick_pe")
    c.tick_act = gate("tick_act")
    c.tick_dve = gate("tick_dve")
    c.tick_pool = gate("tick_pool")
    c.tick_sp = gate("tick_sp")
    c.staged = gate("staged")
    c.cleared = gate("cleared")
    c.applied = gate("applied")
    c.keyed = gate("keyed")
    c.expanded = gate("expanded")
    c.fed = gate("fed")
    c.kept = gate("kept")
    c.counted = gate("counted")
    c.told = gate("told")
    c.gathered = [gate(f"gathered{i}", 0) for i in range(RING)]
    c.attrs = [gate(f"attrs{i}", 0) for i in range(RING)]
    c.loaded = gate("loaded", 0)
    c.stored = [gate(f"stored{i}", 0) for i in range(2)]
    c.spilled = [gate(f"spilled{i}", 0) for i in range(RING)]
    c.moved = gate("moved", 0)
    c.whole = gate("whole")
    c.names = [0]

    def name(what):
        c.names[0] += 1
        return f"{what}_{c.names[0]}"
    c.name = name
    return c


def _hold(eng, gate, n, tick=None):
    v = gate.at(n)
    eng.wait_ge(gate.sem, v)
    if tick is not None and not isinstance(v, int):
        eng.sem_inc(tick.sem, 1)


def _small(c, eng, gate, count, make):
    make().then_inc(gate.sem, 1)
    gate.passed(1)
    eng.wait_ge(gate.sem, gate.at(0))


def _start(c, ins):
    nc = c.nc
    loads = [
        (c.A[:, :], ins["xT"]),
        (c.W1g[:, :], ins["L0_gnn_W1"]), (c.W2g[:, :], ins["L0_gnn_W2"]), (c.W1T[:, :], ins["L1_W_T"]),
        (c.encW[:, :], ins["L2_gnn_enc_W"]),
        (c.cols[:, 0:ins["cols"].shape[1]], ins["cols"]),
    ]
    for i in (0, 1):
        loads.append((c.We[:, i, :], ins[f"L3_gnn_We{i + 1}"].to_broadcast([P, D])))
    with nc.Block() as block:
        @block.sync
        def _(e):
            gates = c.stored + c.spilled
            gates += [c.loaded] * (len(loads) - len(gates))
            for (dst, src), g in zip(loads, gates):
                e.dma_start(dst, src).then_inc(g.sem, 16)
                g.passed(16)
            for g in c.stored + c.spilled + [c.loaded]:
                e.wait_ge(g.sem, g.at(0))

        @block.vector
        def _(e):
            for g in c.gates.values():
                if g.credit:
                    e.sem_inc(g.sem, g.credit)
            e.memset(c.ones[:, :], 1.0)
            e.memset(c.mean[:, :], 1.0 / D)
            e.memset(c.eps[:, :], EPS)

    with nc.Block() as block:
        @block.gpsimd
        def _(e):
            _small(c, e, c.small_pool, 1, lambda: e.iota(
                c.idx[:, :, :].rearrange("p a b -> p (a b)"), [[1, RING * GROUP]], base=0, channel_multiplier=0))
            _small(c, e, c.small_pool, 1, lambda: e.memset(c.ident[:, :], 0.0))
            _small(c, e, c.small_pool, 1, lambda: e.affine_select(
                out=c.ident[:, :], in_=c.ident[:, :], compare_op=ALU.not_equal, fill=1.0, base=0,
                pattern=[[-1, P]], channel_multiplier=1))
            _small(c, e, c.small_pool, 1, lambda: e.iota(c.iota[:, :], [[1, P]], base=0, channel_multiplier=0,
                                                          allow_small_or_imprecise_dtypes=True))


def _walk(c, ins, dram):
    nc = c.nc
    s = c.small
    start, edge_lo, edge_hi, full, steps, ends, shift, number = (
        c.B[:, 64 * i:64 * i + WINDOWS] for i in range(8))
    raw = c.B[:, 1024:1024 + EDGE_TILES].bitcast(I32)
    flat = c.B[:, 2048:2048 + EDGE_TILES]
    hit = c.B[:, 3072:3072 + EDGE_TILES]
    whole = c.B[:, 512:512 + 2 * 64].bitcast(I32)
    pair = c.B[:, 704:704 + KBLOCKS]
    node = c.B[:, 720:720 + KBLOCKS]
    edge = c.B[:, 736:736 + KBLOCKS]
    node_i = c.B[:, 752:752 + KBLOCKS].bitcast(I32)
    edge_i = c.B[:, 768:768 + KBLOCKS].bitcast(I32)
    far = c.B[:, 784:784 + KBLOCKS]
    grid = c.grid = c.C[:, 0:KBLOCKS * NODE_TILES].rearrange("p (k n) -> p k n", n=NODE_TILES)
    grid2 = c.C[:, 512:512 + KBLOCKS * NODE_TILES].rearrange("p (k n) -> p k n", n=NODE_TILES)
    bounds = c.B[:, 832:832 + WINDOWS]
    n = NODE_TILES
    with nc.psum_tensor("walk_ps", [P, WINDOWS], F32) as ps:
        with nc.Block() as block:
            @block.sync
            def _(e):
                e.dma_start(raw, ins["dst"].rearrange("t p -> (t p)").rearrange("(a b) -> a b", a=P)
                            ).then_inc(c.loaded.sem, 16)
                e.wait_ge(c.loaded.sem, c.loaded.at(16))

            @block.gpsimd
            def _(e):
                e.iota(bounds, [[P, WINDOWS]], base=0, channel_multiplier=0, allow_small_or_imprecise_dtypes=True)
                e.iota(number, [[1, WINDOWS]], base=0, channel_multiplier=0, allow_small_or_imprecise_dtypes=True)
                e.iota(pair, [[P, KBLOCKS]], base=0, channel_multiplier=1, allow_small_or_imprecise_dtypes=True)
        c.loaded.passed(16)
        with nc.Block() as block:
            @block.vector
            def _(e):
                _small(c, e, c.small_dve, 1, lambda: e.tensor_copy(flat, raw))
                with e.Fori(0, WINDOWS) as i:
                    _hold(e, c.added, i, c.tick_dve)
                    e.tensor_scalar(hit, flat, bounds[:, bass.ds(i, 1)], 0.0, ALU.is_lt, ALU.add,
                                    accum_out=start[:, bass.ds(i, 1)]).then_inc(c.added.sem, 1)
        c.added.passed(WINDOWS)
        with nc.Block() as block:
            @block.tensor
            def _(e):
                e.matmul(ps[:, :], c.ones[:, :], start, start=True, stop=True).then_inc(c.small_pe.sem, 1)

            @block.vector
            def _(e):
                def step(make):
                    _small(c, e, c.small_dve, 1, make)
                e.wait_ge(c.small_pe.sem, c.small_pe.at(1))
                step(lambda: e.tensor_copy(start, ps[:, :]))
                step(lambda: e.tensor_copy(whole[:, 0:WINDOWS], start))
                step(lambda: e.tensor_scalar(whole[:, 0:WINDOWS], whole[:, 0:WINDOWS], 7, None,
                                             ALU.arith_shift_right))
                step(lambda: e.tensor_copy(edge_lo, whole[:, 0:WINDOWS]))
                step(lambda: e.tensor_scalar(edge_hi, start, -1.0, None, ALU.add))
                step(lambda: e.tensor_copy(whole[:, 64:64 + WINDOWS], edge_hi))
                step(lambda: e.tensor_scalar(whole[:, 64:64 + WINDOWS], whole[:, 64:64 + WINDOWS], 7, None,
                                             ALU.arith_shift_right))
                step(lambda: e.tensor_copy(edge_hi, whole[:, 64:64 + WINDOWS]))
                step(lambda: e.tensor_tensor(full[:, 0:n], start[:, 1:n + 1], start[:, 0:n], ALU.is_gt))
                step(lambda: e.tensor_tensor(steps[:, 0:n], edge_hi[:, 1:n + 1], edge_lo[:, 0:n], ALU.subtract))
                step(lambda: e.scalar_tensor_tensor(steps[:, 0:n], steps[:, 0:n], 1.0, full[:, 0:n],
                                                    ALU.add, ALU.mult))
                step(lambda: e.tensor_tensor_scan(ends[:, 0:n], c.ones[:, 0:n], steps[:, 0:n], 0.0,
                                                  ALU.mult, ALU.add))
                step(lambda: e.tensor_tensor(shift[:, 0:n], steps[:, 0:n], ends[:, 0:n], ALU.subtract))
                step(lambda: e.tensor_tensor(shift[:, 0:n], shift[:, 0:n], edge_lo[:, 0:n], ALU.add))
                step(lambda: e.tensor_tensor(grid, ends[:, 0:n].unsqueeze(1).to_broadcast([P, KBLOCKS, n]),
                                             pair.unsqueeze(2).to_broadcast([P, KBLOCKS, n]), ALU.is_le))
                step(lambda: e.tensor_reduce(node, grid, AX.X, ALU.add))
                step(lambda: e.tensor_tensor(grid, number[:, 0:n].unsqueeze(1).to_broadcast([P, KBLOCKS, n]),
                                             node.unsqueeze(2).to_broadcast([P, KBLOCKS, n]), ALU.is_equal))
                step(lambda: e.tensor_tensor(grid2, grid,
                                             shift[:, 0:n].unsqueeze(1).to_broadcast([P, KBLOCKS, n]), ALU.mult))
                step(lambda: e.tensor_reduce(edge, grid2, AX.X, ALU.add))
                step(lambda: e.tensor_tensor(edge, edge, pair, ALU.add))
                step(lambda: e.tensor_scalar(edge, edge, float(EDGE_TILES - 1), 0.0, ALU.min, ALU.max))
                step(lambda: e.tensor_copy(edge_i, edge))
                step(lambda: e.tensor_copy(node_i, node))
                step(lambda: e.tensor_scalar(far, node, float(P), None, ALU.mult))
    c.small_pe.passed(1)
    rows_d = c.C[:, 1024:1024 + KBLOCKS * P].rearrange("p (k x) -> p k x", x=P)
    rows_s = c.C[:, 2048:2048 + KBLOCKS * P].rearrange("p (k x) -> p k x", x=P)
    rows_w = c.C[:, 3072:3072 + KBLOCKS * P].rearrange("p (k x) -> p k x", x=P)
    with nc.Block() as block:
        @block.sync
        def _(e):
            with nc.allow_non_contiguous_dma(reason="two rows of small integers"):
                e.dma_start(dram.t.rearrange("(k p) -> p k", p=P), edge_i).then_inc(c.moved.sem, 16)
                e.dma_start(dram.n.rearrange("(k p) -> p k", p=P), node_i).then_inc(c.moved.sem, 16)
            e.wait_ge(c.moved.sem, c.moved.at(32))
            e.dma_start(c.tRow[:, :], dram.t.rearrange("(a x) -> a x", a=1)).then_inc(c.moved.sem, 16)
            e.dma_start(c.nRow[:, :], dram.n.rearrange("(a x) -> a x", a=1)).then_inc(c.moved.sem, 16)
            e.wait_ge(c.moved.sem, c.moved.at(64))

        @block.gpsimd
        def _(e):
            for k in range(KBLOCKS):
                e.tensor_copy(c.idx[:, 0, 0:1], edge_i[:, k:k + 1]).then_inc(c.small_pool.sem, 1)
                c.small_pool.passed(1)
                e.wait_ge(c.small_pool.sem, c.small_pool.at(0))
                for t, (rows, src) in enumerate(((rows_d, "dst"), (rows_s, "src"), (rows_w, "w"))):
                    out = rows[:, k, :] if src == "w" else rows[:, k, :].bitcast(I32)
                    e.indirect_dma_start(out, None, ins[src],
                                         bass.IndirectOffsetOnAxis(ap=c.idx[:, 0, 0:1], axis=0)
                                         ).then_inc(c.gathered[t].sem, 16)
                for t in range(3):
                    c.gathered[t].passed(16)
                    e.wait_ge(c.gathered[t].sem, c.gathered[t].at(0))
    c.moved.passed(64)
    size = P * KBLOCKS
    with nc.psum_tensor("rel_ps", [P, 1024], F32) as rel_ps, nc.psum_tensor("src_ps", [P, 1024], F32) as src_ps, \
            nc.psum_tensor("w_ps", [P, 1024], F32) as w_ps:
        wide_d = c.C[:, 1024:1024 + size]
        wide_s = c.C[:, 2048:2048 + size]
        with nc.Block() as block:
            @block.vector
            def _(e):
                def step(make):
                    _small(c, e, c.small_dve, 1, make)
                step(lambda: e.tensor_copy(c.B[:, 1024:1024 + size], wide_d.bitcast(I32)))
                step(lambda: e.tensor_copy(c.B[:, 2048:2048 + size], wide_s.bitcast(I32)))
                step(lambda: e.tensor_tensor(
                    c.B[:, 3072:3072 + size].rearrange("p (k x) -> p k x", x=P),
                    c.B[:, 1024:1024 + size].rearrange("p (k x) -> p k x", x=P),
                    far.unsqueeze(2).to_broadcast([P, KBLOCKS, P]), ALU.subtract))
        with nc.Block() as block:
            @block.sync
            def _(e):
                e.dma_start(dram.seq[1:1 + KCOLS * P].rearrange("(k p x) -> p k x", p=P, x=P),
                            c.B[:, 1024:1024 + size].rearrange("p (k x) -> p k x", x=P)).then_inc(c.moved.sem, 16)
                e.wait_ge(c.moved.sem, c.moved.at(16))

            @block.tensor
            def _(e):
                for k in range(KBLOCKS):
                    for ps, at in ((rel_ps, c.B[:, 3072:]), (src_ps, c.B[:, 2048:])):
                        e.transpose(ps[:, k * P:k * P + P], at[:, k * P:k * P + P], c.ident[:, :])
                    last = e.transpose(w_ps[:, k * P:k * P + P], rows_w[:, k, :], c.ident[:, :])
                last.then_inc(c.small_pe.sem, 1)

            @block.vector
            def _(e):
                e.wait_ge(c.small_pe.sem, c.small_pe.at(1))
                e.tensor_copy(c.relK[:, :], rel_ps[:, 0:KCOLS])
                e.tensor_copy(c.srcK[:, :], src_ps[:, 0:KCOLS])
                e.tensor_copy(c.wK[:, :], w_ps[:, 0:KCOLS])
                e.memset(s[0:1, 0:1], -1.0)
                e.memset(s[0:1, 1:2], -2.0)
        c.small_pe.passed(1)
        c.moved.passed(16)
    with nc.Block() as block:
        @block.sync
        def _(e):
            e.dma_start(dram.seq[0:1].rearrange("(a b) -> a b", a=1), s[0:1, 0:1]).then_inc(c.moved.sem, 16)
            end = 1 + PAIRS * P
            e.dma_start(dram.seq[end:end + 1].rearrange("(a b) -> a b", a=1), s[0:1, 1:2]
                        ).then_inc(c.moved.sem, 16)
            e.wait_ge(c.moved.sem, c.moved.at(32))
    c.moved.passed(32)


def _degree(c, root, share, dram):
    nc = c.nc
    count = c.F[:, 0:KCOLS]
    by_pair = c.F[:, KCOLS:2 * KCOLS]
    total, shared = (c.F[0:WINDOWS, 2 * KCOLS + i * P:2 * KCOLS + i * P + P] for i in range(2))
    half = c.gbuf[:, :, :, :].rearrange("p a b x -> p (a b x)").bitcast(BF16)
    near, iota, one = half[:, 0:KCOLS], half[:, KCOLS:KCOLS + P], half[:, KCOLS + P:KCOLS + P + 1]
    sel = c.sel[:, :, :, :].rearrange("p a b x -> p (a b x)").bitcast(BF16)[:, 0:RING * GROUP * P].rearrange(
        "p (a b x) -> p a b x", a=RING, b=GROUP)
    with nc.psum_tensor(c.name("count"), [P, RING, 512], F32) as ps:
        with nc.Block() as block:
            @block.tensor
            def _(e):
                with e.Fori(0, ROUNDS) as i:
                    for g in range(RING):
                        q = i * RING + g
                        _hold(e, c.select, q + 1, c.tick_pe)
                        _hold(e, c.counted, q - RING + 1, c.tick_pe)
                        for r in range(GROUP):
                            last = e.matmul(ps[:, g, r:r + 1], sel[:, g, r, :], one,
                                            start=True, stop=True)
                        last.then_inc(c.product.sem, 1)

            @block.vector
            def _(e):
                e.memset(count[:, PAIRS:KCOLS], 0.0)
                e.memset(total, 0.0)
                _small(c, e, c.small_dve, 1, lambda: e.tensor_copy(near, c.relK[:, :]))
                _small(c, e, c.small_dve, 1, lambda: e.tensor_copy(iota, c.iota[:, :]))
                _small(c, e, c.small_dve, 1, lambda: e.tensor_copy(one, c.ones[:, 0:1]))
                with e.Fori(0, ROUNDS) as i:
                    for g in range(RING):
                        _select(c, e, i * RING + g, g, sel, near, iota)

            @block.scalar
            def _(e):
                with e.Fori(0, ROUNDS) as i:
                    for g in range(RING):
                        q = i * RING + g
                        _hold(e, c.product, q + 1, c.tick_act)
                        e.activation(count[:, bass.ds(q * GROUP, GROUP)], ps[:, g, 0:GROUP], ACT.Copy
                                     ).then_inc(c.counted.sem, 1)
        for gate in (c.product, c.select, c.counted):
            gate.passed(GROUPS)
    with nc.psum_tensor(c.name("by_pair"), [P, 1024], F32) as ps, \
            nc.psum_tensor(c.name("total"), [P, P], F32) as sum_ps:
        with nc.Block() as block:
            @block.tensor
            def _(e):
                for k in range(KBLOCKS):
                    last = e.transpose(ps[:, k * P:k * P + P], count[:, k * P:k * P + P], c.ident[:, :])
                last.then_inc(c.turned.sem, 1)
                e.wait_ge(c.chunked.sem, c.chunked.at(1))
                for k in range(KBLOCKS):
                    last = e.matmul(sum_ps[0:NODE_TILES, :], c.grid[:, k, :], by_pair[:, k * P:k * P + P],
                                    start=k == 0, stop=k == KBLOCKS - 1)
                last.then_inc(c.product.sem, 1)

            @block.scalar
            def _(e):
                e.wait_ge(c.turned.sem, c.turned.at(1))
                e.copy(by_pair, ps[:, 0:KCOLS]).then_inc(c.chunked.sem, 1)
                e.wait_ge(c.product.sem, c.product.at(1))
                e.copy(total[0:NODE_TILES, :], sum_ps[0:NODE_TILES, :]).then_inc(c.counted.sem, 1)
    for gate in (c.turned, c.chunked, c.product, c.counted):
        gate.passed(1)
    _whole(c,
           ("v", lambda e: e.tensor_scalar(shared, total, 1.0, None, ALU.max)),
           ("s", lambda e: e.activation(total, total, ACT.Sqrt, bias=c.ones[0:WINDOWS, 0:1])),
           ("v", lambda e: e.reciprocal(total, total)),
           ("v", lambda e: e.reciprocal(shared, shared)))
    with nc.Block() as block:
        @block.sync
        def _(e):
            for row, src in ((dram.root, total), (dram.share, shared)):
                e.dma_start(row.rearrange("(w p) -> w p", p=P), src).then_inc(c.moved.sem, 16)
            e.wait_ge(c.moved.sem, c.moved.at(32))
            for row, to in ((dram.root, root), (dram.share, share)):
                e.dma_start(to, row.rearrange("(a x) -> a x", a=1).to_broadcast([P, COLS])).then_inc(c.moved.sem, 16)
            e.wait_ge(c.moved.sem, c.moved.at(64))
    c.moved.passed(64)


def _select(c, e, q, g, sel=None, near=None, iota=None):
    e.wait_ge(c.product.sem, c.product.at(q - RING + 1))
    sel = c.sel if sel is None else sel
    near = c.relK if near is None else near
    iota = c.iota if iota is None else iota
    e.tensor_tensor(sel[:, g, :, :],
                    near[:, bass.ds(q * GROUP, GROUP)].unsqueeze(2).to_broadcast([P, GROUP, P]),
                    iota[:, :].unsqueeze(1).to_broadcast([P, GROUP, P]), ALU.is_equal
                    ).then_inc(c.select.sem, 1)


def _words(nc, eng, row, q, top, why):
    return nc.values_load_multi_w_load_instructions(
        row[0:1, bass.ds(q * GROUP, GROUP)], engines=[eng.engine], min_val=0, max_val=top,
        skip_runtime_bounds_check_because=why)[1]


def _nodes(nc, c, eng, q):
    return _words(nc, eng, c.nRow, q, WINDOWS - 1, "it counts node tiles")


def _pass(c, kind, table, agg, width=D, attr=None, query=None, score=None, spill=None):
    nc = c.nc
    cell = D + 2 * HEADS if kind == "attend" else P
    win = None if agg is None else agg.rearrange("p (w x) -> p w x", w=WINDOWS)
    banks = 2 if kind == "look" else RING
    gbuf, msg = c.gbuf, None
    if kind == "look":
        size = RING * GROUP * 2 * D
        gbuf = c.DE[:, 0:size].rearrange("p (a b x) -> p a b x", a=RING, b=GROUP)
        prod, turn = (c.DE[:, size + i * 2 * GROUP * P:size + (i + 1) * 2 * GROUP * P].rearrange(
            "p (a b x) -> p a b x", a=2, b=GROUP) for i in range(2))
        size += 4 * GROUP * P
        bare, edge = (c.DE[:, size + i * 2 * GROUP * HEADS:size + (i + 1) * 2 * GROUP * HEADS].rearrange(
            "p (a x) -> p a x", a=2) for i in range(2))
    if kind == "attend":
        msg = c.DE[:, WINDOWS * cell:WINDOWS * cell + RING * GROUP * cell].rearrange(
            "p (a b x) -> p a b x", a=RING, b=GROUP)
    with ExitStack() as ctx:
        part = ctx.enter_context(nc.psum_tensor(
            c.name("part"), [P, banks, GROUP, 2 * P if kind in ("look", "attend") else P], F32))
        if kind == "look":
            turned = ctx.enter_context(nc.psum_tensor(c.name("turned"), [P, 2, GROUP, P], F32))
        block = ctx.enter_context(nc.Block())

        if kind == "edge":
            @block.sync
            def _(e):
                with e.Fori(0, ROUNDS) as i:
                    for g in range(RING):
                        q = i * RING + g
                        tile = _words(nc, e, c.tRow, q, EDGE_TILES - 1, "clamped when it was made")
                        _hold(e, c.joined, q - RING + 1, c.tick_sp)
                        for r in range(GROUP):
                            e.dma_start(c.ebuf[:, g, r, :],
                                        attr[bass.ds(tile[r], 1), :, :].rearrange("a p f -> (a p) f")
                                        ).then_inc(c.attrs[g].sem, 16)

        if kind == "look":
            @block.sync
            def _(e):
                with e.Fori(0, ROUNDS) as i:
                    for g in range(RING):
                        _hold(e, c.gathered[g], 16 * GROUP * (i + 1), c.tick_sp)
                        e.dma_start(spill[bass.ds(i * RING + g, 1), :, :, :].rearrange("a p r f -> (a p) r f"),
                                    gbuf[:, g, :, D:2 * D]).then_inc(c.spilled[g].sem, 16)
                for g in range(RING):
                    e.wait_ge(c.spilled[g].sem, c.spilled[g].at(16 * ROUNDS))

        if kind == "attend":
            @block.sync
            def _(e):
                with e.Fori(0, ROUNDS) as i:
                    for g in range(RING):
                        q = i * RING + g
                        _hold(e, c.scored, q - RING + 1, c.tick_sp)
                        e.dma_start(gbuf[:, g, :, :], spill[bass.ds(q, 1), :, :, :].rearrange(
                            "a p r f -> (a p) r f")).then_inc(c.attrs[g].sem, 16)

            @block.scalar
            def _(e):
                with e.Fori(0, ROUNDS) as i:
                    for g in range(RING):
                        q = i * RING + g
                        _hold(e, c.product, q - RING + 1, c.tick_act)
                        e.copy(msg[:, g, :, D:D + HEADS],
                               score[:, bass.ds(q * GROUP * HEADS, GROUP * HEADS)].rearrange(
                                   "p (r h) -> p r h", h=HEADS)).then_inc(c.expanded.sem, 1)
        else:
            @block.gpsimd
            def _(e):
                with e.Fori(0, ROUNDS) as i:
                    for g in range(RING):
                        _hold(e, c.index, i * RING + g + 1, c.tick_pool)
                        for r in range(GROUP):
                            e.indirect_dma_start(gbuf[:, g, r, 0:table.shape[1]], None, table,
                                                 bass.IndirectOffsetOnAxis(ap=c.idx[:, g, r:r + 1], axis=0)
                                                 ).then_inc(c.gathered[g].sem, 16)

            @block.scalar
            def _(e):
                def index(q, g, rounds):
                    _hold(e, c.joined if kind == "look" else c.product, q - RING + 1, c.tick_act)
                    if kind == "look":
                        _hold(e, c.spilled[g], 16 * rounds, c.tick_act)
                    e.copy(c.idx[:, g, :], c.srcK[:, bass.ds(q * GROUP, GROUP)]).then_inc(c.index.sem, 1)

                index(0, 0, 0)
                index(1, 1, 0)
                with e.Fori(0, ROUNDS) as i:
                    for g in range(RING):
                        q = i * RING + g
                        index(q + 2, (g + 2) % RING, i + (g + 2) // RING)
                        if kind == "edge":
                            e.wait_ge(c.joined.sem, c.joined.at(q + 1))
                            e.activation(gbuf[:, g, :, :], gbuf[:, g, :, :], ACT.Relu).then_inc(c.message.sem, 1)
                        elif kind == "look":
                            _hold(e, c.product, q - 1, c.tick_act)
                            e.wait_ge(c.turned.sem, c.turned.at(q + 1))
                            e.activation(turn[:, g % 2, :, :], turned[:, g % 2, :, :], ACT.Copy
                                         ).then_inc(c.message.sem, 1)

        @block.tensor
        def _(e):
            with e.Fori(0, ROUNDS) as i:
                for g in range(RING):
                    q = i * RING + g
                    b = g % banks
                    _hold(e, c.select, q + 1, c.tick_pe)
                    if kind == "look":
                        _hold(e, c.message, q - 1, c.tick_pe)
                        for r in range(GROUP):
                            last = e.transpose(turned[:, b, r, :], c.sel[:, g, r, :], c.ident[:, :])
                        last.then_inc(c.turned.sem, 1)
                        where = _nodes(nc, c, e, q)
                        _hold(e, c.message, q + 1, c.tick_pe)
                        _hold(e, c.scored, q - 1, c.tick_pe)
                        for r in range(GROUP):
                            last = e.matmul(part[:, b, r, 0:D + HEADS], turn[:, b, r, :],
                                            query[:, bass.ds(where[r] * (D + HEADS), D + HEADS)],
                                            start=True, stop=True)
                        last.then_inc(c.product.sem, 1)
                        continue
                    _hold(e, c.added, (q - banks + 1) * GROUP, c.tick_pe)
                    if kind == "sum":
                        _hold(e, c.gathered[g], 16 * GROUP * (i + 1), c.tick_pe)
                    elif kind == "edge":
                        _hold(e, c.message, q + 1, c.tick_pe)
                    elif kind == "attend":
                        _hold(e, c.expanded, q + 1, c.tick_pe)
                        _hold(e, c.keyed, q + 1, c.tick_pe)
                        _hold(e, c.scored, q + 1, c.tick_pe)
                    for r in range(GROUP):
                        if kind == "attend":
                            last = e.matmul(part[:, b, r, 0:cell], c.sel[:, g, r, :], msg[:, g, r, :],
                                            start=True, stop=True)
                        else:
                            last = e.matmul(part[0:width, b, r, :], gbuf[:, g, r, 0:width], c.sel[:, g, r, :],
                                            start=True, stop=True)
                    last.then_inc(c.product.sem, 1)

        @block.vector
        def _(e):
            def heads(x, g):
                return x[:, g, :, 0:D].rearrange("p r (h x) -> p r h x", h=HEADS)

            def prepare(q, g, i):
                scores = None if score is None else score[:, bass.ds(q * GROUP * HEADS, GROUP * HEADS)]
                if kind == "edge":
                    _hold(e, c.gathered[g], 16 * GROUP * (i + 1), c.tick_dve)
                    _hold(e, c.attrs[g], 16 * GROUP * (i + 1), c.tick_dve)
                    e.tensor_tensor(gbuf[:, g, :, :], gbuf[:, g, :, :], c.ebuf[:, g, :, :], ALU.add
                                    ).then_inc(c.joined.sem, 1)
                elif kind == "look":
                    b = g % 2
                    weight = c.wK[:, bass.ds(q * GROUP, GROUP)].unsqueeze(2).to_broadcast([P, GROUP, HEADS])
                    _hold(e, c.product, q + 1, c.tick_dve)
                    e.tensor_tensor(edge[:, b, :].rearrange("p (r h) -> p r h", h=HEADS),
                                    part[:, b, :, D:D + HEADS], weight, ALU.mult).then_inc(c.told.sem, 1)
                    _hold(e, c.gathered[g], 16 * GROUP * (i + 1), c.tick_dve)
                    e.tensor_tensor(prod[:, b, :, :], gbuf[:, g, :, 0:D], part[:, b, :, 0:D], ALU.mult
                                    ).then_inc(c.scored.sem, 1)
                    _hold(e, c.scored, q + 1, c.tick_dve)
                    e.tensor_reduce(bare[:, b, :], prod[:, b, :, :].rearrange("p r (h x) -> p (r h) x", h=HEADS),
                                    AX.X, ALU.add).then_inc(c.keyed.sem, 1)
                    _hold(e, c.told, q + 1, c.tick_dve)
                    _hold(e, c.keyed, q + 1, c.tick_dve)
                    e.tensor_tensor(scores, bare[:, b, :], edge[:, b, :], ALU.add).then_inc(c.joined.sem, 1)
                elif kind == "attend":
                    weight = c.wK[:, bass.ds(q * GROUP, GROUP)].unsqueeze(2).to_broadcast([P, GROUP, HEADS])
                    prob = scores.rearrange("p (r h) -> p r h", h=HEADS)
                    _hold(e, c.product, q - RING + 1, c.tick_dve)
                    e.tensor_tensor(msg[:, g, :, D + HEADS:cell], prob, weight, ALU.mult
                                    ).then_inc(c.keyed.sem, 1)
                    _hold(e, c.attrs[g], 16 * (i + 1), c.tick_dve)
                    e.tensor_tensor(heads(msg, g), heads(gbuf, g),
                                    prob.unsqueeze(3).to_broadcast([P, GROUP, HEADS, HEAD]), ALU.mult
                                    ).then_inc(c.scored.sem, 1)

            def add(q, g, where, r):
                into = win[0:width, bass.ds(where[r], 1), :].rearrange("p a x -> p (a x)")
                e.wait_ge(c.added.sem, c.added.at(q * GROUP + r))
                e.tensor_tensor(into, into, part[0:width, g % banks, r, 0:cell], ALU.add
                                ).then_inc(c.added.sem, 1)

            if agg is None:
                _select(c, e, 0, 0)
                with e.Fori(0, ROUNDS) as i:
                    for g in range(RING):
                        q = i * RING + g
                        _select(c, e, q + 1, (g + 1) % RING)
                        prepare(q, g, i)
                return
            e.memset(agg, 0.0).then_inc(c.cleared.sem, 1)
            e.wait_ge(c.cleared.sem, c.cleared.at(1))
            for g in range(3):
                _select(c, e, g, g)
            for g in range(2):
                prepare(g, g, 0)

            def steps(i, last):
                for g in range(RING):
                    q = i * RING + g
                    left = RING - 1 - g if last else RING
                    where = _nodes(nc, c, e, q)
                    _hold(e, c.product, q + 1, c.tick_dve)
                    add(q, g, where, 0)
                    if left > 2:
                        _select(c, e, q + 3, (g + 3) % RING)
                    add(q, g, where, 1)
                    if left > 1:
                        prepare(q + 2, (g + 2) % RING, i + (g + 2) // RING)
                    add(q, g, where, 2)
                    add(q, g, where, 3)
            with e.Fori(0, ROUNDS - 1) as i:
                steps(i, False)
            steps(ROUNDS - 1, True)

    c.product.passed(GROUPS)
    c.select.passed(GROUPS + (agg is None))
    if agg is not None:
        c.added.passed(PAIRS)
        c.cleared.passed(1)
    if kind != "attend":
        c.index.passed(GROUPS + 2)
        for g in c.gathered:
            g.passed(16 * GROUP * ROUNDS)
    if kind == "edge":
        for g in c.attrs:
            g.passed(16 * GROUP * ROUNDS)
    if kind == "look":
        c.turned.passed(GROUPS)
        c.told.passed(GROUPS)
        for g in c.spilled:
            g.passed(16 * ROUNDS)
    if kind == "attend":
        c.expanded.passed(GROUPS)
        for g in c.attrs:
            g.passed(16 * ROUNDS)
    if kind in ("edge", "look"):
        c.joined.passed(GROUPS)
        c.message.passed(GROUPS)
    if kind in ("look", "attend"):
        c.scored.passed(GROUPS)
        c.keyed.passed(GROUPS)


def _chunk(i, size=CHUNK):
    return bass.ds(i * size, size)


def _load(c, *pairs):
    with c.nc.Block() as block:
        @block.sync
        def _(e):
            for dst, src in pairs:
                e.dma_start(dst, src).then_inc(c.loaded.sem, 16)
            c.loaded.passed(16 * len(pairs))
            e.wait_ge(c.loaded.sem, c.loaded.at(0))


def _dense(c, parts, by="act", prepare=None, feed=None, batch=None):
    nc = c.nc
    rounds = CHUNKS // 2
    k = len(parts)
    tail = []
    if batch:
        gain, offset, scale, shift = batch
        means = c.small[:, 2:2 + 2 * k].rearrange("p (k t) -> p k t", t=2)
        root = c.small[:, 8:8 + k]
        for o in range(k):
            tail.append(("v", lambda e, o=o: e.bn_aggr(means[:, o, :], c.stats[:, o, :])))
        tail += [
            ("s", lambda e: e.activation(root, means[:, :, 1], ACT.Sqrt, bias=c.eps[:, :])),
            ("v", lambda e: e.reciprocal(root, root)),
            ("v", lambda e: e.tensor_tensor(scale, root, gain, ALU.mult)),
            ("v", lambda e: e.tensor_tensor(root, means[:, :, 0], scale, ALU.mult)),
            ("v", lambda e: e.tensor_tensor(shift, offset, root, ALU.subtract)),
        ]
    with nc.psum_tensor(c.name("dense"), [P, 2, k, 512], F32) as ps, nc.Block() as block:
        def take(e, who, n, b, tick):
            _hold(e, c.product, n + 1, tick)
            for o, (_, out, bias, func, rows) in enumerate(parts):
                to, got = out[0:rows, _chunk(n)], ps[0:rows, b, o, 0:CHUNK]
                if who == "dve":
                    e.tensor_scalar(to, got, bias, None, ALU.add).then_inc(c.chunked.sem, 1)
                elif bias is None:
                    e.activation(to, got, func).then_inc(c.chunked.sem, 1)
                else:
                    e.activation(to, got, func, bias=bias).then_inc(c.chunked.sem, 1)

        @block.scalar
        def _(e):
            def ready(n):
                for x, by_, plus in prepare or ():
                    e.activation(x[:, _chunk(n)], x[:, _chunk(n)], ACT.Relu, bias=plus, scale=by_
                                 ).then_inc(c.applied.sem, 1)

            def steps(n, b, last):
                if not last:
                    ready(n + 1)
                if by == "act":
                    take(e, "act", n, b, c.tick_act)
            ready(0)
            with e.Fori(0, rounds - 1) as i:
                steps(i * 2, 0, False)
                steps(i * 2 + 1, 1, False)
            steps(CHUNKS - 2, 0, False)
            steps(CHUNKS - 1, 1, True)
            _chain(c, e, "s", tail)

        @block.tensor
        def _(e):
            with e.Fori(0, rounds) as i:
                for b in range(2):
                    n = i * 2 + b
                    _hold(e, c.chunked, (n - 1) * k, c.tick_pe)
                    if feed:
                        _hold(e, c.fed, n + 1, c.tick_pe)
                    if prepare:
                        _hold(e, c.applied, (n + 1) * len(prepare), c.tick_pe)
                    for o, (terms, _, _, _, rows) in enumerate(parts):
                        for j, (w, x) in enumerate(terms):
                            last = e.matmul(ps[0:rows, b, o, 0:CHUNK], w, x[0:w.shape[0], _chunk(n)],
                                            start=j == 0, stop=j == len(terms) - 1)
                    last.then_inc(c.product.sem, 1)

        if feed or batch or by == "dve":
            @block.vector
            def _(e):
                def add(n):
                    if feed:
                        x, a, b_ = (t[:, _chunk(n)] for t in feed)
                        e.tensor_tensor(x, a, b_, ALU.add).then_inc(c.fed.sem, 1)

                def steps(n, b, last):
                    if not last:
                        add(n + 1)
                    if by == "dve":
                        take(e, "dve", n, b, c.tick_dve)
                    if batch:
                        _hold(e, c.chunked, (n + 1) * k, c.tick_dve)
                        for o, (_, out, _, _, _) in enumerate(parts):
                            real = out[:, n * CHUNK:N] if isinstance(n, int) and n == FULL else out[:, _chunk(n)]
                            e.bn_stats(c.stats[:, o, bass.ds(n * 6, 6)], real).then_inc(c.varied.sem, 1)
                add(0)
                with e.Fori(0, rounds - 1) as i:
                    steps(i * 2, 0, False)
                    steps(i * 2 + 1, 1, False)
                steps(CHUNKS - 2, 0, False)
                steps(CHUNKS - 1, 1, True)
                if batch:
                    e.wait_ge(c.varied.sem, c.varied.at(CHUNKS * k))
                _chain(c, e, "v", tail)
    c.product.passed(CHUNKS)
    c.chunked.passed(CHUNKS * k)
    c.whole.passed(len(tail))
    if feed:
        c.fed.passed(CHUNKS)
    if batch:
        c.varied.passed(CHUNKS * k)
    if prepare:
        c.applied.passed(CHUNKS * len(prepare))


def _chain(c, eng, mine, steps):
    for n, (who, make) in enumerate(steps):
        if who == mine:
            make(eng).then_inc(c.whole.sem, 1)
        eng.wait_ge(c.whole.sem, c.whole.at(n + 1))


def _whole(c, *steps):
    with c.nc.Block() as block:
        @block.vector
        def _(e):
            _chain(c, e, "v", steps)

        @block.scalar
        def _(e):
            _chain(c, e, "s", steps)
    c.whole.passed(len(steps))


def _table(c, x, out, width=D, other=None, op=None, apply=None, scale=1.0, stride=P):
    nc = c.nc
    to_dram = out.shape[0] != P
    size = TURN * P
    steps = WINDOWS // TURN
    stage = c.sel[:, :, :, :].rearrange("p a b x -> p (a b x)")
    rows = c.ebuf[:, :, :, :].rearrange("p a b x -> p (a b x)")
    with nc.psum_tensor(c.name("turn"), [P, 2, 1024], F32) as ps, nc.Block() as block:
        @block.vector
        def _(e):
            with e.Fori(0, steps // 2) as i:
                for b in range(2):
                    n = i * 2 + b
                    to = stage[0:width, b * size:b * size + size]
                    _hold(e, c.turned, n - 1, c.tick_dve)
                    if other is None:
                        e.tensor_copy(to, x[0:width, _chunk(n, size)]).then_inc(c.staged.sem, 1)
                        continue
                    _hold(e, c.kept, n - 1, c.tick_dve)
                    if apply:
                        _hold(e, c.applied, n + 1, c.tick_dve)
                    e.tensor_tensor(to, x[0:width, _chunk(n, size)], other[0:width, _chunk(n, size)], op
                                    ).then_inc(c.staged.sem, 1)

        if other is not None:
            @block.gpsimd
            def _(e):
                with e.Fori(0, steps // 2) as i:
                    for b in range(2):
                        n = i * 2 + b
                        _hold(e, c.staged, n + 1, c.tick_pool)
                        e.tensor_copy(x[0:width, _chunk(n, size)], stage[0:width, b * size:b * size + size]
                                      ).then_inc(c.kept.sem, 1)

        @block.tensor
        def _(e):
            with e.Fori(0, steps // 2) as i:
                for b in range(2):
                    n = i * 2 + b
                    _hold(e, c.staged, n + 1, c.tick_pe)
                    _hold(e, c.chunked, n - 1, c.tick_pe)
                    for t in range(TURN):
                        at = b * size + t * P
                        last = e.transpose(ps[:, b, t * width:t * width + width], stage[0:width, at:at + P],
                                           c.ident[0:width, 0:width])
                    last.then_inc(c.turned.sem, 1)

        @block.scalar
        def _(e):
            def ready(n):
                if apply:
                    func, by, plus = apply
                    e.activation(other[:, _chunk(n, size)], other[:, _chunk(n, size)], func, bias=plus, scale=by
                                 ).then_inc(c.applied.sem, 1)

            def copy(i, b, last):
                n = i * 2 + b
                got = ps[:, b, 0:TURN * width]
                if not last:
                    ready(n + 1)
                _hold(e, c.turned, n + 1, c.tick_act)
                if to_dram:
                    _hold(e, c.stored[b], 16 * i, c.tick_act)
                    to = rows[:, b * size:b * size + TURN * width]
                else:
                    to = out[:, bass.ds(n * TURN * stride, TURN * stride)].rearrange(
                        "p (t x) -> p t x", t=TURN)[:, :, 0:P]
                    got = got.rearrange("p (t x) -> p t x", t=TURN)
                e.activation(to, got, ACT.Copy, scale=scale).then_inc(c.chunked.sem, 1)
            ready(0)
            with e.Fori(0, steps // 2 - 1) as i:
                for b in range(2):
                    copy(i, b, False)
            copy(steps // 2 - 1, 0, False)
            copy(steps // 2 - 1, 1, True)

        if to_dram:
            view = out.rearrange("(n t p) f -> n p t f", p=P, t=TURN)

            @block.sync
            def _(e):
                with e.Fori(0, steps // 2) as i:
                    for b in range(2):
                        n = i * 2 + b
                        _hold(e, c.chunked, n + 1, c.tick_sp)
                        e.dma_start(view[bass.ds(n, 1), :, :, :].rearrange("a p t f -> (a p) t f"),
                                    rows[:, b * size:b * size + TURN * width].rearrange("p (t f) -> p t f", t=TURN)
                                    ).then_inc(c.stored[b].sem, 16)
                for g in c.stored:
                    e.wait_ge(g.sem, g.at(16 * (steps // 2)))
    c.staged.passed(steps)
    c.turned.passed(steps)
    c.chunked.passed(steps)
    if other is not None:
        c.kept.passed(steps)
    if apply:
        c.applied.passed(steps)
    if to_dram:
        for g in c.stored:
            g.passed(16 * (steps // 2))


def _norm(c, x, plus):
    nc = c.nc
    sq = c.gbuf[:, 0:2, :, :].rearrange("p a b x -> p a (b x)")
    root = c.gbuf[:, 2:4, :, :].rearrange("p a b x -> p a (b x)")
    rounds = CHUNKS // 2

    def loop(e, steps):
        with e.Fori(0, rounds - 1) as i:
            for b in range(2):
                steps(i * 2 + b, b, 2)
        for b in range(2):
            steps(CHUNKS - 2 + b, b, 1 - b)
    with nc.psum_tensor(c.name("mean"), [P, 2, 512], F32) as mean_ps, \
            nc.psum_tensor(c.name("var"), [P, 2, 512], F32) as var_ps, nc.Block() as block:
        @block.tensor
        def _(e):
            def mean(n, b):
                _hold(e, c.fed, n + 1, c.tick_pe)
                _hold(e, c.centred, n - 1, c.tick_pe)
                e.matmul(mean_ps[:, b, 0:CHUNK], c.mean[:, :], x[:, _chunk(n)], start=True, stop=True
                         ).then_inc(c.meaned.sem, 1)

            def steps(n, b, left):
                if left > 0:
                    mean(n + 1, 1 - b)
                _hold(e, c.squared, n + 1, c.tick_pe)
                _hold(e, c.rooted, n - 1, c.tick_pe)
                e.matmul(var_ps[:, b, 0:CHUNK], c.mean[:, :], sq[:, b, 0:CHUNK], start=True, stop=True
                         ).then_inc(c.varied.sem, 1)
            mean(0, 0)
            loop(e, steps)

        @block.scalar
        def _(e):
            def square(n, b):
                _hold(e, c.varied, n - 1, c.tick_act)
                _hold(e, c.centred, n + 1, c.tick_act)
                e.activation(sq[:, b, 0:CHUNK], x[:, _chunk(n)], ACT.Square).then_inc(c.squared.sem, 1)

            def steps(n, b, left):
                if left > 0:
                    square(n + 1, 1 - b)
                _hold(e, c.applied, n - 1, c.tick_act)
                _hold(e, c.varied, n + 1, c.tick_act)
                e.activation(root[:, b, 0:CHUNK], var_ps[:, b, 0:CHUNK], ACT.Sqrt, bias=c.eps[:, :]
                             ).then_inc(c.rooted.sem, 1)
            square(0, 0)
            loop(e, steps)

        @block.vector
        def _(e):
            def add(n):
                e.tensor_tensor(x[:, _chunk(n)], x[:, _chunk(n)], plus[:, _chunk(n)], ALU.add
                                ).then_inc(c.fed.sem, 1)

            def centre(n, b):
                _hold(e, c.meaned, n + 1, c.tick_dve)
                e.tensor_tensor(x[:, _chunk(n)], x[:, _chunk(n)], mean_ps[:, b, 0:CHUNK], ALU.subtract
                                ).then_inc(c.centred.sem, 1)

            def steps(n, b, left):
                if left > 1:
                    add(n + 2)
                if left > 0:
                    centre(n + 1, 1 - b)
                _hold(e, c.rooted, n + 1, c.tick_dve)
                e.reciprocal(root[:, b, 0:CHUNK], root[:, b, 0:CHUNK]).then_inc(c.scored.sem, 1)
                _hold(e, c.scored, n + 1, c.tick_dve)
                e.tensor_tensor(x[:, _chunk(n)], x[:, _chunk(n)], root[:, b, 0:CHUNK], ALU.mult
                                ).then_inc(c.applied.sem, 1)
            add(0)
            add(1)
            centre(0, 0)
            loop(e, steps)
    for g in (c.fed, c.centred, c.meaned, c.squared, c.varied, c.rooted, c.scored, c.applied):
        g.passed(CHUNKS)


def _settle(c, agg, we, skip):
    nc = c.nc
    cell = D + 2 * HEADS
    cells = agg.rearrange("p (w x) -> p w x", x=cell)
    down, edge = cells[:, :, D:D + HEADS], cells[:, :, D + HEADS:cell]
    wide = c.DE[:, WINDOWS * cell:WINDOWS * cell + 2 * TURN * D].rearrange("p (a x) -> p a x", a=2)
    stage = c.sel[:, :, :, :].rearrange("p a b x -> p (a b x)")
    size = TURN * P
    steps = WINDOWS // TURN
    _whole(c, ("v", lambda e: e.tensor_scalar(down, down, 1e-30, None, ALU.max)),
           ("v", lambda e: e.reciprocal(down, down)),
           ("v", lambda e: e.tensor_tensor(edge, edge, down, ALU.mult)))
    with nc.psum_tensor(c.name("settle"), [P, 2, 1024], F32) as ps, nc.Block() as block:
        @block.vector
        def _(e):
            def mix(n, b):
                here = cells[:, bass.ds(n * TURN, TURN), :]
                to = stage[:, b * size:b * size + size].rearrange("p (t h x) -> p t h x", t=TURN, h=HEADS)
                part = wide[:, b, :].rearrange("p (t h x) -> p t h x", t=TURN, h=HEADS)

                def spread(x):
                    return x.unsqueeze(3).to_broadcast([P, TURN, HEADS, HEAD])
                _hold(e, c.turned, n - 1, c.tick_dve)
                e.tensor_tensor(to, here[:, :, 0:D].rearrange("p t (h x) -> p t h x", h=HEADS),
                                spread(here[:, :, D:D + HEADS]), ALU.mult).then_inc(c.keyed.sem, 1)
                e.tensor_tensor(part, we.rearrange("p (h x) -> p h x", h=HEADS).unsqueeze(1).to_broadcast(
                    [P, TURN, HEADS, HEAD]), spread(here[:, :, D + HEADS:cell]), ALU.mult).then_inc(c.keyed.sem, 1)
                _hold(e, c.keyed, 2 * (n + 1), c.tick_dve)
                e.tensor_tensor(to, to, part, ALU.add).then_inc(c.staged.sem, 1)

            def finish(n, b):
                _hold(e, c.turned, n + 1, c.tick_dve)
                e.tensor_tensor(skip[:, _chunk(n, size)], skip[:, _chunk(n, size)], ps[:, b, 0:size], ALU.add
                                ).then_inc(c.chunked.sem, 1)
            mix(0, 0)
            with e.Fori(0, steps // 2 - 1) as i:
                for b in range(2):
                    mix(i * 2 + b + 1, 1 - b)
                    finish(i * 2 + b, b)
            mix(steps - 1, 1)
            finish(steps - 2, 0)
            finish(steps - 1, 1)

        @block.tensor
        def _(e):
            with e.Fori(0, steps // 2) as i:
                for b in range(2):
                    n = i * 2 + b
                    _hold(e, c.staged, n + 1, c.tick_pe)
                    _hold(e, c.chunked, n - 1, c.tick_pe)
                    for t in range(TURN):
                        at = b * size + t * P
                        last = e.transpose(ps[:, b, t * P:t * P + P], stage[:, at:at + P], c.ident[:, :])
                    last.then_inc(c.turned.sem, 1)
    c.keyed.passed(2 * steps)
    for g in (c.staged, c.turned, c.chunked):
        g.passed(steps)


def _softmax(c, score, dram):
    nc = c.nc
    flags = c.DE[:, 0:SEQ + 2]
    new = c.DE[:, SEQ + 2:2 * SEQ + 3]
    run = c.DE[:, 2 * SEQ + 4:3 * SEQ + 4]
    alpha = c.soft
    rows = c.rows
    cols = c.small[:, 32:40]
    view = score.rearrange("p (c j h) -> p j h c", h=HEADS, j=SEQ_PAIRS)
    with nc.Block() as block:
        @block.sync
        def _(e):
            src = dram.seq[0:SEQ_ROWS * SEQ].rearrange("(c x) -> c x", x=SEQ)
            wide = bass.AP(src.tensor, src.offset, [[SEQ, SEQ_ROWS], [1, SEQ + 2]])
            for h in range(HEADS):
                e.dma_start(flags[h * SEQ_ROWS:(h + 1) * SEQ_ROWS, :], wide).then_inc(c.moved.sem, 16)
            e.wait_ge(c.moved.sem, c.moved.at(16 * HEADS))
    c.moved.passed(16 * HEADS)
    turns = [(a, min(a + 8, SEQ_PAIRS)) for a in range(0, SEQ_PAIRS, 8)]

    def turned(forward):
        with nc.psum_tensor(c.name("soft"), [P, 2, 8 * P], F32) as ps, nc.Block() as block:
            @block.tensor
            def _(e):
                for n, (a, z) in enumerate(turns):
                    e.wait_ge(c.chunked.sem, c.chunked.at(n - 1))
                    for j in range(a, z):
                        at = ps[:, n % 2, (j - a) * P:(j - a + 1) * P]
                        if forward:
                            last = e.transpose(at, run[:, j * P:(j + 1) * P], c.ident[:, :])
                        else:
                            last = e.transpose(at, alpha[:, j * P:(j + 1) * P], c.ident[:, :])
                    last.then_inc(c.turned.sem, 1)

            @block.scalar
            def _(e):
                for n, (a, z) in enumerate(turns):
                    e.wait_ge(c.turned.sem, c.turned.at(n + 1))
                    if forward:
                        e.copy(alpha[:, a * P:z * P], ps[:, n % 2, 0:(z - a) * P]).then_inc(c.chunked.sem, 1)
                        continue
                    for h in range(HEADS):
                        k = e.copy(view[:, a:z, h, :],
                                   ps[:, n % 2, 0:(z - a) * P].rearrange("p (j h c) -> p j h c", h=HEADS,
                                                                         c=SEQ_ROWS)[:, :, h, :])
                    k.then_inc(c.chunked.sem, 1)
        c.turned.passed(len(turns))
        c.chunked.passed(len(turns))

    _whole(c, *(("v", lambda e, h=h: e.tensor_copy(
        run.rearrange("p (j h c) -> p j h c", h=HEADS, c=SEQ_ROWS)[:, :, h, :], view[:, :, h, :]))
        for h in range(HEADS)))
    turned(True)
    _whole(c,
           ("v", lambda e: e.tensor_tensor(new, flags[:, 1:SEQ + 2], flags[:, 0:SEQ + 1], ALU.not_equal)),
           ("v", lambda e: e.tensor_scalar(new, new, FAR, None, ALU.mult)))

    for back in (False, True):
        data = run if back else alpha
        if back:
            fence, line = new[:, 1:SEQ + 1][:, ::-1], run[:, ::-1]
            end = run[:, 0:1]
        else:
            fence, line = new[:, 0:SEQ], alpha
            end = run[:, SEQ - 1:SEQ]
        out = run[:, ::-1] if back else run
        _whole(c,
               ("v", lambda e: e.tensor_tensor_scan(out, fence, line, FAR, ALU.add, ALU.max)),
               ("v", lambda e: e.tensor_copy(cols[:, 0:1], end)),
               ("v", lambda e: e.tensor_reduce(cols[:, 1:2], new[:, 1:SEQ + 1] if back else new[:, 0:SEQ],
                                               AX.X, ALU.min)))
        with nc.psum_tensor(c.name("carry"), [P, 2 * P + 8], F32) as ps:
            with nc.Block() as block:
                @block.tensor
                def _(e):
                    e.transpose(ps[0:1, 0:P], cols[:, 0:1], c.ident[:, :])
                    e.transpose(ps[0:1, P:2 * P], cols[:, 1:2], c.ident[:, :]).then_inc(c.small_pe.sem, 1)
            c.small_pe.passed(1)
            best, shut = rows[:, 0:P], rows[:, P:2 * P]
            carry = rows[:, 2 * P:3 * P + 2]
            if back:
                chain = ("v", lambda e: e.tensor_tensor_scan(carry[:, 0:P][:, ::-1], shut[:, ::-1], best[:, ::-1],
                                                             FAR, ALU.add, ALU.max))
                enter = carry[:, 1:P + 1]
            else:
                chain = ("v", lambda e: e.tensor_tensor_scan(carry[:, 1:P + 1], shut, best, FAR,
                                                             ALU.add, ALU.max))
                enter = carry[:, 0:P]
            _whole(c,
                   ("v", lambda e: e.tensor_copy(rows[:, 0:2 * P], ps[0:1, 0:2 * P])),
                   ("v", lambda e: e.memset(carry, FAR)),
                   chain)
            with nc.Block() as block:
                @block.tensor
                def _(e):
                    e.transpose(ps[:, 2 * P:2 * P + 1], enter, c.ident[0:1, 0:1]).then_inc(c.small_pe.sem, 1)
            c.small_pe.passed(1)
            _whole(c,
                   ("v", lambda e: e.tensor_copy(cols[:, 2:3], ps[:, 2 * P:2 * P + 1])),
                   ("v", lambda e: e.tensor_tensor_scan(out, fence, line, cols[:, 2:3], ALU.add, ALU.max)))
    _whole(c,
           ("v", lambda e: e.tensor_tensor(alpha, alpha, run, ALU.subtract)),
           ("s", lambda e: e.activation(alpha, alpha, ACT.Exp)))
    turned(False)


def build(nc, ins, out):
    with ExitStack() as ctx:
        c = _setup(ctx, nc)
        dram = Ctx()
        dram.t = nc.dram_tensor("walk_edge", [KCOLS], I32, kind="Internal").ap()
        dram.n = nc.dram_tensor("walk_node", [KCOLS], I32, kind="Internal").ap()
        dram.seq = nc.dram_tensor("walk_dst", [KCOLS * P + 2], F32, kind="Internal").ap()
        hid = nc.dram_tensor("rows_hidden", [COLS, HID], F32, kind="Internal").ap()
        keys = nc.dram_tensor("rows_key", [COLS, D], F32, kind="Internal").ap()
        both = nc.dram_tensor("rows_key_value", [COLS, 2 * D], F32, kind="Internal").ap()
        spill = nc.dram_tensor("walk_value", [GROUPS, P, GROUP, D], F32, kind="Internal").ap()
        dram.root = nc.dram_tensor("degree_root", [COLS], F32, kind="Internal").ap()
        dram.share = nc.dram_tensor("degree_share", [COLS], F32, kind="Internal").ap()
        A, B, C, D_, E_, F = c.A[:, :], c.B, c.C[:, :], c.D, c.E, c.F[:, :]
        column = {name: c.cols[:, i:i + w] for name, (i, w) in ins["at"].items()}

        def vv(out_, a, b, op):
            return ("v", lambda e: e.tensor_tensor(out_, a, b, op))

        _start(c, ins)
        _walk(c, ins, dram)

        _degree(c, F, C, dram)
        h = slice(0, HID)
        _dense(c, [([(c.W1g[:, :], A)], B, None, ACT.Copy, HID)])
        _table(c, B, hid, HID, other=F, op=ALU.mult)
        _pass(c, "sum", hid, D_, HID)
        _whole(c, vv(D_[h, :], D_[h, :], B[h, :], ALU.add),
               vv(D_[h, :], D_[h, :], F[h, :], ALU.mult),
               ("s", lambda e: e.activation(B[h, :], D_[h, :], ACT.Relu, bias=column["L0_gnn_b1"][h, :])))
        _table(c, B, hid, HID, other=F, op=ALU.mult)
        _pass(c, "sum", hid, D_, HID)
        _whole(c, vv(D_[h, :], D_[h, :], B[h, :], ALU.add),
               vv(D_[h, :], D_[h, :], F[h, :], ALU.mult))
        _dense(c, [([(c.W2g[:, :], D_)], B, column["L0_gnn_b2"], ACT.Identity, P)])
        _norm(c, A, B)

        _table(c, A, keys)
        _pass(c, "sum", keys, D_)
        _whole(c, vv(D_, D_, C, ALU.mult))
        _dense(c, [([(c.W1T[:, :], D_)], B, column["L1_gnn_b"], ACT.Relu, P)], feed=(D_, D_, A))
        _norm(c, A, B)

        _dense(c, [([(c.encW[:, :], A)], B, column["L2_gnn_enc_b"], ACT.Identity, P)])
        _table(c, B, keys)
        wide = (E_, F)
        for layer in range(LAYERS):
            def col(name, n, w=1):
                return column[name][:, n:n + w]
            scale, shift = c.small[:, 20:22], c.small[:, 22:24]
            scale2, shift2 = c.small[:, 24:25], c.small[:, 25:26]
            _load(c, (c.W1[:, :], ins["L2_gnn_W1"][layer, :, :]),
                  (c.W2[:, :, :], ins["L2_gnn_W2"][layer, :, :].rearrange("(h k) m -> k h m", h=2)))
            _pass(c, "edge", keys, D_, attr=ins["attr"])
            _dense(c, [([(c.W1[:, j * P:(j + 1) * P], D_)], wide[j], col("L2_gnn_b1", 2 * layer + j),
                        ACT.Identity, P) for j in range(2)], feed=(D_, D_, B),
                   batch=(col("L2_gnn_bn1_g", 2 * layer, 2), col("L2_gnn_bn1_b", 2 * layer, 2), scale, shift))
            _dense(c, [([(c.W2[:, j, :], wide[j]) for j in range(2)], D_, col("L2_gnn_b2", layer), None, P)],
                   by="dve", prepare=[(wide[j], scale[:, j:j + 1], shift[:, j:j + 1]) for j in range(2)],
                   batch=(col("L2_gnn_bn_g", layer), col("L2_gnn_bn_b", layer), scale2, shift2))
            if layer < LAYERS - 1:
                _table(c, B, keys, other=D_, op=ALU.add, apply=(ACT.Relu, scale2, shift2))
        _whole(c, ("s", lambda e: e.activation(D_, D_, ACT.Identity, bias=shift2, scale=scale2)),
               vv(B, B, D_, ALU.add))
        _norm(c, A, B)

        score = c.F[:, 0:PAIRS * HEADS]
        query = c.Bwide[:, :].rearrange("p (w x) -> p w x", w=WINDOWS)
        agg = c.DE[:, 0:WINDOWS * (D + 2 * HEADS)]
        x = A
        for conv in range(2):
            tag = str(conv + 1)
            we = c.We[:, conv, :]
            _load(c, *((c.W3[:, j, :], ins[f"L3_gnn_W{w}{tag}"]) for j, w in enumerate("qkvs")))
            _dense(c, [([(c.W3[:, j, :], x)], to, column["L3_gnn_b" + w + tag], ACT.Identity, P)
                       for j, w, to in ((1, "k", D_), (2, "v", E_), (0, "q", F), (3, "s", C))])
            _table(c, D_, both[:, 0:D])
            _table(c, E_, both[:, D:2 * D])
            _table(c, F, c.Bwide[:, :], scale=HEAD ** -0.5, stride=D + HEADS)
            spread = E_.rearrange("p (w h x) -> p w h x", h=HEADS, x=HEAD)
            _whole(c,
                   ("v", lambda e: e.tensor_tensor(
                       E_.rearrange("p (w x) -> p w x", w=WINDOWS), query[:, :, 0:D],
                       we.unsqueeze(1).to_broadcast([P, WINDOWS, D]), ALU.mult)),
                   ("v", lambda e: e.tensor_reduce(query[:, :, D:D + HEADS], spread, AX.X, ALU.add)))
            _pass(c, "look", both, None, query=c.Bwide, score=score, spill=spill)
            _softmax(c, score, dram)
            _pass(c, "attend", None, agg, score=score, spill=spill)
            _settle(c, agg, we, C)
            x = C
        _norm(c, A, C)
        with nc.Block() as block:
            @block.sync
            def _(e):
                e.dma_start(out, A).then_inc(c.moved.sem, 16)
                e.wait_ge(c.moved.sem, c.moved.at(16))


_COLUMNS = ["L0_gnn_b1", "L0_gnn_b2", "L1_gnn_b", "L2_gnn_enc_b", "L2_gnn_b1", "L2_gnn_bn1_g", "L2_gnn_bn1_b",
            "L2_gnn_b2", "L2_gnn_bn_g", "L2_gnn_bn_b", "L3_gnn_bq1", "L3_gnn_bk1", "L3_gnn_bv1", "L3_gnn_bs1",
            "L3_gnn_bq2", "L3_gnn_bk2", "L3_gnn_bv2", "L3_gnn_bs2"]


def kernel(**inputs):
    import numpy as np
    import concourse.bacc as bacc
    from concourse.bass_utils import run_bass_kernel_spmd

    nc = bacc.Bacc("TRN2", target_bir_lowering=False, num_devices=1)
    given = {k: np.asarray(v) for k, v in inputs.items()}
    x_cols = np.zeros((P, COLS), np.float32)
    x_cols[:, :N] = given["x"].T
    arrays = {"xT": x_cols}
    for name, key, fill in (("src", "src", 0), ("dst", "dst", PAD_NODE), ("edge_weight", "w", 0)):
        tiles = np.full((EDGE_TILES * P,), fill, given[name].dtype)
        tiles[:E] = given[name]
        arrays[key] = tiles.reshape(EDGE_TILES, P)
    attr = np.zeros((EDGE_TILES * P, D), np.float32)
    attr[:E] = given["edge_attr_128"]
    arrays["attr"] = attr.reshape(EDGE_TILES, P, D)
    arrays["L1_W_T"] = np.ascontiguousarray(given["L1_gnn_W"].T)
    for name in ("L0_gnn_W1", "L0_gnn_W2", "L2_gnn_enc_W", "L2_gnn_W1", "L2_gnn_W2"):
        arrays[name] = given[name]
    for i in (1, 2):
        for w in ("Wq", "Wk", "Wv", "Ws", "We"):
            arrays[f"L3_gnn_{w}{i}"] = given[f"L3_gnn_{w}{i}"]
    columns, at = [], {}
    for name in _COLUMNS:
        v = given[name].reshape(-1)
        width = -(-v.size // P)
        block = np.zeros((width * P,), np.float32)
        block[:v.size] = v
        at[name] = (sum(b.shape[1] for b in columns), width)
        columns.append(block.reshape(width, P).T)
    arrays["cols"] = np.concatenate(columns, axis=1)
    ins = {"at": at}
    for name, a in arrays.items():
        arrays[name] = np.ascontiguousarray(a)
        ins[name] = nc.dram_tensor(f"in_{name}", a.shape, mybir.dt.from_np(a.dtype), kind="ExternalInput").ap()
    out = nc.dram_tensor("out_0", (P, COLS), F32, kind="ExternalOutput").ap()
    build(nc, ins, out)
    r = run_bass_kernel_spmd(nc, [{f"in_{k}": v for k, v in arrays.items()}], core_ids=[0])
    return np.ascontiguousarray(r.results[0]["out_0"][:, :N].T)
```

```python
import concourse.bass as bass
import concourse.mybir as mybir
from contextlib import ExitStack

F32 = mybir.dt.float32
I32 = mybir.dt.int32
BF16 = mybir.dt.bfloat16
ALU = mybir.AluOpType
ACT = mybir.ActivationFunctionType
AX = mybir.AxisListType

P = 128
N, E, D, HID = 6250, 100000, 128, 64
LAYERS, HEADS, HEAD = 5, 4, 32
EDGE_TILES = -(-E // P)
NODE_TILES = -(-N // P)
WINDOWS = NODE_TILES + 1
COLS = WINDOWS * P
GROUP = 4
RING = 4
PAIRS = -(-(EDGE_TILES + NODE_TILES - 1) // (GROUP * RING)) * GROUP * RING
GROUPS = PAIRS // GROUP
ROUNDS = GROUPS // RING
KBLOCKS = -(-(PAIRS + 2 * GROUP) // P)
KCOLS = KBLOCKS * P
CHUNK = 400
CHUNKS = COLS // CHUNK
FULL = N // CHUNK
TURN = 5
STEPS = WINDOWS // TURN
SLOTS = 4
assert STEPS % SLOTS == 2
SEQ_ROWS = 32
SEQ = PAIRS * P // SEQ_ROWS
SEQ_PAIRS = PAIRS // SEQ_ROWS
FAR = -1.0e30
EPS = 1e-5
CREDIT = 64
PAD_NODE = WINDOWS * P


class Gate:

    def __init__(self, ctx, nc, name, credit=CREDIT):
        self.sem = ctx.enter_context(nc.semaphore(name))
        self.base = credit
        self.credit = credit

    def at(self, n):
        return self.base + n

    def passed(self, n):
        self.base += n


class Ctx:
    pass


def _setup(ctx, nc):
    c = Ctx()
    c.nc = nc

    def sb(name, shape, dt=F32):
        return ctx.enter_context(nc.sbuf_tensor(name, shape, dt))

    c.A = sb("bigA", [P, COLS])
    c.Bwide = sb("bigB", [P, WINDOWS * (D + 2 * HEADS)])
    c.B = c.Bwide[:, 0:COLS]
    c.C = sb("bigC", [P, COLS])
    c.DE = sb("bigDE", [P, 2 * COLS])
    c.D = c.DE[:, 0:COLS]
    c.E = c.DE[:, COLS:2 * COLS]
    c.F = sb("bigF", [P, COLS])
    rings = sb("rings", [P, 3 * RING * GROUP * P])
    c.gbuf, c.ebuf, c.sel = (
        rings[:, i * RING * GROUP * P:(i + 1) * RING * GROUP * P].rearrange("p (a b x) -> p a b x", a=RING, b=GROUP)
        for i in range(3))
    c.normal = rings[:, 0:SLOTS * TURN * P]
    c.soft = rings[:, 0:SEQ]
    c.rows = c.DE[0:1, 3 * SEQ + 8:3 * SEQ + 8 + 3 * P + 2]
    c.idx = sb("idx", [P, RING, GROUP], I32)
    c.srcK = sb("srcK", [P, KCOLS], I32)
    c.relK = sb("relK", [P, KCOLS])
    c.wK = sb("wK", [P, KCOLS])
    c.tRow = sb("tRow", [1, KCOLS], I32)
    c.nRow = sb("nRow", [1, KCOLS], I32)
    c.ident = sb("ident", [P, P])
    c.ones = sb("ones", [P, P])
    c.bias = sb("bias", [P, 3, D])
    c.iota = sb("iota", [P, P])
    c.small = sb("small", [P, 64])
    c.eps = sb("eps", [P, 1])
    c.stats = sb("stats", [P, 2, (FULL + 1) * 6])
    c.W1g = sb("W1g", [P, HID])
    c.W2g = sb("W2g", [HID, D])
    c.W1T = sb("W1T", [P, D])
    c.encW = sb("encW", [P, D])
    c.W1 = sb("W1", [P, 2 * D])
    c.W2 = sb("W2", [P, 2, D])
    c.W3 = sb("W3", [P, 4, D])
    c.We = sb("We", [P, 2, D])
    c.cols = sb("cols", [P, 64])
    c.gates = {}

    def gate(name, credit=CREDIT):
        g = Gate(ctx, nc, name, credit)
        c.gates[name] = g
        return g

    c.index = gate("index")
    c.select = gate("select")
    c.joined = gate("joined")
    c.message = gate("message")
    c.product = gate("product")
    c.added = gate("added")
    c.turned = gate("turned")
    c.scored = gate("scored")
    c.centred = gate("centred")
    c.squared = gate("squared")
    c.varied = gate("varied")
    c.rooted = gate("rooted")
    c.chunked = gate("chunked")
    c.meaned = gate("meaned")
    c.small_dve = gate("small_dve")
    c.small_pe = gate("small_pe")
    c.small_pool = gate("small_pool")
    c.tick_pe = gate("tick_pe")
    c.tick_act = gate("tick_act")
    c.tick_dve = gate("tick_dve")
    c.tick_pool = gate("tick_pool")
    c.tick_sp = gate("tick_sp")
    c.staged = gate("staged")
    c.cleared = gate("cleared")
    c.applied = gate("applied")
    c.keyed = gate("keyed")
    c.expanded = gate("expanded")
    c.fed = gate("fed")
    c.counted = gate("counted")
    c.told = gate("told")
    c.gathered = [gate(f"gathered{i}", 0) for i in range(RING)]
    c.attrs = [gate(f"attrs{i}", 0) for i in range(RING)]
    c.loaded = gate("loaded", 0)
    c.stored = [gate(f"stored{i}", 0) for i in range(SLOTS)]
    c.spilled = [gate(f"spilled{i}", 0) for i in range(RING)]
    c.moved = gate("moved", 0)
    c.whole = gate("whole")
    c.names = [0]

    def name(what):
        c.names[0] += 1
        return f"{what}_{c.names[0]}"
    c.name = name
    return c


def _hold(eng, gate, n, tick=None):
    v = gate.at(n)
    eng.wait_ge(gate.sem, v)
    if tick is not None and not isinstance(v, int):
        eng.sem_inc(tick.sem, 1)


def _small(c, eng, gate, count, make):
    make().then_inc(gate.sem, 1)
    gate.passed(1)
    eng.wait_ge(gate.sem, gate.at(0))


def _start(c, ins):
    nc = c.nc
    loads = [
        (c.A[:, :], ins["xT"]),
        (c.W1g[:, :], ins["L0_gnn_W1"]), (c.W2g[:, :], ins["L0_gnn_W2"]), (c.W1T[:, :], ins["L1_W_T"]),
        (c.encW[:, :], ins["L2_gnn_enc_W"]),
        (c.cols[:, 0:ins["cols"].shape[1]], ins["cols"]),
    ]
    for i in (0, 1):
        loads.append((c.We[:, i, :], ins[f"L3_gnn_We{i + 1}"].to_broadcast([P, D])))
    with nc.Block() as block:
        @block.sync
        def _(e):
            gates = c.stored + c.spilled
            assert len(gates) == len(loads)
            for (dst, src), g in zip(loads, gates):
                e.dma_start(dst, src).then_inc(g.sem, 16)
                g.passed(16)
            for g in gates:
                e.wait_ge(g.sem, g.at(0))

        @block.vector
        def _(e):
            for g in c.gates.values():
                if g.credit:
                    e.sem_inc(g.sem, g.credit)
            e.memset(c.ones[:, :], 1.0)
            e.memset(c.eps[:, :], EPS)

    with nc.Block() as block:
        @block.gpsimd
        def _(e):
            _small(c, e, c.small_pool, 1, lambda: e.iota(
                c.idx[:, :, :].rearrange("p a b -> p (a b)"), [[1, RING * GROUP]], base=0, channel_multiplier=0))
            _small(c, e, c.small_pool, 1, lambda: e.memset(c.ident[:, :], 0.0))
            _small(c, e, c.small_pool, 1, lambda: e.affine_select(
                out=c.ident[:, :], in_=c.ident[:, :], compare_op=ALU.not_equal, fill=1.0, base=0,
                pattern=[[-1, P]], channel_multiplier=1))
            _small(c, e, c.small_pool, 1, lambda: e.iota(c.iota[:, :], [[1, P]], base=0, channel_multiplier=0,
                                                          allow_small_or_imprecise_dtypes=True))


def _walk(c, ins, dram):
    nc = c.nc
    s = c.small
    start, edge_lo, edge_hi, full, steps, ends, shift, number = (
        c.B[:, 64 * i:64 * i + WINDOWS] for i in range(8))
    raw = c.B[:, 1024:1024 + EDGE_TILES].bitcast(I32)
    flat = c.B[:, 2048:2048 + EDGE_TILES]
    hit = c.B[:, 3072:3072 + EDGE_TILES]
    whole = c.B[:, 512:512 + 2 * 64].bitcast(I32)
    pair = c.B[:, 704:704 + KBLOCKS]
    node = c.B[:, 720:720 + KBLOCKS]
    edge = c.B[:, 736:736 + KBLOCKS]
    node_i = c.B[:, 752:752 + KBLOCKS].bitcast(I32)
    edge_i = c.B[:, 768:768 + KBLOCKS].bitcast(I32)
    far = c.B[:, 784:784 + KBLOCKS]
    grid = c.grid = c.C[:, 0:KBLOCKS * NODE_TILES].rearrange("p (k n) -> p k n", n=NODE_TILES)
    grid2 = c.C[:, 512:512 + KBLOCKS * NODE_TILES].rearrange("p (k n) -> p k n", n=NODE_TILES)
    bounds = c.B[:, 832:832 + WINDOWS]
    n = NODE_TILES
    with nc.psum_tensor("walk_ps", [P, WINDOWS], F32) as ps:
        with nc.Block() as block:
            @block.sync
            def _(e):
                e.dma_start(raw, ins["dst"].rearrange("t p -> (t p)").rearrange("(a b) -> a b", a=P)
                            ).then_inc(c.loaded.sem, 16)
                e.wait_ge(c.loaded.sem, c.loaded.at(16))

            @block.gpsimd
            def _(e):
                e.iota(bounds, [[P, WINDOWS]], base=0, channel_multiplier=0, allow_small_or_imprecise_dtypes=True)
                e.iota(number, [[1, WINDOWS]], base=0, channel_multiplier=0, allow_small_or_imprecise_dtypes=True)
                e.iota(pair, [[P, KBLOCKS]], base=0, channel_multiplier=1, allow_small_or_imprecise_dtypes=True)
        c.loaded.passed(16)
        with nc.Block() as block:
            @block.vector
            def _(e):
                _small(c, e, c.small_dve, 1, lambda: e.tensor_copy(flat, raw))
                with e.Fori(0, WINDOWS) as i:
                    _hold(e, c.added, i, c.tick_dve)
                    e.tensor_scalar(hit, flat, bounds[:, bass.ds(i, 1)], 0.0, ALU.is_lt, ALU.add,
                                    accum_out=start[:, bass.ds(i, 1)]).then_inc(c.added.sem, 1)
        c.added.passed(WINDOWS)
        with nc.Block() as block:
            @block.tensor
            def _(e):
                e.matmul(ps[:, :], c.ones[:, :], start, start=True, stop=True).then_inc(c.small_pe.sem, 1)

            @block.vector
            def _(e):
                def step(make):
                    _small(c, e, c.small_dve, 1, make)
                e.wait_ge(c.small_pe.sem, c.small_pe.at(1))
                step(lambda: e.tensor_copy(start, ps[:, :]))
                step(lambda: e.tensor_copy(whole[:, 0:WINDOWS], start))
                step(lambda: e.tensor_scalar(whole[:, 0:WINDOWS], whole[:, 0:WINDOWS], 7, None,
                                             ALU.arith_shift_right))
                step(lambda: e.tensor_copy(edge_lo, whole[:, 0:WINDOWS]))
                step(lambda: e.tensor_scalar(edge_hi, start, -1.0, None, ALU.add))
                step(lambda: e.tensor_copy(whole[:, 64:64 + WINDOWS], edge_hi))
                step(lambda: e.tensor_scalar(whole[:, 64:64 + WINDOWS], whole[:, 64:64 + WINDOWS], 7, None,
                                             ALU.arith_shift_right))
                step(lambda: e.tensor_copy(edge_hi, whole[:, 64:64 + WINDOWS]))
                step(lambda: e.tensor_tensor(full[:, 0:n], start[:, 1:n + 1], start[:, 0:n], ALU.is_gt))
                step(lambda: e.tensor_tensor(steps[:, 0:n], edge_hi[:, 1:n + 1], edge_lo[:, 0:n], ALU.subtract))
                step(lambda: e.scalar_tensor_tensor(steps[:, 0:n], steps[:, 0:n], 1.0, full[:, 0:n],
                                                    ALU.add, ALU.mult))
                step(lambda: e.tensor_tensor_scan(ends[:, 0:n], c.ones[:, 0:n], steps[:, 0:n], 0.0,
                                                  ALU.mult, ALU.add))
                step(lambda: e.tensor_tensor(shift[:, 0:n], steps[:, 0:n], ends[:, 0:n], ALU.subtract))
                step(lambda: e.tensor_tensor(shift[:, 0:n], shift[:, 0:n], edge_lo[:, 0:n], ALU.add))
                step(lambda: e.tensor_tensor(grid, ends[:, 0:n].unsqueeze(1).to_broadcast([P, KBLOCKS, n]),
                                             pair.unsqueeze(2).to_broadcast([P, KBLOCKS, n]), ALU.is_le))
                step(lambda: e.tensor_reduce(node, grid, AX.X, ALU.add))
                step(lambda: e.tensor_tensor(grid, number[:, 0:n].unsqueeze(1).to_broadcast([P, KBLOCKS, n]),
                                             node.unsqueeze(2).to_broadcast([P, KBLOCKS, n]), ALU.is_equal))
                step(lambda: e.tensor_tensor(grid2, grid,
                                             shift[:, 0:n].unsqueeze(1).to_broadcast([P, KBLOCKS, n]), ALU.mult))
                step(lambda: e.tensor_reduce(edge, grid2, AX.X, ALU.add))
                step(lambda: e.tensor_tensor(edge, edge, pair, ALU.add))
                step(lambda: e.tensor_scalar(edge, edge, float(EDGE_TILES - 1), 0.0, ALU.min, ALU.max))
                step(lambda: e.tensor_copy(edge_i, edge))
                step(lambda: e.tensor_copy(node_i, node))
                step(lambda: e.tensor_scalar(far, node, float(P), None, ALU.mult))
    c.small_pe.passed(1)
    rows_d = c.C[:, 1024:1024 + KBLOCKS * P].rearrange("p (k x) -> p k x", x=P)
    rows_s = c.C[:, 2048:2048 + KBLOCKS * P].rearrange("p (k x) -> p k x", x=P)
    rows_w = c.C[:, 3072:3072 + KBLOCKS * P].rearrange("p (k x) -> p k x", x=P)
    with nc.Block() as block:
        @block.sync
        def _(e):
            with nc.allow_non_contiguous_dma(reason="two rows of small integers"):
                e.dma_start(dram.t.rearrange("(k p) -> p k", p=P), edge_i).then_inc(c.moved.sem, 16)
                e.dma_start(dram.n.rearrange("(k p) -> p k", p=P), node_i).then_inc(c.moved.sem, 16)
            e.wait_ge(c.moved.sem, c.moved.at(32))
            e.dma_start(c.tRow[:, :], dram.t.rearrange("(a x) -> a x", a=1)).then_inc(c.moved.sem, 16)
            e.dma_start(c.nRow[:, :], dram.n.rearrange("(a x) -> a x", a=1)).then_inc(c.moved.sem, 16)
            e.wait_ge(c.moved.sem, c.moved.at(64))

        @block.gpsimd
        def _(e):
            tiles = c.idx[:, :, :].rearrange("p a b -> p (a b)")
            _small(c, e, c.small_pool, 1, lambda: e.tensor_copy(tiles[:, 0:KBLOCKS], edge_i))
            for k in range(KBLOCKS):
                for t, (rows, src) in enumerate(((rows_d, "dst"), (rows_s, "src"), (rows_w, "w"))):
                    out = rows[:, k, :] if src == "w" else rows[:, k, :].bitcast(I32)
                    e.indirect_dma_start(out, None, ins[src],
                                         bass.IndirectOffsetOnAxis(ap=tiles[:, k:k + 1], axis=0)
                                         ).then_inc(c.gathered[t].sem, 16)
            for t in range(3):
                c.gathered[t].passed(16 * KBLOCKS)
                e.wait_ge(c.gathered[t].sem, c.gathered[t].at(0))
    c.moved.passed(64)
    size = P * KBLOCKS
    with nc.psum_tensor("rel_ps", [P, 1024], F32) as rel_ps, nc.psum_tensor("src_ps", [P, 1024], F32) as src_ps, \
            nc.psum_tensor("w_ps", [P, 1024], F32) as w_ps:
        wide_d = c.C[:, 1024:1024 + size]
        wide_s = c.C[:, 2048:2048 + size]
        with nc.Block() as block:
            @block.vector
            def _(e):
                def step(make):
                    _small(c, e, c.small_dve, 1, make)
                step(lambda: e.tensor_copy(c.B[:, 1024:1024 + size], wide_d.bitcast(I32)))
                step(lambda: e.tensor_copy(c.B[:, 2048:2048 + size], wide_s.bitcast(I32)))
                step(lambda: e.tensor_tensor(
                    c.B[:, 3072:3072 + size].rearrange("p (k x) -> p k x", x=P),
                    c.B[:, 1024:1024 + size].rearrange("p (k x) -> p k x", x=P),
                    far.unsqueeze(2).to_broadcast([P, KBLOCKS, P]), ALU.subtract))
        with nc.Block() as block:
            @block.sync
            def _(e):
                e.dma_start(dram.seq[1:1 + KCOLS * P].rearrange("(k p x) -> p k x", p=P, x=P),
                            c.B[:, 1024:1024 + size].rearrange("p (k x) -> p k x", x=P)).then_inc(c.moved.sem, 16)
                e.wait_ge(c.moved.sem, c.moved.at(16))

            @block.tensor
            def _(e):
                for k in range(KBLOCKS):
                    for ps, at in ((rel_ps, c.B[:, 3072:]), (src_ps, c.B[:, 2048:])):
                        e.transpose(ps[:, k * P:k * P + P], at[:, k * P:k * P + P], c.ident[:, :])
                    last = e.transpose(w_ps[:, k * P:k * P + P], rows_w[:, k, :], c.ident[:, :])
                last.then_inc(c.small_pe.sem, 1)

            @block.vector
            def _(e):
                e.wait_ge(c.small_pe.sem, c.small_pe.at(1))
                e.tensor_copy(c.relK[:, :], rel_ps[:, 0:KCOLS])
                e.tensor_copy(c.srcK[:, :], src_ps[:, 0:KCOLS])
                e.tensor_copy(c.wK[:, :], w_ps[:, 0:KCOLS])
                e.memset(s[0:1, 0:1], -1.0)
                e.memset(s[0:1, 1:2], -2.0)
        c.small_pe.passed(1)
        c.moved.passed(16)
    with nc.Block() as block:
        @block.sync
        def _(e):
            e.dma_start(dram.seq[0:1].rearrange("(a b) -> a b", a=1), s[0:1, 0:1]).then_inc(c.moved.sem, 16)
            end = 1 + PAIRS * P
            e.dma_start(dram.seq[end:end + 1].rearrange("(a b) -> a b", a=1), s[0:1, 1:2]
                        ).then_inc(c.moved.sem, 16)
            e.wait_ge(c.moved.sem, c.moved.at(32))
    c.moved.passed(32)


def _degree(c, root, share, dram):
    nc = c.nc
    count = c.F[:, 0:KCOLS]
    by_pair = c.F[:, KCOLS:2 * KCOLS]
    total, shared = (c.D[0:WINDOWS, i * P:i * P + P] for i in range(2))
    half = c.gbuf[:, :, :, :].rearrange("p a b x -> p (a b x)").bitcast(BF16)
    near, iota, one = half[:, 0:KCOLS], half[:, KCOLS:KCOLS + P], half[:, KCOLS + P:KCOLS + P + 1]
    sel = c.sel[:, :, :, :].rearrange("p a b x -> p (a b x)").bitcast(BF16)[:, 0:RING * GROUP * P].rearrange(
        "p (a b x) -> p a b x", a=RING, b=GROUP)
    with nc.psum_tensor(c.name("count"), [P, RING, 512], F32) as ps:
        with nc.Block() as block:
            @block.tensor
            def _(e):
                with e.Fori(0, ROUNDS) as i:
                    for g in range(RING):
                        q = i * RING + g
                        _hold(e, c.select, q + 1, c.tick_pe)
                        _hold(e, c.counted, q - RING + 1, c.tick_pe)
                        for r in range(GROUP):
                            last = e.matmul(ps[:, g, r:r + 1], sel[:, g, r, :], one,
                                            start=True, stop=True)
                        last.then_inc(c.product.sem, 1)

            @block.vector
            def _(e):
                e.memset(count[:, PAIRS:KCOLS], 0.0)
                e.memset(total, 0.0)
                _small(c, e, c.small_dve, 1, lambda: e.tensor_copy(near, c.relK[:, :]))
                _small(c, e, c.small_dve, 1, lambda: e.tensor_copy(iota, c.iota[:, :]))
                _small(c, e, c.small_dve, 1, lambda: e.tensor_copy(one, c.ones[:, 0:1]))
                with e.Fori(0, ROUNDS) as i:
                    for g in range(RING):
                        _select(c, e, i * RING + g, g, sel, near, iota)

            @block.scalar
            def _(e):
                with e.Fori(0, ROUNDS) as i:
                    for g in range(RING):
                        q = i * RING + g
                        _hold(e, c.product, q + 1, c.tick_act)
                        e.activation(count[:, bass.ds(q * GROUP, GROUP)], ps[:, g, 0:GROUP], ACT.Copy
                                     ).then_inc(c.counted.sem, 1)
        for gate in (c.product, c.select, c.counted):
            gate.passed(GROUPS)
    with nc.psum_tensor(c.name("by_pair"), [P, 1024], F32) as ps, \
            nc.psum_tensor(c.name("total"), [P, P], F32) as sum_ps:
        with nc.Block() as block:
            @block.tensor
            def _(e):
                for k in range(KBLOCKS):
                    last = e.transpose(ps[:, k * P:k * P + P], count[:, k * P:k * P + P], c.ident[:, :])
                last.then_inc(c.turned.sem, 1)
                e.wait_ge(c.chunked.sem, c.chunked.at(1))
                for k in range(KBLOCKS):
                    last = e.matmul(sum_ps[0:NODE_TILES, :], c.grid[:, k, :], by_pair[:, k * P:k * P + P],
                                    start=k == 0, stop=k == KBLOCKS - 1)
                last.then_inc(c.product.sem, 1)

            @block.scalar
            def _(e):
                e.wait_ge(c.turned.sem, c.turned.at(1))
                e.copy(by_pair, ps[:, 0:KCOLS]).then_inc(c.chunked.sem, 1)
                e.wait_ge(c.product.sem, c.product.at(1))
                e.copy(total[0:NODE_TILES, :], sum_ps[0:NODE_TILES, :]).then_inc(c.counted.sem, 1)
    for gate in (c.turned, c.chunked, c.product, c.counted):
        gate.passed(1)
    _whole(c,
           ("v", lambda e: e.tensor_scalar(shared, total, 1.0, None, ALU.max)),
           ("s", lambda e: e.activation(total, total, ACT.Sqrt, bias=c.ones[0:WINDOWS, 0:1])),
           ("v", lambda e: e.reciprocal(total, total)),
           ("v", lambda e: e.reciprocal(shared, shared)))

    def spread(e):
        for row, src in ((dram.root, total), (dram.share, shared)):
            e.dma_start(row.rearrange("(w p) -> w p", p=P), src).then_inc(c.moved.sem, 16)
        e.wait_ge(c.moved.sem, c.moved.at(32))
        for row, to in ((dram.root, root), (dram.share, share)):
            e.dma_start(to, row.rearrange("(a x) -> a x", a=1).to_broadcast([P, COLS])).then_inc(c.moved.sem, 16)
        c.moved.passed(64)
        e.wait_ge(c.moved.sem, c.moved.at(0))
    return spread


def _select(c, e, q, g, sel=None, near=None, iota=None):
    e.wait_ge(c.product.sem, c.product.at(q - RING + 1))
    sel = c.sel if sel is None else sel
    near = c.relK if near is None else near
    iota = c.iota if iota is None else iota
    e.tensor_tensor(sel[:, g, :, :],
                    near[:, bass.ds(q * GROUP, GROUP)].unsqueeze(2).to_broadcast([P, GROUP, P]),
                    iota[:, :].unsqueeze(1).to_broadcast([P, GROUP, P]), ALU.is_equal
                    ).then_inc(c.select.sem, 1)


def _words(nc, eng, row, q, top, why, groups=1):
    return nc.values_load_multi_w_load_instructions(
        row[0:1, bass.ds(q * GROUP, groups * GROUP)], engines=[eng.engine], min_val=0, max_val=top,
        skip_runtime_bounds_check_because=why)[1]


def _nodes(nc, c, eng, q, groups=1):
    return _words(nc, eng, c.nRow, q, WINDOWS - 1, "it counts node tiles", groups)


def _pass(c, kind, table, agg, width=D, attr=None, query=None, score=None, spill=None, odd=None, weights=()):
    nc = c.nc
    cell = D + 2 * HEADS if kind == "attend" else P
    lanes = 2 if kind == "attend" else 1
    wins = [] if agg is None else [a.rearrange("p (w x) -> p w x", w=WINDOWS) for a in (agg, odd)[0:lanes]]
    banks = 2 if kind == "look" else RING
    gbuf, msg = c.gbuf, None
    if kind == "look":
        size = RING * GROUP * 2 * D
        gbuf = c.DE[:, 0:size].rearrange("p (a b x) -> p a b x", a=RING, b=GROUP)
        prod, turn = (c.DE[:, size + i * 2 * GROUP * P:size + (i + 1) * 2 * GROUP * P].rearrange(
            "p (a b x) -> p a b x", a=2, b=GROUP) for i in range(2))
        size += 4 * GROUP * P
        bare, edge = (c.DE[:, size + i * 2 * GROUP * HEADS:size + (i + 1) * 2 * GROUP * HEADS].rearrange(
            "p (a x) -> p a x", a=2) for i in range(2))
    if kind == "attend":
        msg = c.DE[:, WINDOWS * cell:WINDOWS * cell + RING * GROUP * cell].rearrange(
            "p (a b x) -> p a b x", a=RING, b=GROUP)
    with ExitStack() as ctx:
        part = ctx.enter_context(nc.psum_tensor(
            c.name("part"), [P, banks, GROUP, 2 * P if kind in ("look", "attend") else P], F32))
        if kind == "look":
            turned = ctx.enter_context(nc.psum_tensor(c.name("turned"), [P, 2, GROUP, P], F32))
        block = ctx.enter_context(nc.Block())

        if kind == "edge":
            @block.sync
            def _(e):
                _load(c, e, weights)
                with e.Fori(0, ROUNDS) as i:
                    for g in range(RING):
                        q = i * RING + g
                        tile = _words(nc, e, c.tRow, q, EDGE_TILES - 1, "clamped when it was made")
                        _hold(e, c.joined, q - RING + 1, c.tick_sp)
                        for r in range(GROUP):
                            e.dma_start(c.ebuf[:, g, r, :],
                                        attr[bass.ds(tile[r], 1), :, :].rearrange("a p f -> (a p) f")
                                        ).then_inc(c.attrs[g].sem, 16)
                e.wait_ge(c.loaded.sem, c.loaded.at(0))

        if kind == "look":
            @block.sync
            def _(e):
                _load(c, e, weights)
                with e.Fori(0, ROUNDS) as i:
                    for g in range(RING):
                        _hold(e, c.gathered[g], 16 * GROUP * (i + 1), c.tick_sp)
                        e.dma_start(spill[bass.ds(i * RING + g, 1), :, :, :].rearrange("a p r f -> (a p) r f"),
                                    gbuf[:, g, :, D:2 * D]).then_inc(c.spilled[g].sem, 16)
                for g in range(RING):
                    e.wait_ge(c.spilled[g].sem, c.spilled[g].at(16 * ROUNDS))
                if weights:
                    e.wait_ge(c.loaded.sem, c.loaded.at(0))

        if kind == "attend":
            @block.sync
            def _(e):
                with e.Fori(0, ROUNDS) as i:
                    for g in range(RING):
                        q = i * RING + g
                        _hold(e, c.scored, q - RING + 1, c.tick_sp)
                        e.dma_start(gbuf[:, g, :, :], spill[bass.ds(q, 1), :, :, :].rearrange(
                            "a p r f -> (a p) r f")).then_inc(c.attrs[g].sem, 16)

            @block.gpsimd
            def _(e):
                def heads(x, g):
                    return x[:, g, :, 0:D].rearrange("p r (h x) -> p r h x", h=HEADS)
                with e.Fori(0, ROUNDS) as i:
                    for g in range(RING):
                        q = i * RING + g
                        prob = score[:, bass.ds(q * GROUP * HEADS, GROUP * HEADS)].rearrange(
                            "p (r h) -> p r h", h=HEADS)
                        weight = c.wK[:, bass.ds(q * GROUP, GROUP)].unsqueeze(2).to_broadcast([P, GROUP, HEADS])
                        _hold(e, c.product, q - RING + 1, c.tick_pool)
                        _hold(e, c.attrs[g], 16 * (i + 1), c.tick_pool)
                        e.tensor_tensor(msg[:, g, :, D + HEADS:cell], prob, weight, ALU.mult
                                        ).then_inc(c.keyed.sem, 1)
                        e.tensor_tensor(heads(msg, g), heads(gbuf, g),
                                        prob.unsqueeze(3).to_broadcast([P, GROUP, HEADS, HEAD]), ALU.mult
                                        ).then_inc(c.scored.sem, 1)

            @block.scalar
            def _(e):
                with e.Fori(0, ROUNDS) as i:
                    for g in range(RING):
                        q = i * RING + g
                        _hold(e, c.product, q - RING + 1, c.tick_act)
                        e.copy(msg[:, g, :, D:D + HEADS],
                               score[:, bass.ds(q * GROUP * HEADS, GROUP * HEADS)].rearrange(
                                   "p (r h) -> p r h", h=HEADS)).then_inc(c.expanded.sem, 1)
        else:
            @block.gpsimd
            def _(e):
                with e.Fori(0, ROUNDS) as i:
                    for g in range(RING):
                        _hold(e, c.index, i * RING + g + 1, c.tick_pool)
                        for r in range(GROUP):
                            e.indirect_dma_start(gbuf[:, g, r, 0:table.shape[1]], None, table,
                                                 bass.IndirectOffsetOnAxis(ap=c.idx[:, g, r:r + 1], axis=0)
                                                 ).then_inc(c.gathered[g].sem, 16)

            @block.scalar
            def _(e):
                def index(q, g, rounds):
                    _hold(e, c.joined if kind == "look" else c.product, q - RING + 1, c.tick_act)
                    if kind == "look":
                        _hold(e, c.spilled[g], 16 * rounds, c.tick_act)
                    e.copy(c.idx[:, g, :], c.srcK[:, bass.ds(q * GROUP, GROUP)]).then_inc(c.index.sem, 1)

                index(0, 0, 0)
                index(1, 1, 0)
                with e.Fori(0, ROUNDS) as i:
                    for g in range(RING):
                        q = i * RING + g
                        index(q + 2, (g + 2) % RING, i + (g + 2) // RING)
                        if kind == "edge":
                            e.wait_ge(c.joined.sem, c.joined.at(q + 1))
                            e.activation(gbuf[:, g, :, :], gbuf[:, g, :, :], ACT.Relu).then_inc(c.message.sem, 1)
                        elif kind == "look":
                            _hold(e, c.product, q - 1, c.tick_act)
                            e.wait_ge(c.turned.sem, c.turned.at(q + 1))
                            e.activation(turn[:, g % 2, :, :], turned[:, g % 2, :, :], ACT.Copy
                                         ).then_inc(c.message.sem, 1)

        @block.tensor
        def _(e):
            with e.Fori(0, ROUNDS) as i:
                for g in range(RING):
                    q = i * RING + g
                    b = g % banks
                    _hold(e, c.select, q + 1, c.tick_pe)
                    if kind == "look":
                        _hold(e, c.message, q - 1, c.tick_pe)
                        for r in range(GROUP):
                            last = e.transpose(turned[:, b, r, :], c.sel[:, g, r, :], c.ident[:, :])
                        last.then_inc(c.turned.sem, 1)
                        where = _nodes(nc, c, e, q)
                        _hold(e, c.message, q + 1, c.tick_pe)
                        _hold(e, c.scored, q - 1, c.tick_pe)
                        for r in range(GROUP):
                            last = e.matmul(part[:, b, r, 0:D + HEADS], turn[:, b, r, :],
                                            query[:, bass.ds(where[r] * (D + HEADS), D + HEADS)],
                                            start=True, stop=True)
                        last.then_inc(c.product.sem, 1)
                        continue
                    _hold(e, c.added, (q - banks + 1) * GROUP, c.tick_pe)
                    if kind == "sum":
                        _hold(e, c.gathered[g], 16 * GROUP * (i + 1), c.tick_pe)
                    elif kind == "edge":
                        _hold(e, c.message, q + 1, c.tick_pe)
                    elif kind == "attend":
                        _hold(e, c.expanded, q + 1, c.tick_pe)
                        _hold(e, c.keyed, q + 1, c.tick_pe)
                        _hold(e, c.scored, q + 1, c.tick_pe)
                    for r in range(GROUP):
                        if kind == "attend":
                            last = e.matmul(part[:, b, r, 0:cell], c.sel[:, g, r, :], msg[:, g, r, :],
                                            start=True, stop=True)
                        else:
                            last = e.matmul(part[0:width, b, r, :], gbuf[:, g, r, 0:width], c.sel[:, g, r, :],
                                            start=True, stop=True)
                    last.then_inc(c.product.sem, 1)

        @block.vector
        def _(e):
            def prepare(q, g, i):
                scores = None if score is None else score[:, bass.ds(q * GROUP * HEADS, GROUP * HEADS)]
                if kind == "edge":
                    _hold(e, c.gathered[g], 16 * GROUP * (i + 1), c.tick_dve)
                    _hold(e, c.attrs[g], 16 * GROUP * (i + 1), c.tick_dve)
                    e.tensor_tensor(gbuf[:, g, :, :], gbuf[:, g, :, :], c.ebuf[:, g, :, :], ALU.add
                                    ).then_inc(c.joined.sem, 1)
                elif kind == "look":
                    b = g % 2
                    weight = c.wK[:, bass.ds(q * GROUP, GROUP)].unsqueeze(2).to_broadcast([P, GROUP, HEADS])
                    _hold(e, c.product, q + 1, c.tick_dve)
                    e.tensor_tensor(edge[:, b, :].rearrange("p (r h) -> p r h", h=HEADS),
                                    part[:, b, :, D:D + HEADS], weight, ALU.mult).then_inc(c.told.sem, 1)
                    _hold(e, c.gathered[g], 16 * GROUP * (i + 1), c.tick_dve)
                    e.tensor_tensor(prod[:, b, :, :], gbuf[:, g, :, 0:D], part[:, b, :, 0:D], ALU.mult
                                    ).then_inc(c.scored.sem, 1)
                    _hold(e, c.scored, q + 1, c.tick_dve)
                    e.tensor_reduce(bare[:, b, :], prod[:, b, :, :].rearrange("p r (h x) -> p (r h) x", h=HEADS),
                                    AX.X, ALU.add).then_inc(c.keyed.sem, 1)
                    _hold(e, c.told, q + 1, c.tick_dve)
                    _hold(e, c.keyed, q + 1, c.tick_dve)
                    e.tensor_tensor(scores, bare[:, b, :], edge[:, b, :], ALU.add).then_inc(c.joined.sem, 1)

            def add(q, g, where, r):
                into = wins[r % lanes][0:width, bass.ds(where, 1), :].rearrange("p a x -> p (a x)")
                e.wait_ge(c.added.sem, c.added.at(q * GROUP + r + 1 - lanes))
                e.tensor_tensor(into, into, part[0:width, g % banks, r, 0:cell], ALU.add
                                ).then_inc(c.added.sem, 1)

            if agg is None:
                _select(c, e, 0, 0)
                with e.Fori(0, ROUNDS) as i:
                    for g in range(RING):
                        q = i * RING + g
                        _select(c, e, q + 1, (g + 1) % RING)
                        prepare(q, g, i)
                return
            for a in (agg, odd)[0:lanes]:
                e.memset(a, 0.0).then_inc(c.cleared.sem, 1)
            e.wait_ge(c.cleared.sem, c.cleared.at(lanes))
            for g in range(3):
                _select(c, e, g, g)
            for g in range(2):
                prepare(g, g, 0)

            def steps(i, last):
                for g in range(RING):
                    q = i * RING + g
                    left = RING - 1 - g if last else RING
                    if left > 2:
                        _select(c, e, q + 3, (g + 3) % RING)
                    if left > 1:
                        prepare(q + 2, (g + 2) % RING, i + (g + 2) // RING)
                    if g % 2 == 0:
                        where = _nodes(nc, c, e, q, 2)
                    _hold(e, c.product, q + 1, c.tick_dve)
                    for r in range(GROUP):
                        add(q, g, where[g % 2 * GROUP + r], r)
            with e.Fori(0, ROUNDS - 1) as i:
                steps(i, False)
            steps(ROUNDS - 1, True)

    c.product.passed(GROUPS)
    c.select.passed(GROUPS + (agg is None))
    if agg is not None:
        c.added.passed(PAIRS)
        c.cleared.passed(lanes)
    if kind != "attend":
        c.index.passed(GROUPS + 2)
        for g in c.gathered:
            g.passed(16 * GROUP * ROUNDS)
    if kind == "edge":
        for g in c.attrs:
            g.passed(16 * GROUP * ROUNDS)
    if kind == "look":
        c.turned.passed(GROUPS)
        c.told.passed(GROUPS)
        for g in c.spilled:
            g.passed(16 * ROUNDS)
    if kind == "attend":
        c.expanded.passed(GROUPS)
        for g in c.attrs:
            g.passed(16 * ROUNDS)
    if kind in ("edge", "look"):
        c.joined.passed(GROUPS)
        c.message.passed(GROUPS)
    if kind in ("look", "attend"):
        c.scored.passed(GROUPS)
        c.keyed.passed(GROUPS)


def _chunk(i, size=CHUNK):
    return bass.ds(i * size, size)


def _load(c, e, pairs):
    for dst, src in pairs:
        e.dma_start(dst, src).then_inc(c.loaded.sem, 16)
    c.loaded.passed(16 * len(pairs))


def _dense(c, parts, by="act", prepare=None, feed=None, batch=None, sync=None):
    nc = c.nc
    k = len(parts)
    banks = 4 if k <= 2 else 2
    rounds = CHUNKS // banks
    ahead = banks // 2
    tail = []
    if batch:
        gain, offset, scale, shift = batch
        means = c.small[:, 2:2 + 2 * k].rearrange("p (k t) -> p k t", t=2)
        root = c.small[:, 8:8 + k]
        for o in range(k):
            tail.append(("v", lambda e, o=o: e.bn_aggr(means[:, o, :], c.stats[:, o, :])))
        tail += [
            ("s", lambda e: e.activation(root, means[:, :, 1], ACT.Sqrt, bias=c.eps[:, :])),
            ("v", lambda e: e.reciprocal(root, root)),
            ("v", lambda e: e.tensor_tensor(scale, root, gain, ALU.mult)),
            ("v", lambda e: e.tensor_tensor(root, means[:, :, 0], scale, ALU.mult)),
            ("v", lambda e: e.tensor_tensor(shift, offset, root, ALU.subtract)),
        ]
    with nc.psum_tensor(c.name("dense"), [P, banks, k, 512], F32) as ps, nc.Block() as block:
        if sync:
            block.sync(sync)

        def loop(steps):
            def run(e):
                with e.Fori(0, rounds - 1) as i:
                    for b in range(banks):
                        steps(e, i * banks + b, b, CHUNKS)
                for b in range(banks):
                    steps(e, CHUNKS - banks + b, b, banks - 1 - b)
            return run

        def take(e, who, n, b, tick):
            _hold(e, c.product, n + 1, tick)
            for o, (_, out, bias, func, rows) in enumerate(parts):
                to, got = out[0:rows, _chunk(n)], ps[0:rows, b, o, 0:CHUNK]
                if who == "dve":
                    e.tensor_scalar(to, got, bias, None, ALU.add).then_inc(c.chunked.sem, 1)
                elif bias is None:
                    e.activation(to, got, func).then_inc(c.chunked.sem, 1)
                else:
                    e.activation(to, got, func, bias=bias).then_inc(c.chunked.sem, 1)

        @block.scalar
        def _(e):
            def ready(n):
                for x, by_, plus in prepare or ():
                    e.activation(x[:, _chunk(n)], x[:, _chunk(n)], ACT.Relu, bias=plus, scale=by_
                                 ).then_inc(c.applied.sem, 1)

            def steps(e, n, b, left):
                if left >= ahead:
                    ready(n + ahead)
                if by == "act":
                    take(e, "act", n, b, c.tick_act)
            for n in range(ahead):
                ready(n)
            loop(steps)(e)
            _chain(c, e, "s", tail)

        @block.tensor
        def _(e):
            with e.Fori(0, rounds) as i:
                for b in range(banks):
                    n = i * banks + b
                    _hold(e, c.chunked, (n - banks + 1) * k, c.tick_pe)
                    if feed:
                        _hold(e, c.fed, n + 1, c.tick_pe)
                    if prepare:
                        _hold(e, c.applied, (n + 1) * len(prepare), c.tick_pe)
                    for o, (terms, _, _, _, rows) in enumerate(parts):
                        for j, (w, x) in enumerate(terms):
                            last = e.matmul(ps[0:rows, b, o, 0:CHUNK], w, x[0:w.shape[0], _chunk(n)],
                                            start=j == 0, stop=j == len(terms) - 1)
                    last.then_inc(c.product.sem, 1)

        if feed or batch or by == "dve":
            @block.vector
            def _(e):
                def add(n):
                    if feed:
                        x, a, b_ = (t[:, _chunk(n)] for t in feed)
                        e.tensor_tensor(x, a, b_, ALU.add).then_inc(c.fed.sem, 1)

                def steps(e, n, b, left):
                    if left >= ahead:
                        add(n + ahead)
                    if by == "dve":
                        take(e, "dve", n, b, c.tick_dve)
                    if batch:
                        _hold(e, c.chunked, (n + 1) * k, c.tick_dve)
                        for o, (_, out, _, _, _) in enumerate(parts):
                            real = out[:, n * CHUNK:N] if isinstance(n, int) and n == FULL else out[:, _chunk(n)]
                            e.bn_stats(c.stats[:, o, bass.ds(n * 6, 6)], real).then_inc(c.varied.sem, 1)
                for n in range(ahead):
                    add(n)
                loop(steps)(e)
                if batch:
                    e.wait_ge(c.varied.sem, c.varied.at(CHUNKS * k))
                _chain(c, e, "v", tail)
    c.product.passed(CHUNKS)
    c.chunked.passed(CHUNKS * k)
    c.whole.passed(len(tail))
    if feed:
        c.fed.passed(CHUNKS)
    if batch:
        c.varied.passed(CHUNKS * k)
    if prepare:
        c.applied.passed(CHUNKS * len(prepare))


def _chain(c, eng, mine, steps):
    for n, (who, make) in enumerate(steps):
        if who == mine:
            make(eng).then_inc(c.whole.sem, 1)
        eng.wait_ge(c.whole.sem, c.whole.at(n + 1))


def _whole(c, *steps):
    with c.nc.Block() as block:
        @block.vector
        def _(e):
            _chain(c, e, "v", steps)

        @block.scalar
        def _(e):
            _chain(c, e, "s", steps)
    c.whole.passed(len(steps))


def _turns(e, step, steps=STEPS):
    rounds = steps // SLOTS
    with e.Fori(0, rounds) as i:
        for b in range(SLOTS):
            step(i * SLOTS + b, b, i)
    for b in range(steps % SLOTS):
        step(rounds * SLOTS + b, b, rounds)


def _project(c, x, both, query):
    nc = c.nc
    stage = c.sel[:, 0, :, :]
    steps = WINDOWS
    with nc.psum_tensor(c.name("project"), [P, SLOTS, 512], F32) as ps, nc.Block() as block:
        @block.scalar
        def _(e):
            def step(n, b, i):
                _hold(e, c.product, n + 1 - SLOTS, c.tick_act)
                e.copy(stage[:, b, :], x[:, _chunk(n, P)]).then_inc(c.staged.sem, 1)
            _turns(e, step, steps)

        @block.tensor
        def _(e):
            def step(n, b, i):
                _hold(e, c.staged, n + 1, c.tick_pe)
                _hold(e, c.chunked, 2 * (n + 1 - SLOTS), c.tick_pe)
                e.matmul(ps[:, b, 0:3 * D], stage[:, b, :], c.W3[:, 0:3, :].rearrange("p j d -> p (j d)"),
                         start=True, stop=True).then_inc(c.product.sem, 1)
            _turns(e, step, steps)

        @block.vector
        def _(e):
            def step(n, b, i):
                _hold(e, c.product, n + 1, c.tick_dve)
                _hold(e, c.stored[b], 16 * i, c.tick_dve)
                e.tensor_tensor(c.normal[:, b * 2 * D:(b + 1) * 2 * D], ps[:, b, D:3 * D],
                                c.bias[:, 1:3, :].rearrange("p j d -> p (j d)"), ALU.add
                                ).then_inc(c.chunked.sem, 1)
                e.tensor_tensor(query[:, bass.ds(n * (D + HEADS), D)], ps[:, b, 0:D], c.bias[:, 0, :], ALU.add
                                ).then_inc(c.chunked.sem, 1)
            _turns(e, step, steps)

        @block.sync
        def _(e):
            view = both.rearrange("(n p) f -> n p f", p=P)

            def step(n, b, i):
                _hold(e, c.chunked, 2 * n + 1, c.tick_sp)
                e.dma_start(view[bass.ds(n, 1), :, :].rearrange("a p f -> (a p) f"),
                            c.normal[:, b * 2 * D:(b + 1) * 2 * D]).then_inc(c.stored[b].sem, 16)
            _turns(e, step, steps)
            for b, g in enumerate(c.stored):
                g.passed(16 * (steps // SLOTS + (b < steps % SLOTS)))
                e.wait_ge(g.sem, g.at(0))
    c.staged.passed(steps)
    c.product.passed(steps)
    c.chunked.passed(2 * steps)


def _store(c, out, gate, of, width=D):
    view = out.rearrange("(n t p) f -> n p t f", p=P, t=TURN)

    def program(e):
        def step(n, b, i):
            _hold(e, gate, (n + 1) * of, c.tick_sp)
            at = b * TURN * P
            e.dma_start(view[bass.ds(n, 1), :, :, :].rearrange("a p t f -> (a p) t f"),
                        c.normal[:, at:at + TURN * width].rearrange("p (t f) -> p t f", t=TURN)
                        ).then_inc(c.stored[b].sem, 16)
        _turns(e, step)
        for b, g in enumerate(c.stored):
            g.passed(16 * (STEPS // SLOTS + (b < STEPS % SLOTS)))
            e.wait_ge(g.sem, g.at(0))
    return program


def _table(c, x, out, width=D, other=None, op=None, apply=None):
    nc = c.nc
    size = TURN * P
    stage = c.sel[:, :, :, :].rearrange("p a b x -> p (a b x)")
    with nc.psum_tensor(c.name("turn"), [P, SLOTS, 1024], F32) as ps, nc.Block() as block:
        @block.vector
        def _(e):
            def step(n, b, i):
                at = b % 2 * size
                here = x[0:width, _chunk(n, size)]
                _hold(e, c.turned, n - 1, c.tick_dve)
                if other is None:
                    e.tensor_copy(stage[0:width, at:at + size], here).then_inc(c.staged.sem, 1)
                    return
                if apply:
                    _hold(e, c.applied, n + 1, c.tick_dve)
                plus = other[0:width, _chunk(n, size)]
                e.tensor_tensor(stage[0:width, at:at + size], here, plus, op).then_inc(c.staged.sem, 1)
                e.tensor_tensor(here, here, plus, op)
            _turns(e, step)

        @block.tensor
        def _(e):
            def step(n, b, i):
                _hold(e, c.staged, n + 1, c.tick_pe)
                _hold(e, c.chunked, n + 1 - SLOTS, c.tick_pe)
                for t in range(TURN):
                    at = b % 2 * size + t * P
                    last = e.transpose(ps[:, b, t * width:t * width + width], stage[0:width, at:at + P],
                                       c.ident[0:width, 0:width])
                last.then_inc(c.turned.sem, 1)
            _turns(e, step)

        @block.scalar
        def _(e):
            def ready(n):
                if apply:
                    func, by, plus = apply
                    e.activation(other[:, _chunk(n, size)], other[:, _chunk(n, size)], func, bias=plus, scale=by
                                 ).then_inc(c.applied.sem, 1)

            def step(n, b, i):
                got = ps[:, b, 0:TURN * width]
                if not isinstance(n, int):
                    ready(n + 2)
                _hold(e, c.turned, n + 1, c.tick_act)
                _hold(e, c.stored[b], 16 * i, c.tick_act)
                e.activation(c.normal[:, b * size:b * size + TURN * width], got, ACT.Copy
                             ).then_inc(c.chunked.sem, 1)
            ready(0)
            ready(1)
            _turns(e, step)

        block.sync(_store(c, out, c.chunked, 1, width))
    c.staged.passed(STEPS)
    c.turned.passed(STEPS)
    c.chunked.passed(STEPS)
    if apply:
        c.applied.passed(STEPS)


def _norm(c, x, plus, rows, out=None, back=True):
    nc = c.nc
    size = TURN * P
    stage = c.sel[:, :, :, :].rearrange("p a b x -> p (a b x)")
    room = stage[:, 2 * size:]
    stats = room[:, 0:2 * TURN * 6].rearrange("p (a t x) -> p a t x", a=2, x=6)
    merged = room[:, 64:64 + 2 * TURN * 2].rearrange("p (a x) -> p a x", a=2)
    means = room[:, 128:128 + WINDOWS * 2]
    by_node = means.rearrange("p (w t) -> p w t", t=2)
    root = room[:, 256:256 + WINDOWS]
    with nc.psum_tensor(c.name("turn"), [P, SLOTS, 1024], F32) as ps, nc.Block() as block:
        @block.vector
        def _(e):
            def add(n, b):
                _hold(e, c.turned, n - 1, c.tick_dve)
                at = b % 2 * size
                e.tensor_tensor(stage[:, at:at + size], x[:, _chunk(n, size)], plus[:, _chunk(n, size)],
                                ALU.add).then_inc(c.staged.sem, 1)

            def merge(n, b):
                _hold(e, c.varied, (n + 1) * TURN, c.tick_dve)
                for t in range(TURN):
                    e.bn_aggr(merged[:, b, t * 2:t * 2 + 2], stats[:, b, t, :]).then_inc(c.meaned.sem, 1)
                _hold(e, c.meaned, (n + 1) * TURN, c.tick_dve)
                e.tensor_copy(means[:, bass.ds(n * TURN * 2, TURN * 2)], merged[:, b, :]).then_inc(c.scored.sem, 1)

            def step(n, b, last):
                if not last:
                    add(n + 1, 1 - b)
                _hold(e, c.chunked, n + 1, c.tick_dve)
                for t in range(TURN):
                    e.bn_stats(stats[:, b, t, :], rows[:, bass.ds((n * TURN + t) * P, P)]
                               ).then_inc(c.varied.sem, 1)
            add(0, 0)
            step(0, 0, False)
            step(1, 1, False)
            with e.Fori(1, STEPS // 2 - 1) as i:
                for b in range(2):
                    merge(i * 2 + b - 2, b)
                    step(i * 2 + b, b, False)
            for n in (STEPS - 2, STEPS - 1):
                merge(n - 2, n % 2)
                step(n, n % 2, n == STEPS - 1)
            merge(STEPS - 2, 0)
            merge(STEPS - 1, 1)
            e.wait_ge(c.scored.sem, c.scored.at(STEPS))
            e.sem_inc(c.whole.sem, 1)
            e.wait_ge(c.rooted.sem, c.rooted.at(1))
            _small(c, e, c.small_dve, 1, lambda: e.reciprocal(root, root))

            def scale(n, b, i):
                _hold(e, c.fed, n + 1 - SLOTS, c.tick_dve)
                if out is not None:
                    _hold(e, c.stored[b], 16 * i, c.tick_dve)
                for t in range(TURN):
                    e.tensor_scalar(c.normal[:, b * size + t * P:b * size + t * P + P],
                                    rows[:, bass.ds((n * TURN + t) * P, P)],
                                    means[:, bass.ds((n * TURN + t) * 2, 1)], root[:, bass.ds(n * TURN + t, 1)],
                                    ALU.subtract, ALU.mult).then_inc(c.applied.sem, 1)
            _turns(e, scale)

        @block.scalar
        def _(e):
            def copy(n, b, i):
                _hold(e, c.turned, n + 1, c.tick_act)
                e.copy(rows[:, _chunk(n, size)], ps[:, b, 0:size]).then_inc(c.chunked.sem, 1)

            def back_copy(n, b, i):
                _hold(e, c.fed, n + 1, c.tick_act)
                e.copy(x[:, _chunk(n, size)], ps[:, b, 0:size]).then_inc(c.chunked.sem, 1)
            _turns(e, copy)
            e.wait_ge(c.whole.sem, c.whole.at(1))
            e.activation(root, by_node[:, :, 1], ACT.Sqrt, bias=c.eps[:, :]).then_inc(c.rooted.sem, 1)
            if back:
                _turns(e, back_copy)

        @block.tensor
        def _(e):
            def turn(n, b, i):
                _hold(e, c.staged, n + 1, c.tick_pe)
                _hold(e, c.chunked, n + 1 - SLOTS, c.tick_pe)
                for t in range(TURN):
                    at = b % 2 * size + t * P
                    last = e.transpose(ps[:, b, t * P:t * P + P], stage[:, at:at + P], c.ident[:, :])
                last.then_inc(c.turned.sem, 1)

            def back_turn(n, b, i):
                _hold(e, c.applied, (n + 1) * TURN, c.tick_pe)
                _hold(e, c.chunked, STEPS + n + 1 - SLOTS, c.tick_pe)
                for t in range(TURN):
                    at = b * size + t * P
                    last = e.transpose(ps[:, b, t * P:t * P + P], c.normal[:, at:at + P], c.ident[:, :])
                last.then_inc(c.fed.sem, 1)
            _turns(e, turn)
            if back:
                e.wait_ge(c.chunked.sem, c.chunked.at(STEPS))
                _turns(e, back_turn)
            else:
                e.sem_inc(c.fed.sem, STEPS)

        if out is not None:
            block.sync(_store(c, out, c.applied, TURN))
    for g in (c.staged, c.turned, c.fed, c.scored):
        g.passed(STEPS)
    c.chunked.passed(2 * STEPS if back else STEPS)
    for g in (c.varied, c.meaned, c.applied):
        g.passed(WINDOWS)
    for g in (c.rooted, c.whole):
        g.passed(1)


def _settle(c, agg, odd, we, skip):
    nc = c.nc
    cell = D + 2 * HEADS
    cells = agg.rearrange("p (w x) -> p w x", x=cell)
    down, edge = cells[:, :, D:D + HEADS], cells[:, :, D + HEADS:cell]
    wide = c.DE[:, WINDOWS * cell:WINDOWS * cell + 2 * TURN * D].rearrange("p (a x) -> p a x", a=2)
    stage = c.sel[:, :, :, :].rearrange("p a b x -> p (a b x)")
    size = TURN * P
    steps = WINDOWS // TURN
    _whole(c, ("v", lambda e: e.tensor_tensor(agg, agg, odd, ALU.add)),
           ("v", lambda e: e.tensor_scalar(down, down, 1e-30, None, ALU.max)),
           ("v", lambda e: e.reciprocal(down, down)),
           ("v", lambda e: e.tensor_tensor(edge, edge, down, ALU.mult)))
    with nc.psum_tensor(c.name("settle"), [P, 2, 1024], F32) as ps, nc.Block() as block:
        @block.vector
        def _(e):
            def mix(n, b):
                here = cells[:, bass.ds(n * TURN, TURN), :]
                to = stage[:, b * size:b * size + size].rearrange("p (t h x) -> p t h x", t=TURN, h=HEADS)
                part = wide[:, b, :].rearrange("p (t h x) -> p t h x", t=TURN, h=HEADS)

                def spread(x):
                    return x.unsqueeze(3).to_broadcast([P, TURN, HEADS, HEAD])
                _hold(e, c.turned, n - 1, c.tick_dve)
                e.tensor_tensor(to, here[:, :, 0:D].rearrange("p t (h x) -> p t h x", h=HEADS),
                                spread(here[:, :, D:D + HEADS]), ALU.mult).then_inc(c.keyed.sem, 1)
                e.tensor_tensor(part, we.rearrange("p (h x) -> p h x", h=HEADS).unsqueeze(1).to_broadcast(
                    [P, TURN, HEADS, HEAD]), spread(here[:, :, D + HEADS:cell]), ALU.mult).then_inc(c.keyed.sem, 1)
                _hold(e, c.keyed, 2 * (n + 1), c.tick_dve)
                e.tensor_tensor(to, to, part, ALU.add).then_inc(c.staged.sem, 1)

            def finish(n, b):
                _hold(e, c.turned, n + 1, c.tick_dve)
                e.tensor_tensor(skip[:, _chunk(n, size)], skip[:, _chunk(n, size)], ps[:, b, 0:size], ALU.add
                                ).then_inc(c.chunked.sem, 1)
            mix(0, 0)
            with e.Fori(0, steps // 2 - 1) as i:
                for b in range(2):
                    mix(i * 2 + b + 1, 1 - b)
                    finish(i * 2 + b, b)
            mix(steps - 1, 1)
            finish(steps - 2, 0)
            finish(steps - 1, 1)

        @block.tensor
        def _(e):
            with e.Fori(0, steps // 2) as i:
                for b in range(2):
                    n = i * 2 + b
                    _hold(e, c.staged, n + 1, c.tick_pe)
                    _hold(e, c.chunked, n - 1, c.tick_pe)
                    for t in range(TURN):
                        at = b * size + t * P
                        last = e.transpose(ps[:, b, t * P:t * P + P], stage[:, at:at + P], c.ident[:, :])
                    last.then_inc(c.turned.sem, 1)
    c.keyed.passed(2 * steps)
    for g in (c.staged, c.turned, c.chunked):
        g.passed(steps)


def _softmax(c, score, dram):
    nc = c.nc
    flags = c.DE[:, 0:SEQ + 2]
    new = c.DE[:, SEQ + 2:2 * SEQ + 3]
    run = c.DE[:, 2 * SEQ + 4:3 * SEQ + 4]
    alpha = c.soft
    rows = c.rows
    cols = c.small[:, 32:40]
    view = score.rearrange("p (c j h) -> p j h c", h=HEADS, j=SEQ_PAIRS)
    with nc.Block() as block:
        @block.sync
        def _(e):
            src = dram.seq[0:SEQ_ROWS * SEQ].rearrange("(c x) -> c x", x=SEQ)
            wide = bass.AP(src.tensor, src.offset, [[SEQ, SEQ_ROWS], [1, SEQ + 2]])
            for h in range(HEADS):
                e.dma_start(flags[h * SEQ_ROWS:(h + 1) * SEQ_ROWS, :], wide).then_inc(c.moved.sem, 16)
            e.wait_ge(c.moved.sem, c.moved.at(16 * HEADS))

        @block.vector
        def _(e):
            for h in range(HEADS):
                e.tensor_copy(run.rearrange("p (j h c) -> p j h c", h=HEADS, c=SEQ_ROWS)[:, :, h, :],
                              view[:, :, h, :])
    c.moved.passed(16 * HEADS)
    turns = [(a, min(a + 8, SEQ_PAIRS)) for a in range(0, SEQ_PAIRS, 8)]

    def turned(forward):
        with nc.psum_tensor(c.name("soft"), [P, 2, 8 * P], F32) as ps, nc.Block() as block:
            @block.tensor
            def _(e):
                for n, (a, z) in enumerate(turns):
                    e.wait_ge(c.chunked.sem, c.chunked.at(n - 1))
                    for j in range(a, z):
                        at = ps[:, n % 2, (j - a) * P:(j - a + 1) * P]
                        if forward:
                            last = e.transpose(at, run[:, j * P:(j + 1) * P], c.ident[:, :])
                        else:
                            last = e.transpose(at, alpha[:, j * P:(j + 1) * P], c.ident[:, :])
                    last.then_inc(c.turned.sem, 1)

            if forward:
                @block.vector
                def _(e):
                    _small(c, e, c.small_dve, 1, lambda: e.tensor_tensor(
                        new, flags[:, 1:SEQ + 2], flags[:, 0:SEQ + 1], ALU.not_equal))
                    e.tensor_scalar(new, new, FAR, None, ALU.mult)

            @block.scalar
            def _(e):
                for n, (a, z) in enumerate(turns):
                    e.wait_ge(c.turned.sem, c.turned.at(n + 1))
                    if forward:
                        e.copy(alpha[:, a * P:z * P], ps[:, n % 2, 0:(z - a) * P]).then_inc(c.chunked.sem, 1)
                        continue
                    for h in range(HEADS):
                        k = e.copy(view[:, a:z, h, :],
                                   ps[:, n % 2, 0:(z - a) * P].rearrange("p (j h c) -> p j h c", h=HEADS,
                                                                         c=SEQ_ROWS)[:, :, h, :])
                    k.then_inc(c.chunked.sem, 1)
        c.turned.passed(len(turns))
        c.chunked.passed(len(turns))

    turned(True)

    for back in (False, True):
        if back:
            fence, line = new[:, 1:SEQ + 1][:, ::-1], run[:, ::-1]
            end = run[:, 0:1]
        else:
            fence, line = new[:, 0:SEQ], alpha
            end = run[:, SEQ - 1:SEQ]
        out = run[:, ::-1] if back else run
        _whole(c,
               ("v", lambda e: e.tensor_tensor_scan(out, fence, line, FAR, ALU.add, ALU.max)),
               ("v", lambda e: e.tensor_copy(cols[:, 0:1], end)),
               ("v", lambda e: e.tensor_reduce(cols[:, 1:2], new[:, 1:SEQ + 1] if back else new[:, 0:SEQ],
                                               AX.X, ALU.min)))
        with nc.psum_tensor(c.name("carry"), [P, 2 * P + 8], F32) as ps:
            with nc.Block() as block:
                @block.tensor
                def _(e):
                    e.transpose(ps[0:1, 0:P], cols[:, 0:1], c.ident[:, :])
                    e.transpose(ps[0:1, P:2 * P], cols[:, 1:2], c.ident[:, :]).then_inc(c.small_pe.sem, 1)
            c.small_pe.passed(1)
            best, shut = rows[:, 0:P], rows[:, P:2 * P]
            carry = rows[:, 2 * P:3 * P + 2]
            if back:
                chain = ("v", lambda e: e.tensor_tensor_scan(carry[:, 0:P][:, ::-1], shut[:, ::-1], best[:, ::-1],
                                                             FAR, ALU.add, ALU.max))
                enter = carry[:, 1:P + 1]
            else:
                chain = ("v", lambda e: e.tensor_tensor_scan(carry[:, 1:P + 1], shut, best, FAR,
                                                             ALU.add, ALU.max))
                enter = carry[:, 0:P]
            _whole(c,
                   ("v", lambda e: e.tensor_copy(rows[:, 0:2 * P], ps[0:1, 0:2 * P])),
                   ("v", lambda e: e.memset(carry, FAR)),
                   chain)
            with nc.Block() as block:
                @block.tensor
                def _(e):
                    e.transpose(ps[:, 2 * P:2 * P + 1], enter, c.ident[0:1, 0:1]).then_inc(c.small_pe.sem, 1)
            c.small_pe.passed(1)
            _whole(c,
                   ("v", lambda e: e.tensor_copy(cols[:, 2:3], ps[:, 2 * P:2 * P + 1])),
                   ("v", lambda e: e.tensor_tensor_scan(out, fence, line, cols[:, 2:3], ALU.add, ALU.max)))
    _whole(c,
           ("v", lambda e: e.tensor_tensor(alpha, alpha, run, ALU.subtract)),
           ("s", lambda e: e.activation(alpha, alpha, ACT.Exp, scale=HEAD ** -0.5)))
    turned(False)


def build(nc, ins, out):
    with ExitStack() as ctx:
        c = _setup(ctx, nc)
        dram = Ctx()
        dram.t = nc.dram_tensor("walk_edge", [KCOLS], I32, kind="Internal").ap()
        dram.n = nc.dram_tensor("walk_node", [KCOLS], I32, kind="Internal").ap()
        dram.seq = nc.dram_tensor("walk_dst", [KCOLS * P + 2], F32, kind="Internal").ap()
        hid = nc.dram_tensor("rows_hidden", [COLS, HID], F32, kind="Internal").ap()
        keys = nc.dram_tensor("rows_key", [COLS, D], F32, kind="Internal").ap()
        both = nc.dram_tensor("rows_key_value", [COLS, 2 * D], F32, kind="Internal").ap()
        spill = nc.dram_tensor("walk_value", [GROUPS, P, GROUP, D], F32, kind="Internal").ap()
        dram.root = nc.dram_tensor("degree_root", [COLS], F32, kind="Internal").ap()
        dram.share = nc.dram_tensor("degree_share", [COLS], F32, kind="Internal").ap()
        A, B, C, D_, E_, F = c.A[:, :], c.B, c.C[:, :], c.D, c.E, c.F[:, :]
        column = {name: c.cols[:, i:i + w] for name, (i, w) in ins["at"].items()}

        def vv(out_, a, b, op):
            return ("v", lambda e: e.tensor_tensor(out_, a, b, op))

        _start(c, ins)
        _walk(c, ins, dram)

        spread = _degree(c, F, C, dram)
        h = slice(0, HID)
        _dense(c, [([(c.W1g[:, :], A)], B, None, ACT.Copy, HID)], sync=spread)
        _table(c, B, hid, HID, other=F, op=ALU.mult)
        _pass(c, "sum", hid, D_, HID)
        _whole(c, vv(D_[h, :], D_[h, :], B[h, :], ALU.add),
               vv(D_[h, :], D_[h, :], F[h, :], ALU.mult),
               ("s", lambda e: e.activation(B[h, :], D_[h, :], ACT.Relu, bias=column["L0_gnn_b1"][h, :])))
        _table(c, B, hid, HID, other=F, op=ALU.mult)
        _pass(c, "sum", hid, D_, HID)
        _whole(c, vv(D_[h, :], D_[h, :], B[h, :], ALU.add),
               vv(D_[h, :], D_[h, :], F[h, :], ALU.mult))
        _dense(c, [([(c.W2g[:, :], D_)], B, column["L0_gnn_b2"], ACT.Identity, P)])
        _norm(c, A, B, D_, out=keys)

        _pass(c, "sum", keys, D_)
        _whole(c, vv(D_, D_, C, ALU.mult))
        _dense(c, [([(c.W1T[:, :], D_)], B, column["L1_gnn_b"], ACT.Relu, P)], feed=(D_, D_, A))
        _norm(c, A, B, D_)

        _dense(c, [([(c.encW[:, :], A)], B, column["L2_gnn_enc_b"], ACT.Identity, P)])
        _table(c, B, keys)
        wide = (E_, F)

        def queries(tag):
            return [(c.W3[:, j, :], ins[f"L3_gnn_W{w}{tag}"]) for j, w in enumerate("qkvs")] + [
                (c.bias[:, j, :], ins[f"L3_gnn_b{w}{tag}"].to_broadcast([P, D])) for j, w in enumerate("qkv")]
        for layer in range(LAYERS):
            def col(name, n, w=1):
                return column[name][:, n:n + w]
            scale, shift = c.small[:, 20:22], c.small[:, 22:24]
            scale2, shift2 = c.small[:, 24:25], c.small[:, 25:26]
            weights = [(c.W1[:, :], ins["L2_gnn_W1"][layer, :, :]),
                       (c.W2[:, :, :], ins["L2_gnn_W2"][layer, :, :].rearrange("(h k) m -> k h m", h=2))]
            if layer == LAYERS - 1:
                weights += queries("1")
            _pass(c, "edge", keys, D_, attr=ins["attr"], weights=weights)
            _dense(c, [([(c.W1[:, j * P:(j + 1) * P], D_)], wide[j], col("L2_gnn_b1", 2 * layer + j),
                        ACT.Identity, P) for j in range(2)], feed=(D_, D_, B),
                   batch=(col("L2_gnn_bn1_g", 2 * layer, 2), col("L2_gnn_bn1_b", 2 * layer, 2), scale, shift))
            _dense(c, [([(c.W2[:, j, :], wide[j]) for j in range(2)], D_, col("L2_gnn_b2", layer), None, P)],
                   by="dve", prepare=[(wide[j], scale[:, j:j + 1], shift[:, j:j + 1]) for j in range(2)],
                   batch=(col("L2_gnn_bn_g", layer), col("L2_gnn_bn_b", layer), scale2, shift2))
            if layer < LAYERS - 1:
                _table(c, B, keys, other=D_, op=ALU.add, apply=(ACT.Relu, scale2, shift2))
        _whole(c, ("s", lambda e: e.activation(D_, D_, ACT.Identity, bias=shift2, scale=scale2)),
               vv(B, B, D_, ALU.add))
        _norm(c, A, B, E_)

        score = c.F[:, 0:PAIRS * HEADS]
        query = c.Bwide[:, 0:WINDOWS * (D + HEADS)].rearrange("p (w x) -> p w x", w=WINDOWS)
        agg, odd = c.DE[:, 0:WINDOWS * (D + 2 * HEADS)], c.Bwide[:, :]
        x = A
        for conv in range(2):
            tag = str(conv + 1)
            we = c.We[:, conv, :]
            _project(c, x, both, c.Bwide)
            _dense(c, [([(c.W3[:, 3, :], x)], C, column["L3_gnn_bs" + tag], ACT.Identity, P)])
            spread = E_.rearrange("p (w h x) -> p w h x", h=HEADS, x=HEAD)
            _whole(c,
                   ("v", lambda e: e.tensor_tensor(
                       E_.rearrange("p (w x) -> p w x", w=WINDOWS), query[:, :, 0:D],
                       we.unsqueeze(1).to_broadcast([P, WINDOWS, D]), ALU.mult)),
                   ("v", lambda e: e.tensor_reduce(query[:, :, D:D + HEADS], spread, AX.X, ALU.add)))
            _pass(c, "look", both, None, query=c.Bwide, score=score, spill=spill,
                  weights=queries("2") if conv == 0 else ())
            _softmax(c, score, dram)
            _pass(c, "attend", None, agg, score=score, spill=spill, odd=odd)
            _settle(c, agg, odd, we, C)
            x = C
        _norm(c, A, C, F, out=out, back=False)


_COLUMNS = ["L0_gnn_b1", "L0_gnn_b2", "L1_gnn_b", "L2_gnn_enc_b", "L2_gnn_b1", "L2_gnn_bn1_g", "L2_gnn_bn1_b",
            "L2_gnn_b2", "L2_gnn_bn_g", "L2_gnn_bn_b", "L3_gnn_bs1", "L3_gnn_bs2"]


def kernel(**inputs):
    import numpy as np
    import concourse.bacc as bacc
    from concourse.bass_utils import run_bass_kernel_spmd

    nc = bacc.Bacc("TRN2", target_bir_lowering=False, num_devices=1)
    given = {k: np.asarray(v) for k, v in inputs.items()}
    x_cols = np.zeros((P, COLS), np.float32)
    x_cols[:, :N] = given["x"].T
    arrays = {"xT": x_cols}
    for name, key, fill in (("src", "src", 0), ("dst", "dst", PAD_NODE), ("edge_weight", "w", 0)):
        tiles = np.full((EDGE_TILES * P,), fill, given[name].dtype)
        tiles[:E] = given[name]
        arrays[key] = tiles.reshape(EDGE_TILES, P)
    attr = np.zeros((EDGE_TILES * P, D), np.float32)
    attr[:E] = given["edge_attr_128"]
    arrays["attr"] = attr.reshape(EDGE_TILES, P, D)
    arrays["L1_W_T"] = np.ascontiguousarray(given["L1_gnn_W"].T)
    for name in ("L0_gnn_W1", "L0_gnn_W2", "L2_gnn_enc_W", "L2_gnn_W1", "L2_gnn_W2"):
        arrays[name] = given[name]
    for i in (1, 2):
        for w in ("Wq", "Wk", "Wv", "Ws", "We"):
            arrays[f"L3_gnn_{w}{i}"] = given[f"L3_gnn_{w}{i}"]
        for w in ("bq", "bk", "bv"):
            arrays[f"L3_gnn_{w}{i}"] = given[f"L3_gnn_{w}{i}"].reshape(1, D)
    columns, at = [], {}
    for name in _COLUMNS:
        v = given[name].reshape(-1)
        width = -(-v.size // P)
        block = np.zeros((width * P,), np.float32)
        block[:v.size] = v
        at[name] = (sum(b.shape[1] for b in columns), width)
        columns.append(block.reshape(width, P).T)
    arrays["cols"] = np.concatenate(columns, axis=1)
    ins = {"at": at}
    for name, a in arrays.items():
        arrays[name] = np.ascontiguousarray(a)
        ins[name] = nc.dram_tensor(f"in_{name}", a.shape, mybir.dt.from_np(a.dtype), kind="ExternalInput").ap()
    out = nc.dram_tensor("out_0", (COLS, D), F32, kind="ExternalOutput").ap()
    build(nc, ins, out)
    r = run_bass_kernel_spmd(nc, [{f"in_{k}": v for k, v in arrays.items()}], core_ids=[0])
    return np.ascontiguousarray(r.results[0]["out_0"][:N])
```
